# Optimizing a Trainium2 kernel written in Bass

```python
import numpy as np
import jax
import jax.numpy as jnp

def _softmax(x, axis=-1):
    return jax.nn.softmax(x, axis=axis)

def _gelu(x):
    return jax.nn.gelu(x, approximate=True)

def _silu(x):
    return jax.nn.silu(x)

def _sigmoid(x):
    return jax.nn.sigmoid(x)

def _layernorm(x, axis=-1, eps=1e-05):
    m = jnp.mean(x, axis=axis, keepdims=True)
    v = jnp.var(x, axis=axis, keepdims=True)
    return (x - m) / jnp.sqrt(v + eps)

def _scatter_add(tgt, idx, src, axis=0):
    return tgt.at[idx].add(src)

def _segment_sum(src, seg, n):
    return jax.ops.segment_sum(src, seg, n)
kernel_name = 'mk_seq_postln_d2_jaxref_r4_0bd434'

def setup_inputs(seed: int=0):
    np.random.seed(seed)
    _w = jnp.asarray

    def _L0_attn_setup():
        import jax, jax.numpy as jnp
        import numpy as np
        from jax import lax
        D_MODEL = 256
        D_STATE = 16
        D_CONV = 4
        EXPAND = 2
        D_INNER = EXPAND * D_MODEL
        DT_RANK = (D_MODEL + 15) // 16
        BATCH, LENGTH = (2, 256)
        DT_MIN, DT_MAX = (0.001, 0.1)

        def silu(v):
            return v * jax.nn.sigmoid(v)
        key = jax.random.key(seed)
        ks = jax.random.split(key, 8)
        s = lambda n: 1.0 / np.sqrt(n)
        x = jax.random.normal(ks[0], (BATCH, LENGTH, D_MODEL), jnp.float32)
        W_in = jax.random.normal(ks[1], (2 * D_INNER, D_MODEL), jnp.float32) * s(D_MODEL)
        W_conv = jax.random.normal(ks[2], (D_INNER, 1, D_CONV), jnp.float32) * s(D_CONV)
        W_xproj = jax.random.normal(ks[3], (DT_RANK + 2 * D_STATE, D_INNER), jnp.float32) * s(D_INNER)
        dt_init_std = DT_RANK ** (-0.5)
        W_dt = jax.random.uniform(ks[4], (D_INNER, DT_RANK), jnp.float32, minval=-dt_init_std, maxval=dt_init_std)
        dt = jnp.exp(jax.random.uniform(ks[5], (D_INNER,), jnp.float32) * (np.log(DT_MAX) - np.log(DT_MIN)) + np.log(DT_MIN))
        dt = jnp.maximum(dt, dt_init_std)
        b_dt = dt + jnp.log(-jnp.expm1(-dt))
        A_log = jnp.log(jnp.broadcast_to(jnp.arange(1, D_STATE + 1, dtype=jnp.float32), (D_INNER, D_STATE)))
        D = jnp.ones((D_INNER,), jnp.float32)
        W_out = jax.random.normal(ks[6], (D_MODEL, D_INNER), jnp.float32) * s(D_INNER)
        return dict(x=x, W_in=W_in, W_conv=W_conv, W_xproj=W_xproj, W_dt=W_dt, b_dt=b_dt, A_log=A_log, D=D, W_out=W_out)
    _L0_attn_in = _L0_attn_setup()

    def _L0_ffn_setup():
        import jax, jax.numpy as jnp
        import numpy as np
        DIM = 256
        DEPTH = 7
        PAR = 8
        N_NODES = 2 ** (DEPTH + 1) - 1
        WIDTH = PAR * N_NODES
        key = jax.random.key(seed)
        k1, k2, k3, k4 = jax.random.split(key, 4)
        init_k = float(np.sqrt(1.0 / DIM))
        init_k2 = float(np.sqrt(1.0 / ((DEPTH + 1) * PAR)))
        oldx = jax.random.normal(k1, (4, 512, DIM), dtype=jnp.float32)
        W_in = jax.random.uniform(k2, (WIDTH, DIM), jnp.float32, -init_k, init_k)
        b_in = jax.random.uniform(k3, (WIDTH,), jnp.float32, -init_k, init_k)
        W_out = jax.random.uniform(k4, (DIM, WIDTH), jnp.float32, -init_k2, init_k2)
        return {'oldx': oldx, 'W_in': W_in, 'b_in': b_in, 'W_out': W_out}
    _L0_ffn_in = _L0_ffn_setup()

    def _L1_attn_setup():
        import jax, jax.numpy as jnp
        import numpy as np
        B, S, HID = (1, 512, 256)
        H, HKV, D = (16, 4, 64)
        THETA = 10000.0

        def _rope_tables(seq_len, head_dim):
            inv_freq = 1.0 / THETA ** (jnp.arange(0, head_dim, 2, dtype=jnp.float32) / head_dim)
            freqs = jnp.arange(seq_len, dtype=jnp.float32)[:, None] * inv_freq[None, :]
            emb = jnp.concatenate([freqs, freqs], axis=-1)
            return (jnp.cos(emb)[:, 0::2], jnp.sin(emb)[:, 0::2])

        def _apply_rope(x, cos, sin):
            xe, xo = (x[..., 0::2], x[..., 1::2])
            re = xe * cos - xo * sin
            ro = xe * sin + xo * cos
            return jnp.stack([re, ro], axis=-1).reshape(x.shape)
        key = jax.random.key(seed)
        k0, k1, k2, k3, k4 = jax.random.split(key, 5)
        return {'hidden_states': jax.random.normal(k0, (B, S, HID), dtype=jnp.float32), 'Wq': jax.random.normal(k1, (HID, H * D), dtype=jnp.float32) * 0.02, 'Wk': jax.random.normal(k2, (HID, HKV * D), dtype=jnp.float32) * 0.02, 'Wv': jax.random.normal(k3, (HID, HKV * D), dtype=jnp.float32) * 0.02, 'Wo': jax.random.normal(k4, (H * D, HID), dtype=jnp.float32) * 0.02}
    _L1_attn_in = _L1_attn_setup()

    def _L1_ffn_setup():
        import jax, jax.numpy as jnp
        import numpy as np
        TOP_K = 8
        key = jax.random.key(seed)
        k1, k2, k3, k4, k5 = jax.random.split(key, 5)
        B, S, D, F, E = (2, 512, 256, 192, 64)
        return {'hidden_states': jax.random.normal(k1, (B, S, D), dtype=jnp.float32), 'gate_w': jax.random.normal(k2, (E, D), dtype=jnp.float32) * 0.02, 'w_gate': jax.random.normal(k3, (E, F, D), dtype=jnp.float32) * 0.02, 'w_up': jax.random.normal(k4, (E, F, D), dtype=jnp.float32) * 0.02, 'w_down': jax.random.normal(k5, (E, D, F), dtype=jnp.float32) * 0.02}
    _L1_ffn_in = _L1_ffn_setup()
    _d = {'L0_attn_x': _L0_attn_in['x'], 'L0_attn_W_in': _L0_attn_in['W_in'], 'L0_attn_W_conv': _L0_attn_in['W_conv'], 'L0_attn_W_xproj': _L0_attn_in['W_xproj'], 'L0_attn_W_dt': _L0_attn_in['W_dt'], 'L0_attn_b_dt': _L0_attn_in['b_dt'], 'L0_attn_A_log': _L0_attn_in['A_log'], 'L0_attn_D': _L0_attn_in['D'], 'L0_attn_W_out': _L0_attn_in['W_out'], 'L0_ffn_W_in': _L0_ffn_in['W_in'], 'L0_ffn_b_in': _L0_ffn_in['b_in'], 'L0_ffn_W_out': _L0_ffn_in['W_out'], 'L1_attn_Wq': _L1_attn_in['Wq'], 'L1_attn_Wk': _L1_attn_in['Wk'], 'L1_attn_Wv': _L1_attn_in['Wv'], 'L1_attn_Wo': _L1_attn_in['Wo'], 'L1_ffn_gate_w': _L1_ffn_in['gate_w'], 'L1_ffn_w_gate': _L1_ffn_in['w_gate'], 'L1_ffn_w_up': _L1_ffn_in['w_up'], 'L1_ffn_w_down': _L1_ffn_in['w_down']}
    _x0 = _d['L0_attn_x']
    _d['L0_attn_x'] = jax.random.normal(jax.random.fold_in(jax.random.key(seed), 1), (2, 2048, 256), dtype=_x0.dtype)
    del _x0
    return _d

def reference(L0_attn_x, L0_attn_W_in, L0_attn_W_conv, L0_attn_W_xproj, L0_attn_W_dt, L0_attn_b_dt, L0_attn_A_log, L0_attn_D, L0_attn_W_out, L0_ffn_W_in, L0_ffn_b_in, L0_ffn_W_out, L1_attn_Wq, L1_attn_Wk, L1_attn_Wv, L1_attn_Wo, L1_ffn_gate_w, L1_ffn_w_gate, L1_ffn_w_up, L1_ffn_w_down):

    def _L0_attn_ref(x, W_in, W_conv, W_xproj, W_dt, b_dt, A_log, D, W_out):
        import jax, jax.numpy as jnp
        import numpy as np
        from jax import lax
        D_MODEL = 256
        D_STATE = 16
        D_CONV = 4
        EXPAND = 2
        D_INNER = EXPAND * D_MODEL
        DT_RANK = (D_MODEL + 15) // 16
        BATCH, LENGTH = (2, 256)
        DT_MIN, DT_MAX = (0.001, 0.1)

        def silu(v):
            return v * jax.nn.sigmoid(v)
        xz = x @ W_in.T
        xc, z = jnp.split(xz, 2, axis=-1)
        xc = lax.conv_general_dilated(xc.transpose(0, 2, 1), W_conv, window_strides=(1,), padding=[(D_CONV - 1, 0)], feature_group_count=D_INNER, dimension_numbers=('NCH', 'OIH', 'NCH')).transpose(0, 2, 1)
        xc = silu(xc)
        dbc = xc @ W_xproj.T
        dlt = dbc[..., :DT_RANK]
        Bm = dbc[..., DT_RANK:DT_RANK + D_STATE]
        Cm = dbc[..., DT_RANK + D_STATE:]
        delta = jax.nn.softplus(dlt @ W_dt.T + b_dt)
        A = -jnp.exp(A_log)
        deltaA = jnp.exp(delta[..., None] * A)
        deltaBx = delta[..., None] * Bm[:, :, None, :] * xc[..., None]

        def step(h, inp):
            dA, dBx, c = inp
            h = dA * h + dBx
            return (h, jnp.einsum('bdn,bn->bd', h, c))
        h0 = jnp.zeros((x.shape[0], D_INNER, D_STATE), xc.dtype)
        _, ys = lax.scan(step, h0, (deltaA.swapaxes(0, 1), deltaBx.swapaxes(0, 1), Cm.swapaxes(0, 1)))
        y = ys.swapaxes(0, 1) + xc * D
        y = y * silu(z)
        return y @ W_out.T

    def _L0_ffn_ref(oldx, W_in, b_in, W_out):
        import jax, jax.numpy as jnp
        import numpy as np
        DIM = 256
        DEPTH = 7
        PAR = 8
        N_NODES = 2 ** (DEPTH + 1) - 1
        WIDTH = PAR * N_NODES
        x = oldx.reshape(-1, DIM)
        B = x.shape[0]
        logits = x @ W_in.T + b_in
        decisions = (logits > 0).astype(jnp.int32).reshape(B, PAR, N_NODES)
        acts = jax.nn.silu(logits).reshape(B, PAR, N_NODES)
        current = jnp.zeros((B, PAR), dtype=jnp.int32)
        dmap = jax.nn.one_hot(current, N_NODES, dtype=acts.dtype)
        for d in range(DEPTH):
            cur_platform = 2 ** d - 1
            next_platform = 2 ** (d + 1) - 1
            moves = jnp.take_along_axis(decisions, current[..., None], axis=2)[..., 0]
            current = (current - cur_platform) * 2 + moves + next_platform
            dmap = dmap + jax.nn.one_hot(current, N_NODES, dtype=acts.dtype)
        masked = acts * jax.lax.stop_gradient(dmap)
        out = masked.reshape(B, WIDTH) @ W_out.T
        return out.reshape(oldx.shape)

    def _L1_attn_ref(hidden_states, Wq, Wk, Wv, Wo):
        import jax, jax.numpy as jnp
        import numpy as np
        B, S, HID = (1, 512, 256)
        H, HKV, D = (16, 4, 64)
        THETA = 10000.0

        def _rope_tables(seq_len, head_dim):
            inv_freq = 1.0 / THETA ** (jnp.arange(0, head_dim, 2, dtype=jnp.float32) / head_dim)
            freqs = jnp.arange(seq_len, dtype=jnp.float32)[:, None] * inv_freq[None, :]
            emb = jnp.concatenate([freqs, freqs], axis=-1)
            return (jnp.cos(emb)[:, 0::2], jnp.sin(emb)[:, 0::2])

        def _apply_rope(x, cos, sin):
            xe, xo = (x[..., 0::2], x[..., 1::2])
            re = xe * cos - xo * sin
            ro = xe * sin + xo * cos
            return jnp.stack([re, ro], axis=-1).reshape(x.shape)
        b, s, _ = hidden_states.shape
        q = (hidden_states @ Wq).reshape(b, s, H, D).transpose(0, 2, 1, 3)
        k = (hidden_states @ Wk).reshape(b, s, HKV, D).transpose(0, 2, 1, 3)
        v = (hidden_states @ Wv).reshape(b, s, HKV, D).transpose(0, 2, 1, 3)
        cos, sin = _rope_tables(s, D)
        q = _apply_rope(q, cos, sin)
        k = _apply_rope(k, cos, sin)
        G = H // HKV
        qg = q.reshape(b, HKV, G, s, D)
        scale = jnp.float32(D) ** (-0.5)
        scores = jnp.einsum('bkgqd,bkpd->bkgqp', qg, k) * scale
        causal = jnp.tril(jnp.ones((s, s), dtype=bool))
        scores = jnp.where(causal, scores, jnp.float32(-1e+30))
        probs = jax.nn.softmax(scores, axis=-1)
        out = jnp.einsum('bkgqp,bkpd->bkgqd', probs, v).reshape(b, H, s, D)
        out = out.transpose(0, 2, 1, 3).reshape(b, s, H * D)
        return out @ Wo

    def _L1_ffn_ref(hidden_states, gate_w, w_gate, w_up, w_down):
        import jax, jax.numpy as jnp
        import numpy as np
        TOP_K = 8
        B, S, D = hidden_states.shape
        E = gate_w.shape[0]
        x = hidden_states.reshape(-1, D)
        logits = x.astype(jnp.float32) @ gate_w.astype(jnp.float32).T
        scores = jax.nn.softmax(logits, axis=-1)
        topk_w, topk_ids = jax.lax.top_k(scores, TOP_K)
        topk_w = topk_w / (topk_w.sum(axis=-1, keepdims=True) + 1e-20)
        flat_ids = topk_ids.reshape(-1)
        sort_idx = jnp.argsort(flat_ids)
        sorted_tokens = x[sort_idx // TOP_K]
        group_sizes = jnp.zeros((E,), jnp.int32).at[flat_ids].add(1)
        g = jax.lax.ragged_dot(sorted_tokens, jnp.swapaxes(w_gate, 1, 2), group_sizes)
        u = jax.lax.ragged_dot(sorted_tokens, jnp.swapaxes(w_up, 1, 2), group_sizes)
        h = jax.nn.silu(g) * u
        out = jax.lax.ragged_dot(h, jnp.swapaxes(w_down, 1, 2), group_sizes)
        unsorted = jnp.zeros_like(out).at[sort_idx].set(out)
        y = (unsorted.reshape(B * S, TOP_K, D) * topk_w[..., None]).sum(axis=1)
        return y.reshape(B, S, D)
    x = L0_attn_x
    x = _layernorm(x + _L0_attn_ref(x, L0_attn_W_in, L0_attn_W_conv, L0_attn_W_xproj, L0_attn_W_dt, L0_attn_b_dt, L0_attn_A_log, L0_attn_D, L0_attn_W_out), axis=-1)
    x = _layernorm(x + _L0_ffn_ref(x, L0_ffn_W_in, L0_ffn_b_in, L0_ffn_W_out), axis=-1)
    x = _layernorm(x + _L1_attn_ref(x, L1_attn_Wq, L1_attn_Wk, L1_attn_Wv, L1_attn_Wo), axis=-1)
    x = _layernorm(x + _L1_ffn_ref(x, L1_ffn_gate_w, L1_ffn_w_gate, L1_ffn_w_up, L1_ffn_w_down), axis=-1)
    return x

_drawn_inputs = setup_inputs


def setup_inputs(seed=0):
    import zlib

    import numpy as np

    out = dict(_drawn_inputs(seed))
    spreads = {'L0_attn_b_dt': (-1.258691668510437, 0.2), 'L0_attn_D': (1.0, 0.2)}
    factors = {'L1_attn_Wq': 8.0,
     'L1_attn_Wk': 8.0,
     'L1_attn_Wv': 3.265,
     'L1_attn_Wo': 3.298,
     'L1_ffn_gate_w': 8.0,
     'L1_ffn_w_gate': 8.0,
     'L1_ffn_w_up': 8.0,
     'L1_ffn_w_down': 8.0}
    for name, (base, spread) in spreads.items():
        noise = np.random.default_rng([zlib.crc32(name.encode()), seed]).standard_normal(out[name].shape)
        drawn = base * np.exp(spread * noise) if base else spread * noise
        out[name] = jnp.asarray(drawn.astype(out[name].dtype))
    for name, factor in factors.items():
        out[name] = (out[name] * factor).astype(out[name].dtype)
    return out
```

```python
from contextlib import ExitStack

import concourse.bass as bass
from concourse import mybir
from concourse.alu_op_type import AluOpType as ALU

ACT = mybir.ActivationFunctionType
F32 = mybir.dt.float32
P = 128
BATCH, LENGTH, DM = 2, 2048, 256
TOKENS = BATCH * LENGTH
KD = DM // P


class Tally:

    def __init__(self, sem, per=1, ahead=0):
        self.sem, self.per, self.ahead = sem, per, ahead

    def credit(self, eng):
        eng.sem_inc(self.sem, self.ahead * self.per)

    def at(self, rnd, k=None):
        return (rnd + self.ahead) * self.per + (self.per if k is None else k)


def mamba(nc, x_T, W_inT, conv_w, W_xprojT, W_dtT, b_dt, A_log, D_skip, sel_bc, keep, ident, y_scr):
    DI, NST, RANK, TAPS = 512, 16, 16, 4
    DB = DI // P
    TC = 512
    CHUNKS = TOKENS // TC
    NBC = RANK + 2 * NST
    IN, XP, USES = 2 * DB, 2 * DB, 2 * DB + 1 + DB
    y_out_view = y_scr.rearrange("(d p) t -> p d t", p=P)
    xT_view = x_T.rearrange("(k p) t -> p k t", p=P)

    sems = []
    with ExitStack() as ctx:
        def sb(name, shape, dt=F32):
            return ctx.enter_context(nc.sbuf_tensor(name, shape, dt))

        def pb(name, shape):
            return ctx.enter_context(nc.psum_tensor(name, shape, F32))

        def tally(name, per=1, ahead=0):
            sems.append(nc.alloc_semaphore(name))
            return Tally(sems[-1], per, ahead)

        w_in = sb("w_in", [P, KD, 2 * DI])
        w_xp = sb("w_xp", [P, DB, NBC])
        w_dt = sb("w_dt", [RANK, DI])
        taps = sb("taps", [P, DB, TAPS])
        dt_bias = sb("dt_bias", [P, DB])
        a_log = sb("a_log", [P, DB, NST])
        neg_a = sb("neg_a", [P, DB, NST])
        d_skip = sb("d_skip", [P, DB])
        sel = sb("sel", [NBC, 2 * NST, P])
        idn = sb("idn1", [P, P])
        keep_sb = sb("keep_sb", [P, CHUNKS // 2])
        xt = sb("xt", [P, 2, KD, TC])
        xraw = sb("xraw", [P, DB, TC + TAPS - 1])
        xc = sb("xc", [P, 2, DB, TC])
        sz = sb("sz", [P, 2, DB, TC])
        dbc = sb("dbc", [NBC, 2, TC])
        sp = sb("sp", [P, DB, TC])
        delta = sb("delta", [P, 2, DB, TC])
        u = sb("u", [P, 2, DB, TC])
        dA = sb("dA", [P, 2, DB, TC])
        dBx = sb("dBx", [P, 2, DB, TC])
        h = sb("h", [P, 2, DB, TC])
        yg = sb("yg", [P, DB, TC])
        h_in = sb("h_in", [P, NST, DB])
        ps_y = pb("ps_y", [P, DB, TC])
        ps_b = pb("ps_b", [P, 2, TC])
        ps_c = pb("ps_c", [P, TC])
        ps_f = pb("ps_f", [P, TC])

        consts = tally("consts")
        xt_ld = [tally("xt_ld0"), tally("xt_ld1")]
        zeroed = tally("zeroed", 2)
        nega_step = tally("nega_step", 2)
        front_ps = tally("front_ps", USES)
        front_ev = tally("front_ev", USES)
        conv_step = tally("conv_step", DB * TAPS + 1, 1)
        xc_ready = tally("xc_ready")
        sz_ready = tally("sz_ready")
        sp_step = tally("sp_step", 3)
        delta_ready = tally("delta_ready", 1, 1)
        u_ready = tally("u_ready")
        b_ready = tally("b_ready", NST)
        c_ready = tally("c_ready", NST)
        dA_ready = tally("dA_ready", NST)
        dbx_done = tally("dbx_done", NST, 1)
        scan_done = tally("scan_done", NST, 1)
        carry_done = tally("carry_done", NST, 1)
        hc_done = tally("hc_done", NST)
        reduce_done = tally("reduce_done", NST, 1)
        y_taken = tally("y_taken", 1, 1)
        ygated = tally("ygated", 1, 2)
        y_out = tally("y_out", 16, 1)
        CONSTS = 11

        block = ctx.enter_context(nc.Block())

        @block.sync
        def _(sp_eng):
            for dst, src in (
                (w_in[:, :, :], W_inT.rearrange("(k p) n -> p k n", p=P)),
                (taps[:, :, :], conv_w.rearrange("(d p) t -> p d t", p=P)),
                (w_xp[:, :, :], W_xprojT.rearrange("(d p) n -> p d n", p=P)),
                (w_dt[:, :], W_dtT),
                (dt_bias[:, :], b_dt.rearrange("(d p) -> p d", p=P)),
                (a_log[:, :, :], A_log.rearrange("(d p) n -> p d n", p=P)),
                (d_skip[:, :], D_skip.rearrange("(d p) -> p d", p=P)),
                (sel[:, :, :], sel_bc),
                (idn[:, :], ident),
                (keep_sb[:, :], keep),
            ):
                with nc.allow_non_contiguous_dma(reason="small vectors, once"):
                    sp_eng.dma_start(dst, src).then_inc(consts.sem, 16)
            for k in range(2):
                sp_eng.dma_start(xt[:, k, :, :], xT_view[:, :, k * TC:(k + 1) * TC]).then_inc(xt_ld[k].sem, 16)
            y_out.credit(sp_eng)
            with sp_eng.Fori(0, CHUNKS // 2) as i:
                ahead = [sp_eng.snap(((2 * i + s + 2) % CHUNKS) * TC) for s in range(2)]
                here = [sp_eng.snap((2 * i + s) * TC) for s in range(2)]
                for s in range(2):
                    c = 2 * i + s
                    sp_eng.wait_ge(front_ps.sem, front_ps.at(c, IN))
                    sp_eng.dma_start(xt[:, s, :, :], xT_view[:, :, bass.ds(ahead[s], TC)]).then_inc(xt_ld[s].sem, 16)
                    sp_eng.wait_ge(ygated.sem, ygated.at(c))
                    sp_eng.dma_start(y_out_view[:, :, bass.ds(here[s], TC)], yg[:, :, :]).then_inc(y_out.sem, 16)
            sp_eng.wait_ge(y_out.sem, y_out.at(CHUNKS - 1))
            for k in range(2):
                sp_eng.wait_ge(xt_ld[k].sem, 16 * (CHUNKS // 2 + 1))

        @block.tensor
        def _(pe):
            def in_proj(k, slot, j, used=True):
                if used:
                    pe.wait_ge(front_ev.sem, front_ev.at(k, j))
                for kd in range(KD):
                    last = nc.tensor.matmul(ps_f[:, :], w_in[:, kd, j * P:(j + 1) * P], xt[:, slot, kd, :],
                                            start=kd == 0, stop=kd == KD - 1)
                last.then_inc(front_ps.sem, 1)

            def x_proj(k, slot):
                pe.wait_ge(front_ev.sem, front_ev.at(k, XP))
                pe.wait_ge(xc_ready.sem, xc_ready.at(k))
                for d in range(DB):
                    last = nc.tensor.matmul(ps_f[0:NBC, :], w_xp[:, d, :], xc[:, slot, d, :],
                                            start=d == 0, stop=d == DB - 1)
                last.then_inc(front_ps.sem, 1)

            def dt_proj(k, slot, d):
                pe.wait_ge(front_ev.sem, front_ev.at(k, XP + 1 + d))
                nc.tensor.matmul(ps_f[:, :], w_dt[:, d * P:(d + 1) * P], dbc[0:RANK, slot, :],
                                 start=True, stop=True).then_inc(front_ps.sem, 1)

            def spread_b(c, slot, n):
                pe.wait_ge(dbx_done.sem, dbx_done.at(c, n - 1))
                if n == 0:
                    pe.wait_ge(front_ev.sem, front_ev.at(c, XP + 1))
                nc.tensor.matmul(ps_b[:, n % 2, :], sel[:, n, :], dbc[:, slot, :],
                                 start=True, stop=True).then_inc(b_ready.sem, 1)

            def spread_c(c, slot, n):
                if n:
                    pe.wait_ge(hc_done.sem, hc_done.at(c, n))
                nc.tensor.matmul(ps_c[:, :], sel[:, NST + n, :], dbc[:, slot, :],
                                 start=True, stop=True).then_inc(c_ready.sem, 1)

            def sum_states(c, n):
                pe.wait_ge(hc_done.sem, hc_done.at(c, n + 1))
                if n == 0:
                    pe.wait_ge(y_taken.sem, y_taken.at(c - 1))
                for d in range(DB):
                    last = nc.tensor.matmul(ps_y[:, d, :], idn[:, :], h[:, n % 2, d, :],
                                            start=n == 0, stop=n == NST - 1)
                last.then_inc(reduce_done.sem, 1)

            pe.wait_ge(consts.sem, 16 * (CONSTS - 1))
            pe.wait_ge(xt_ld[0].sem, 16)
            for j in range(IN):
                in_proj(0, 0, j, j > 0)
            x_proj(0, 0)
            for d in range(DB):
                dt_proj(0, 0, d)
            with pe.Fori(0, CHUNKS // 2) as i:
                for s in range(2):
                    c, k, f = 2 * i + s, 2 * i + s + 1, 1 - s
                    pe.wait_ge(xt_ld[f].sem, 16 * (i + 1 + s))
                    spread_b(c, s, 0)
                    spread_b(c, s, 1)
                    spread_c(c, s, 0)
                    for n in range(NST + 1):
                        if n + 2 < NST:
                            spread_b(c, s, n + 2)
                        if 1 <= n < NST:
                            spread_c(c, s, n)
                        if n >= 1:
                            sum_states(c, n - 1)
                        if n < IN:
                            in_proj(k, f, n)
                        elif n == IN + 1:
                            x_proj(k, f)
                        elif n in (IN + 2, IN + 3):
                            for d in range(2 * (n - IN - 2), 2 * (n - IN - 1)):
                                dt_proj(k, f, d)

        @block.scalar
        def _(act):
            def evac(k, slot, j):
                act.wait_ge(front_ps.sem, front_ps.at(k, j + 1))
                if j < DB:
                    ins = nc.scalar.activation(xraw[:, j, TAPS - 1:], ps_f[:, :], ACT.Copy)
                elif j < IN:
                    ins = nc.scalar.activation(sz[:, slot, j - DB, :], ps_f[:, :], ACT.Copy)
                elif j == XP:
                    ins = nc.scalar.activation(dbc[:, slot, :], ps_f[0:NBC, :], ACT.Copy)
                else:
                    d = j - XP - 1
                    ins = nc.scalar.activation(delta[:, slot, d, :], ps_f[:, :], ACT.Identity,
                                               bias=dt_bias[:, d:d + 1])
                ins.then_inc(front_ev.sem, 1)

            def gates(k, slot):
                act.wait_ge(conv_step.sem, conv_step.at(k, DB * TAPS))
                nc.scalar.activation(xc[:, slot, :, :], xc[:, slot, :, :], ACT.Silu).then_inc(xc_ready.sem, 1)
                act.wait_ge(front_ev.sem, front_ev.at(k, IN))
                nc.scalar.activation(sz[:, slot, :, :], sz[:, slot, :, :], ACT.Silu).then_inc(sz_ready.sem, 1)

            def softplus(k, slot):
                act.wait_ge(front_ev.sem, front_ev.at(k, USES))
                act.wait_ge(delta_ready.sem, delta_ready.at(k - 1))
                nc.scalar.activation(sp[:, :, :], delta[:, slot, :, :], ACT.Abs).then_inc(sp_step.sem, 1)
                act.wait_ge(sp_step.sem, sp_step.at(k, 1))
                nc.scalar.activation(sp[:, :, :], sp[:, :, :], ACT.Exp, scale=-1.0).then_inc(sp_step.sem, 1)
                act.wait_ge(sp_step.sem, sp_step.at(k, 2))
                nc.scalar.activation(sp[:, :, :], sp[:, :, :], ACT.Ln, bias=1.0).then_inc(sp_step.sem, 1)

            def decay(c, slot, n):
                if n == 0:
                    act.wait_ge(delta_ready.sem, delta_ready.at(c))
                act.wait_ge(scan_done.sem, scan_done.at(c, n - 1))
                for d in range(DB):
                    ins = nc.scalar.activation(dA[:, n % 2, d, :], delta[:, slot, d, :], ACT.Exp,
                                               scale=neg_a[:, d, n:n + 1])
                ins.then_inc(dA_ready.sem, 1)

            act.wait_ge(consts.sem, 16 * (CONSTS - 1))
            nc.scalar.activation(neg_a[:, :, :], a_log[:, :, :], ACT.Exp).then_inc(nega_step.sem, 1)
            act.wait_ge(nega_step.sem, 1)
            nc.scalar.activation(neg_a[:, :, :], neg_a[:, :, :], ACT.Copy, scale=-1.0).then_inc(nega_step.sem, 1)
            act.wait_ge(nega_step.sem, 2)
            act.wait_ge(zeroed.sem, 2)
            for j in range(IN):
                evac(0, 0, j)
            gates(0, 0)
            for j in range(XP, USES):
                evac(0, 0, j)
            softplus(0, 0)
            with act.Fori(0, CHUNKS // 2) as i:
                for s in range(2):
                    c, k, f = 2 * i + s, 2 * i + s + 1, 1 - s
                    decay(c, s, 0)
                    act.wait_ge(ygated.sem, ygated.at(k - 2))
                    act.wait_ge(conv_step.sem, conv_step.at(k - 1))
                    for n in range(NST):
                        if n + 1 < NST:
                            decay(c, s, n + 1)
                        if n < IN:
                            evac(k, f, n)
                        elif n == IN:
                            gates(k, f)
                        elif n == IN + 1:
                            evac(k, f, XP)
                        elif n in (IN + 2, IN + 3):
                            for d in range(2 * (n - IN - 2), 2 * (n - IN - 1)):
                                evac(k, f, XP + 1 + d)
                        elif n == IN + 4:
                            softplus(k, f)

        @block.vector
        def _(dve):
            def conv_tap(k, slot, t):
                for j in range(DB):
                    if t == 0:
                        dve.wait_ge(front_ev.sem, front_ev.at(k, j + 1))
                        ins = nc.vector.tensor_scalar(xc[:, slot, j, :], xraw[:, j, 0:TC], taps[:, j, 0:1], None, ALU.mult)
                    else:
                        dve.wait_ge(conv_step.sem, conv_step.at(k, (t - 1) * DB + j + 1))
                        ins = nc.vector.scalar_tensor_tensor(xc[:, slot, j, :], xraw[:, j, t:t + TC], taps[:, j, t:t + 1],
                                                             xc[:, slot, j, :], ALU.mult, ALU.add)
                    ins.then_inc(conv_step.sem, 1)

            def halo(k, keep_col):
                dve.wait_ge(conv_step.sem, conv_step.at(k, DB * TAPS))
                if keep_col is None:
                    ins = nc.vector.tensor_copy(xraw[:, :, 0:TAPS - 1], xraw[:, :, TC:])
                else:
                    ins = nc.vector.tensor_scalar(xraw[:, :, 0:TAPS - 1], xraw[:, :, TC:], keep_col, None, ALU.mult)
                ins.then_inc(conv_step.sem, 1)

            def make_delta(k, slot):
                dve.wait_ge(sp_step.sem, sp_step.at(k, 3))
                nc.vector.scalar_tensor_tensor(delta[:, slot, :, :], delta[:, slot, :, :], 0.0, sp[:, :, :],
                                               ALU.max, ALU.add).then_inc(delta_ready.sem, 1)

            def make_u(k, slot):
                dve.wait_ge(delta_ready.sem, delta_ready.at(k))
                dve.wait_ge(xc_ready.sem, xc_ready.at(k))
                nc.vector.tensor_tensor(u[:, slot, :, :], delta[:, slot, :, :], xc[:, slot, :, :],
                                        ALU.mult).then_inc(u_ready.sem, 1)

            def drive(c, slot, n):
                dve.wait_ge(b_ready.sem, b_ready.at(c, n + 1))
                if n == 0:
                    dve.wait_ge(u_ready.sem, u_ready.at(c))
                dve.wait_ge(scan_done.sem, scan_done.at(c, n - 1))
                nc.vector.tensor_tensor(dBx[:, n % 2, :, :], u[:, slot, :, :],
                                        ps_b[:, n % 2:n % 2 + 1, :].to_broadcast((P, DB, TC)),
                                        ALU.mult).then_inc(dbx_done.sem, 1)

            def scan(c, n, keep_col):
                dve.wait_ge(dA_ready.sem, dA_ready.at(c, n + 1))
                dve.wait_ge(dbx_done.sem, dbx_done.at(c, n + 1))
                dve.wait_ge(carry_done.sem, carry_done.at(c - 1, n + 1))
                dve.wait_ge(reduce_done.sem, reduce_done.at(c, n - 1))
                for d in range(DB):
                    ins = nc.vector.tensor_tensor_scan(h[:, n % 2, d, :], dA[:, n % 2, d, :], dBx[:, n % 2, d, :],
                                                       h_in[:, n, d:d + 1], ALU.mult, ALU.add)
                ins.then_inc(scan_done.sem, 1)
                dve.wait_ge(scan_done.sem, scan_done.at(c, n + 1))
                if keep_col is None:
                    ins = nc.vector.tensor_copy(h_in[:, n, :], h[:, n % 2, :, TC - 1])
                else:
                    ins = nc.vector.tensor_scalar(h_in[:, n, :], h[:, n % 2, :, TC - 1], keep_col, None, ALU.mult)
                ins.then_inc(carry_done.sem, 1)

            def weigh(c, n):
                dve.wait_ge(c_ready.sem, c_ready.at(c, n + 1))
                dve.wait_ge(carry_done.sem, carry_done.at(c, n + 1))
                nc.vector.tensor_tensor(h[:, n % 2, :, :], h[:, n % 2, :, :],
                                        ps_c[:, :].rearrange("p (o t) -> p o t", o=1).to_broadcast((P, DB, TC)),
                                        ALU.mult).then_inc(hc_done.sem, 1)

            def gate_out(c, slot):
                dve.wait_ge(reduce_done.sem, reduce_done.at(c))
                dve.wait_ge(y_out.sem, y_out.at(c - 1))
                for d in range(DB):
                    ins = nc.vector.scalar_tensor_tensor(yg[:, d, :], xc[:, slot, d, :], d_skip[:, d:d + 1],
                                                         ps_y[:, d, :], ALU.mult, ALU.add)
                ins.then_inc(y_taken.sem, 1)
                dve.wait_ge(y_taken.sem, y_taken.at(c))
                dve.wait_ge(sz_ready.sem, sz_ready.at(c))
                nc.vector.tensor_tensor(yg[:, :, :], yg[:, :, :], sz[:, slot, :, :], ALU.mult).then_inc(ygated.sem, 1)

            for t in (conv_step, delta_ready, dbx_done, scan_done, carry_done, reduce_done, y_taken, ygated):
                t.credit(dve)
            nc.vector.memset(xraw[:, :, 0:TAPS - 1], 0.0).then_inc(zeroed.sem, 1)
            nc.vector.memset(h_in[:, :, :], 0.0).then_inc(zeroed.sem, 1)
            dve.wait_ge(zeroed.sem, 2)
            dve.wait_ge(consts.sem, 16 * (CONSTS - 1))
            for t in range(TAPS):
                conv_tap(0, 0, t)
            halo(0, None)
            make_delta(0, 0)
            make_u(0, 0)
            with dve.Fori(0, CHUNKS // 2) as i:
                for s in range(2):
                    c, k, f = 2 * i + s, 2 * i + s + 1, 1 - s
                    keep_col = keep_sb[:, bass.ds(i, 1)]
                    drive(c, s, 0)
                    for n in range(NST):
                        if n + 1 < NST:
                            drive(c, s, n + 1)
                        if n >= 1:
                            weigh(c, n - 1)
                        scan(c, n, keep_col if s else None)
                        if DB <= n < DB + TAPS:
                            if n == DB:
                                dve.wait_ge(ygated.sem, ygated.at(k - 2))
                            conv_tap(k, f, n - DB)
                        elif n == DB + TAPS:
                            halo(k, None if s else keep_col)
                        elif n == IN + 6:
                            make_delta(k, f)
                    weigh(c, NST - 1)
                    make_u(k, f)
                    gate_out(c, s)
    nc.clear_and_free_semaphores(sems)
    nc.all_engine_barrier()


EPS = 1e-5
NT = TOKENS // P


def tree_ffn(nc, y_scr, x_rows, W_outT, F_inT, F_bias, F_outT, ident, x2_rows, x2_T):
    DI, PAR, DEPTH = 512, 8, 7
    NODES = 2 ** (DEPTH + 1) - 1
    WIDTH = PAR * NODES
    DB = DI // P
    LB = 4
    LC = WIDTH // LB
    NB = -(-WIDTH // P)
    TAIL = WIDTH - (NB - 1) * P
    TG = NB // 4
    TR = TG + 2

    y_view = y_scr.rearrange("(d p) t -> p d t", p=P)
    x2T_view = x2_T.rearrange("(k p) t -> p k t", p=P)

    sems = []
    with ExitStack() as ctx:
        def sb(name, shape, dt=F32):
            return ctx.enter_context(nc.sbuf_tensor(name, shape, dt))

        def pb(name, shape):
            return ctx.enter_context(nc.psum_tensor(name, shape, F32))

        def tally(name, per=1, ahead=0):
            sems.append(nc.alloc_semaphore(name))
            return Tally(sems[-1], per, ahead)

        w_out = sb("w_out", [P, DB, DM])
        f_in = sb("f_in", [P, KD, WIDTH])
        f_bias = sb("f_bias", [P, WIDTH])
        f_out = sb("f_out", [P, NB, DM])
        idn = sb("idn2", [P, P])
        yt = sb("yt", [P, 2, DB, P])
        xin = sb("xin", [P, 2, DM])
        r1 = sb("r1", [P, 2, DM])
        x1 = sb("x1", [P, 2, DM])
        x1T = sb("x1T", [P, 2, KD, P])
        lg = sb("lg", [P, 2, PAR, NODES])
        acts = sb("acts", [P, 2, PAR, NODES])
        reach = sb("reach", [P, 2, PAR, NODES])
        mT = sb("mT", [P, NB, P])
        r2 = sb("r2", [P, DM])
        x2 = sb("x2", [P, 2, DM])
        x2T = sb("x2T", [P, 2, KD, P])
        stats = sb("stats2", [P, 2, 6])
        mv = sb("mv2", [P, 2, 2])
        rstd = sb("rstd2", [P, 2, 1])
        nhalf = sb("nhalf2", [P, 1])
        eps_sb = sb("eps2", [P, 1])
        ps_l = pb("ps_l", [P, LB, 512])
        ps_o = pb("ps_o", [P, 512])
        ps_d = pb("ps_d", [P, 512])
        ps_t = pb("ps_t", [P, 2, 4, P])

        consts = tally("consts2")
        in_ld = [tally("in_ld0", 32), tally("in_ld1", 32)]
        ready0 = tally("ready0", 3)
        nh_set = tally("nh_set")
        op_ps = tally("op_ps")
        lg_ps = tally("lg_ps")
        fo_ps = tally("fo_ps", 1, 1)
        tr_ps = tally("tr_ps", TR, 1)
        tr_ev = tally("tr_ev", TR, 1)
        sum1 = tally("sum1", 1, 1)
        stat_seen = tally("stat_seen")
        stat1 = tally("stat1")
        aggr1 = tally("aggr1")
        add1 = tally("add1")
        pow1 = tally("pow1")
        x1_ready = tally("x1_ready")
        kept = tally("kept")
        lg_ready = tally("lg_ready", 1, 1)
        silu_done = tally("silu_done")
        tree = tally("tree", 2 * DEPTH)
        masked = tally("masked", 1, 1)
        sum2 = tally("sum2", 1, 1)
        stat2 = tally("stat2")
        aggr2 = tally("aggr2")
        add2 = tally("add2")
        pow2 = tally("pow2")
        x2_ready = tally("x2_ready", 1, 1)
        x2_out = [tally("x2_out0", 16, 1), tally("x2_out1", 16, 1)]
        x2T_out = [tally("x2T_out0", 16, 1), tally("x2T_out1", 16, 1)]
        NCONST = 6

        block = ctx.enter_context(nc.Block())

        @block.sync
        def _(sp):
            for dst, src in (
                (w_out[:, :, :], W_outT.rearrange("(d p) n -> p d n", p=P)),
                (f_in[:, :, :], F_inT.rearrange("(k p) n -> p k n", p=P)),
                (f_bias[:, :], F_bias.rearrange("(o n) -> o n", o=1).to_broadcast((P, WIDTH))),
                (f_out[:, 0:NB - 1, :], F_outT[0:(NB - 1) * P, :].rearrange("(b p) n -> p b n", p=P)),
                (f_out[0:TAIL, NB - 1, :], F_outT[(NB - 1) * P:WIDTH, :]),
                (idn[:, :], ident),
            ):
                sp.dma_start(dst, src).then_inc(consts.sem, 16)

            def load(slot, col):
                sp.dma_start(yt[:, slot, :, :], y_view[:, :, col]).then_inc(in_ld[slot].sem, 16)
                sp.dma_start(xin[:, slot, :], x_rows[col, :]).then_inc(in_ld[slot].sem, 16)

            load(0, slice(0, P))
            load(1, slice(P, 2 * P))
            for o in x2_out + x2T_out:
                o.credit(sp)
            sp.wait_ge(sum1.sem, sum1.at(0))
            load(0, slice(2 * P, 3 * P))
            with sp.Fori(0, NT // 2) as i:
                ahead = [sp.snap(((2 * i + s + 3) % NT) * P) for s in range(2)]
                here = [sp.snap((2 * i + s) * P) for s in range(2)]
                prev = [sp.snap(((2 * i + s + NT - 1) % NT) * P) for s in range(2)]
                for s in range(2):
                    t = 2 * i + s
                    sp.wait_ge(sum1.sem, sum1.at(t + 1))
                    load(1 - s, bass.ds(ahead[s], P))
                    sp.wait_ge(tr_ev.sem, tr_ev.at(t))
                    sp.dma_start(x2T_view[:, :, bass.ds(prev[s], P)], x2T[:, 1 - s, :, :]).then_inc(x2T_out[1 - s].sem, 16)
                    sp.wait_ge(x2_ready.sem, x2_ready.at(t))
                    sp.dma_start(x2_rows[bass.ds(here[s], P), :], x2[:, s, :]).then_inc(x2_out[s].sem, 16)
            for s in range(2):
                sp.wait_ge(x2T_out[s].sem, x2T_out[s].at(NT // 2 - 1))
            sp.wait_ge(tr_ev.sem, tr_ev.at(NT, 1))
            sp.dma_start(x2T_view[:, :, TOKENS - P:], x2T[:, 1, :, :]).then_inc(x2T_out[1].sem, 16)
            sp.wait_ge(x2T_out[1].sem, x2T_out[1].at(NT // 2))
            for s in range(2):
                sp.wait_ge(x2_out[s].sem, x2_out[s].at(NT // 2 - 1))
            for s in range(2):
                sp.wait_ge(in_ld[s].sem, 32 * (NT // 2 + 2 - s))

        @block.tensor
        def _(pe):
            def out_proj(t, s, loads):
                pe.wait_ge(in_ld[s].sem, 32 * loads)
                pe.wait_ge(sum1.sem, sum1.at(t - 1))
                for d in range(DB):
                    last = nc.tensor.matmul(ps_o[:, 0:DM], yt[:, s, d, :], w_out[:, d, :], start=d == 0, stop=d == DB - 1)
                last.then_inc(op_ps.sem, 1)

            def turn(t, use, blocks):
                pe.wait_ge(tr_ev.sem, tr_ev.at(t, use - 1))
                for b, (rows, src) in enumerate(blocks):
                    last = nc.tensor.transpose(ps_t[0:rows, use % 2, b, :], src, idn[:, :])
                last.then_inc(tr_ps.sem, 1)

            def turn_x1(step, t, s):
                pe.wait_ge(x1_ready.sem, x1_ready.at(t))
                turn(step, 0, [(P, x1[:, s, k * P:(k + 1) * P]) for k in range(KD)])

            def logits(step, t, s, uses=1):
                pe.wait_ge(tr_ev.sem, tr_ev.at(step, uses))
                pe.wait_ge(lg_ready.sem, lg_ready.at(t - 1))
                for b in range(LB):
                    for k in range(KD):
                        last = nc.tensor.matmul(ps_l[:, b, 0:LC], x1T[:, s, k, :], f_in[:, k, b * LC:(b + 1) * LC],
                                                start=k == 0, stop=k == KD - 1)
                last.then_inc(lg_ps.sem, 1)

            def turn_nodes(t, s):
                pe.wait_ge(masked.sem, masked.at(t))
                flat = acts[:, s, :, :].rearrange("p a n -> p (a n)")
                for g in range(TG):
                    blocks = [(min(P, WIDTH - b * P), flat[:, b * P:min((b + 1) * P, WIDTH)]) for b in range(4 * g, 4 * g + 4)]
                    turn(t, 1 + g, blocks)

            def nodes_out(t, s):
                pe.wait_ge(tr_ev.sem, tr_ev.at(t, 1 + TG))
                pe.wait_ge(sum2.sem, sum2.at(t - 1))
                for b in range(NB):
                    rows = min(P, WIDTH - b * P)
                    last = nc.tensor.matmul(ps_d[:, 0:DM], mT[0:rows, b, :], f_out[0:rows, b, :], start=b == 0, stop=b == NB - 1)
                last.then_inc(fo_ps.sem, 1)

            def turn_x2(step, t, s):
                pe.wait_ge(x2_ready.sem, x2_ready.at(t))
                turn(step, 1 + TG, [(P, x2[:, s, k * P:(k + 1) * P]) for k in range(KD)])

            pe.sem_inc(tr_ps.sem, TR - 1)
            pe.wait_ge(consts.sem, 16 * NCONST)
            out_proj(0, 0, 1)
            out_proj(1, 1, 1)
            pe.wait_ge(x1_ready.sem, x1_ready.at(0))
            pe.wait_ge(ready0.sem, 3)
            for k in range(KD):
                last = nc.tensor.transpose(ps_t[:, 1, k, :], x1[:, 0, k * P:(k + 1) * P], idn[:, :])
            last.then_inc(tr_ps.sem, 1)
            logits(-1, 0, 0, TR)
            with pe.Fori(0, NT // 2) as i:
                for s in range(2):
                    t = 2 * i + s
                    turn_x1(t, t + 1, 1 - s)
                    out_proj(t + 2, s, i + 2)
                    logits(t, t + 1, 1 - s)
                    turn_nodes(t, s)
                    nodes_out(t, s)
                    turn_x2(t, t - 1, 1 - s)
            turn_x2_last = [(P, x2[:, 1, k * P:(k + 1) * P]) for k in range(KD)]
            pe.wait_ge(x2_ready.sem, x2_ready.at(NT - 1))
            turn(NT, 0, turn_x2_last)

        @block.scalar
        def _(act):
            def take(t, use, dst, src):
                act.wait_ge(tr_ps.sem, tr_ps.at(t, use + 1))
                return nc.scalar.activation(dst, src, ACT.Copy)

            def take_x(step, use, dst):
                take(step, use, dst, ps_t[:, use % 2, 0:KD, :]).then_inc(tr_ev.sem, 1)

            def gate(t, s, first=False):
                act.wait_ge(lg_ready.sem, lg_ready.at(t))
                if not first:
                    act.wait_ge(tr_ps.sem, tr_ps.at(t - 2, 1 + TG))
                nc.scalar.activation(acts[:, s, :, :], lg[:, s, :, :], ACT.Silu).then_inc(silu_done.sem, 1)

            def take_nodes(t, s):
                act.wait_ge(fo_ps.sem, fo_ps.at(t - 1))
                for g in range(TG):
                    whole = 4 if g < TG - 1 else 3
                    ins = take(t, 1 + g, mT[:, 4 * g:4 * g + whole, :], ps_t[:, (1 + g) % 2, 0:whole, :])
                    if whole < 4:
                        ins = nc.scalar.activation(mT[0:TAIL, NB - 1, :], ps_t[0:TAIL, (1 + g) % 2, 3, :], ACT.Copy)
                    ins.then_inc(tr_ev.sem, 1)

            fo_ps.credit(act)
            act.sem_inc(tr_ev.sem, TR - 1)
            act.wait_ge(tr_ps.sem, tr_ps.at(-1, TR))
            nc.scalar.activation(x1T[:, 0, :, :], ps_t[:, 1, 0:KD, :], ACT.Copy).then_inc(tr_ev.sem, 1)
            gate(0, 0, True)
            with act.Fori(0, NT // 2) as i:
                for s in range(2):
                    t = 2 * i + s
                    take_x(t, 0, x1T[:, 1 - s, :, :])
                    gate(t + 1, 1 - s)
                    take_nodes(t, s)
                    act.wait_ge(x2T_out[1 - s].sem, x2T_out[1 - s].at(i - 1))
                    take_x(t, 1 + TG, x2T[:, 1 - s, :, :])
            act.wait_ge(x2T_out[1].sem, x2T_out[1].at(NT // 2 - 1))
            take_x(NT, 0, x2T[:, 1, :, :])

        @block.gpsimd
        def _(pool):
            def inv_std(t, n, aggr, add, pw):
                pool.wait_ge(aggr.sem, aggr.at(t))
                nc.gpsimd.tensor_tensor(rstd[:, n, :], mv[:, n, 1:2], eps_sb[:, :], ALU.add).then_inc(add.sem, 1)
                pool.wait_ge(add.sem, add.at(t))
                nc.gpsimd.tensor_tensor(rstd[:, n, :], rstd[:, n, :], nhalf[:, :], ALU.pow).then_inc(pw.sem, 1)

            nc.gpsimd.memset(nhalf[:, :], -0.5).then_inc(nh_set.sem, 1)
            nc.gpsimd.memset(eps_sb[:, :], EPS).then_inc(nh_set.sem, 1)
            pool.wait_ge(nh_set.sem, 2)
            inv_std(0, 0, aggr1, add1, pow1)
            inv_std(1, 0, aggr1, add1, pow1)
            with pool.Fori(0, NT // 2) as i:
                for s in range(2):
                    t = 2 * i + s
                    inv_std(t + 2, 0, aggr1, add1, pow1)
                    inv_std(t, 1, aggr2, add2, pow2)

        @block.vector
        def _(dve):
            def moments(t, n, r, stat, aggr):
                nc.vector.bn_stats(stats[:, n, :], r).then_inc(stat.sem, 1)
                dve.wait_ge(stat.sem, stat.at(t))
                dve.sem_inc(stat_seen.sem)
                nc.vector.bn_aggr(mv[:, n, :], stats[:, n, :]).then_inc(aggr.sem, 1)

            def norm1(t, s, first=False):
                dve.wait_ge(op_ps.sem, op_ps.at(t))
                nc.vector.tensor_tensor(r1[:, s, :], ps_o[:, 0:DM], xin[:, s, :], ALU.add).then_inc(sum1.sem, 1)
                dve.wait_ge(sum1.sem, sum1.at(t))
                moments(t, 0, r1[:, s, :], stat1, aggr1)
                dve.wait_ge(pow1.sem, pow1.at(t))
                if not first:
                    dve.wait_ge(tr_ps.sem, tr_ps.at(t - 3, 1))
                    dve.wait_ge(kept.sem, kept.at(t - 2))
                nc.vector.tensor_scalar(x1[:, s, :], r1[:, s, :], mv[:, 0, 0:1], rstd[:, 0, :], ALU.subtract,
                                        ALU.mult).then_inc(x1_ready.sem, 1)
                dve.wait_ge(x1_ready.sem, x1_ready.at(t))

            def path(t, s):
                dve.wait_ge(lg_ps.sem, lg_ps.at(t))
                flat = lg[:, s, :, :].rearrange("p a n -> p (a n)").rearrange("p (b n) -> p b n", b=LB)
                nc.vector.tensor_tensor(flat, ps_l[:, :, 0:LC], f_bias[:, :].rearrange("p (b n) -> p b n", b=LB),
                                        ALU.add).then_inc(lg_ready.sem, 1)
                dve.wait_ge(lg_ready.sem, lg_ready.at(t))
                for d in range(DEPTH):
                    lo, n = 2 ** d - 1, 2 ** d
                    kids = reach[:, s, :, 2 * n - 1:4 * n - 1].rearrange("p a (n two) -> p a n two", two=2)
                    here = reach[:, s, :, lo:lo + n]
                    if d:
                        dve.wait_ge(tree.sem, tree.at(t, 2 * d))
                    nc.vector.scalar_tensor_tensor(kids[:, :, :, 1], lg[:, s, :, lo:lo + n], 0.0, here, ALU.is_gt,
                                                   ALU.mult).then_inc(tree.sem, 1)
                    dve.wait_ge(tree.sem, tree.at(t, 2 * d + 1))
                    nc.vector.tensor_tensor(kids[:, :, :, 0], here, kids[:, :, :, 1], ALU.subtract).then_inc(tree.sem, 1)
                dve.wait_ge(tree.sem, tree.at(t))
                dve.wait_ge(silu_done.sem, silu_done.at(t))
                nc.vector.tensor_tensor(acts[:, s, :, :], acts[:, s, :, :], reach[:, s, :, :], ALU.mult).then_inc(masked.sem, 1)

            def keep_x1(t, s):
                dve.wait_ge(x2_ready.sem, x2_ready.at(t - 1))
                nc.vector.tensor_copy(r2[:, :], x1[:, s, :]).then_inc(kept.sem, 1)

            def norm2(t, s, i):
                dve.wait_ge(fo_ps.sem, fo_ps.at(t))
                dve.wait_ge(kept.sem, kept.at(t))
                nc.vector.tensor_tensor(r2[:, :], ps_d[:, 0:DM], r2[:, :], ALU.add).then_inc(sum2.sem, 1)
                dve.wait_ge(sum2.sem, sum2.at(t))
                moments(t, 1, r2[:, :], stat2, aggr2)
                dve.wait_ge(pow2.sem, pow2.at(t))
                dve.wait_ge(x2_out[s].sem, x2_out[s].at(i - 1))
                dve.wait_ge(tr_ps.sem, tr_ps.at(t - 1))
                nc.vector.tensor_scalar(x2[:, s, :], r2[:, :], mv[:, 1, 0:1], rstd[:, 1, :], ALU.subtract,
                                        ALU.mult).then_inc(x2_ready.sem, 1)
                dve.wait_ge(x2_ready.sem, x2_ready.at(t))

            for t in (sum1, lg_ready, masked, sum2, x2_ready):
                t.credit(dve)
            nc.vector.memset(reach[:, 0, :, 0:1], 1.0).then_inc(ready0.sem, 1)
            nc.vector.memset(reach[:, 1, :, 0:1], 1.0).then_inc(ready0.sem, 1)
            nc.vector.memset(x2[:, 1, :], 0.0).then_inc(ready0.sem, 1)
            dve.wait_ge(ready0.sem, 3)
            dve.wait_ge(consts.sem, 16 * NCONST)
            norm1(0, 0, True)
            norm1(1, 1, True)
            path(0, 0)
            with dve.Fori(0, NT // 2) as i:
                for s in range(2):
                    t = 2 * i + s
                    keep_x1(t, s)
                    norm1(t + 2, s)
                    path(t + 1, 1 - s)
                    norm2(t, s, i)
    nc.clear_and_free_semaphores(sems)
    nc.all_engine_barrier()


F32R = mybir.dt.float32r
HEADS, KV, HD = 16, 4, 64
GROUP = HEADS // KV


def qkv(nc, x2_T, Wqk, Wv, rope_q, rope_k, q_scr, k_scr, v_scr):
    TC = 512
    CHUNKS = TOKENS // TC
    PAIRS = KV + 1
    HALF = HD // 2
    PER = TC // P
    xT_view = x2_T.rearrange("(k p) t -> p k t", p=P)
    v_view = v_scr.rearrange("(n p) d -> p n d", p=P)

    sems = []
    with ExitStack() as ctx:
        def sb(name, shape, dt=F32):
            return ctx.enter_context(nc.sbuf_tensor(name, shape, dt))

        def pb(name, shape):
            return ctx.enter_context(nc.psum_tensor(name, shape, F32))

        def tally(name, per=1, ahead=0):
            sems.append(nc.alloc_semaphore(name))
            return Tally(sems[-1], per, ahead)

        w_qk = sb("w_qk", [P, KD, 2 * PAIRS, P])
        w_v = sb("w_v", [P, KD, KV * HD])
        rope = sb("rope", [P, 2, 4, LENGTH])
        xt = sb("xt3", [P, 2, KD, TC])
        even = sb("even", [P, 2, 2, TC])
        odd = sb("odd", [P, 2, 2, TC])
        rot = sb("rot", [P, 2, 2, TC])
        hi = sb("hi3", [P, 2, 2, TC], F32R)
        lo = sb("lo3", [P, 2, 2, TC], F32R)
        v_sb = sb("v_sb", [P, 2, PER, KV * HD])
        ps_qk = pb("ps_qk", [P, 2, 2, TC])
        ps_v = pb("ps_v", [P, PER, KV * HD])

        consts = tally("consts3")
        xt_ld = [tally("xt3_ld0"), tally("xt3_ld1")]
        qk_ps = tally("qk_ps", PAIRS)
        v_ps = tally("v_ps")
        v_ev = tally("v_ev", 1, 1)
        even_done = tally("even_done", PAIRS)
        odd_done = tally("odd_done", PAIRS, 1)
        rot_done = tally("rot_done", PAIRS)
        hi_done = tally("hi_done", PAIRS)
        lo_done = tally("lo_done", PAIRS, 1)
        qk_out = [tally("qk_out0", 16 * 24, 1), tally("qk_out1", 16 * 24, 1)]
        v_out = [tally("v_out0", 16, 1), tally("v_out1", 16, 1)]
        NCONST = 4

        def stores_before(s, p):
            r = s * PAIRS + p
            return sum(8 if q % PAIRS == KV else 4 for q in range(r) if q % 2 == r % 2)

        block = ctx.enter_context(nc.Block())

        @block.sync
        def _(sp):
            for dst, src in (
                (w_qk[:, :, :, :], Wqk.rearrange("(k p) b n -> p k b n", p=P)),
                (w_v[:, :, :], Wv.rearrange("(k p) n -> p k n", p=P)),
                (rope[:, 0, :, :], rope_q),
                (rope[:, 1, :, :], rope_k),
            ):
                sp.dma_start(dst, src).then_inc(consts.sem, 16)
            for k in range(2):
                sp.dma_start(xt[:, k, :, :], xT_view[:, :, k * TC:(k + 1) * TC]).then_inc(xt_ld[k].sem, 16)
            for o in qk_out + v_out:
                o.credit(sp)
            with sp.Fori(0, CHUNKS // 2) as i:
                ahead = [sp.snap(((2 * i + s + 2) % CHUNKS) * TC) for s in range(2)]
                batch = sp.snap(i // (CHUNKS // 4))
                pos = [sp.snap(((2 * i + s) % (CHUNKS // 2)) * TC) for s in range(2)]
                first = [sp.snap((2 * i + s) * PER) for s in range(2)]
                q_row = [sp.snap(batch * HEADS + GROUP * g) for g in range(KV)]
                k_row = sp.snap(batch * KV)
                for s in range(2):
                    c = 2 * i + s
                    for p in range(PAIRS):
                        slot = (s * PAIRS + p) % 2
                        sp.wait_ge(lo_done.sem, lo_done.at(c, p + 1))
                        for part, src in enumerate((hi, lo)):
                            for eo in range(2):
                                from_sb = src[:, slot, eo, :].bitcast(F32)
                                if p < KV:
                                    row = part * HD + eo * HALF
                                    to = q_scr[bass.ds(q_row[p], GROUP), row:row + HALF, bass.ds(pos[s], TC)]
                                    sp.dma_start(to, from_sb).then_inc(qk_out[slot].sem, 16)
                                else:
                                    for copy in range(2):
                                        row = copy * HD + eo * HALF
                                        to = k_scr[bass.ds(k_row, KV), part, row:row + HALF, bass.ds(pos[s], TC)]
                                        sp.dma_start(to, from_sb).then_inc(qk_out[slot].sem, 16)
                    sp.wait_ge(v_ev.sem, v_ev.at(c))
                    sp.dma_start(v_view[:, bass.ds(first[s], PER), :], v_sb[:, s, :, :]).then_inc(v_out[s].sem, 16)
                    sp.dma_start(xt[:, s, :, :], xT_view[:, :, bass.ds(ahead[s], TC)]).then_inc(xt_ld[s].sem, 16)
            for s in range(2):
                sp.wait_ge(xt_ld[s].sem, 16 * (CHUNKS // 2 + 1))
                sp.wait_ge(v_out[s].sem, v_out[s].at(CHUNKS // 2 - 1))
                sp.wait_ge(qk_out[s].sem, qk_out[s].at(CHUNKS // 2 - 1))

        @block.tensor
        def _(pe):
            pe.wait_ge(consts.sem, 16 * NCONST)
            with pe.Fori(0, CHUNKS // 2) as i:
                for s in range(2):
                    c = 2 * i + s
                    pe.wait_ge(xt_ld[s].sem, 16 * (i + 1))
                    for p in range(PAIRS):
                        slot = (s * PAIRS + p) % 2
                        pe.wait_ge(odd_done.sem, odd_done.at(c, p - 1))
                        for eo in range(2):
                            for k in range(KD):
                                last = nc.tensor.matmul(ps_qk[:, slot, eo, :], w_qk[:, k, 2 * p + eo, :], xt[:, s, k, :],
                                                        start=k == 0, stop=k == KD - 1)
                        last.then_inc(qk_ps.sem, 1)
                    pe.wait_ge(v_ev.sem, v_ev.at(c - 1))
                    for n in range(PER):
                        for k in range(KD):
                            last = nc.tensor.matmul(ps_v[:, n, :], xt[:, s, k, n * P:(n + 1) * P], w_v[:, k, :],
                                                    start=k == 0, stop=k == KD - 1)
                    last.then_inc(v_ps.sem, 1)

        @block.scalar
        def _(act):
            v_ev.credit(act)
            with act.Fori(0, CHUNKS // 2) as i:
                for s in range(2):
                    c = 2 * i + s
                    for p in range(PAIRS):
                        slot = (s * PAIRS + p) % 2
                        act.wait_ge(rot_done.sem, rot_done.at(c, p + 1))
                        act.wait_ge(qk_out[slot].sem, qk_out[slot].at(i, 16 * stores_before(s, p)))
                        nc.scalar.activation(hi[:, slot, :, :], rot[:, slot, :, :], ACT.Copy).then_inc(hi_done.sem, 1)
                    act.wait_ge(v_ps.sem, v_ps.at(c))
                    act.wait_ge(v_out[s].sem, v_out[s].at(i - 1))
                    nc.scalar.activation(v_sb[:, s, :, :], ps_v[:, :, :], ACT.Copy).then_inc(v_ev.sem, 1)

        @block.gpsimd
        def _(pool):
            lo_done.credit(pool)
            with pool.Fori(0, CHUNKS // 2) as i:
                for s in range(2):
                    c = 2 * i + s
                    for p in range(PAIRS):
                        slot = (s * PAIRS + p) % 2
                        pool.wait_ge(hi_done.sem, hi_done.at(c, p + 1))
                        nc.gpsimd.tensor_tensor(lo[:, slot, :, :], rot[:, slot, :, :], hi[:, slot, :, :].bitcast(F32),
                                                ALU.subtract).then_inc(lo_done.sem, 1)

        @block.vector
        def _(dve):
            odd_done.credit(dve)
            dve.wait_ge(consts.sem, 16 * NCONST)
            with dve.Fori(0, CHUNKS // 2) as i:
                pos = [dve.snap(((2 * i + s) % (CHUNKS // 2)) * TC) for s in range(2)]
                for s in range(2):
                    c = 2 * i + s
                    for p in range(PAIRS):
                        slot = (s * PAIRS + p) % 2
                        kind = p // KV
                        dve.wait_ge(qk_ps.sem, qk_ps.at(c, p + 1))
                        for eo, dst, done in ((0, even, even_done), (1, odd, odd_done)):
                            nc.vector.tensor_tensor(dst[:, slot, :, :],
                                                    ps_qk[:, slot, eo:eo + 1, :].to_broadcast((P, 2, TC)),
                                                    rope[:, kind, 2 * eo:2 * eo + 2, bass.ds(pos[s], TC)],
                                                    ALU.mult).then_inc(done.sem, 1)
                        dve.wait_ge(even_done.sem, even_done.at(c, p + 1))
                        dve.wait_ge(odd_done.sem, odd_done.at(c, p + 1))
                        dve.wait_ge(lo_done.sem, lo_done.at(c, p - 1))
                        nc.vector.tensor_tensor(rot[:, slot, :, :], even[:, slot, :, :], odd[:, slot, :, :],
                                                ALU.add).then_inc(rot_done.sem, 1)
    nc.clear_and_free_semaphores(sems)
    nc.all_engine_barrier()


def attention(nc, q_scr, k_scr, v_scr, ident, causal, attn):
    QT = LENGTH // P
    CW = 512
    CB = CW // P
    NCH = [-(-(r + 1) // CB) for r in range(QT)]
    CUM = [sum(NCH[:r]) for r in range(QT + 1)]
    PER = CUM[QT]
    RING = 4
    NHEADS = BATCH * HEADS
    NGROUPS = BATCH * KV
    assert PER % RING == 0
    attn_view = attn.rearrange("(n p) d -> p n d", p=P)

    def blocks(r, c):
        return min(CB, r + 1 - c * CB)

    sems = []
    with ExitStack() as ctx:
        def sb(name, shape, dt=F32):
            return ctx.enter_context(nc.sbuf_tensor(name, shape, dt))

        def pb(name, shape):
            return ctx.enter_context(nc.psum_tensor(name, shape, F32))

        def tally(name, per=1, ahead=0):
            sems.append(nc.alloc_semaphore(name))
            return Tally(sems[-1], per, ahead)

        idn = sb("idn3", [P, P])
        idn_r = sb("idn_r", [P, P], F32R)
        mask = sb("mask", [P, P])
        mask_r = sb("mask_r", [P, P], F32R)
        qbuf = sb("qbuf", [P, QT, P], F32R)
        kbuf = sb("kbuf", [P, 2, 2, LENGTH], F32R)
        qstage = sb("qstage", [P, QT, P])
        kstage = sb("kstage", [P, 2, LENGTH])
        v1 = sb("v1", [P, BATCH * QT, KV, HD + 1])
        probs = sb("probs", [P, RING, CB, P])
        probsT = sb("probsT", [P, RING, CB, P])
        pmax = sb("pmax", [P, 2, 4])
        negm = sb("negm", [P, 2, 1])
        rinv = sb("rinv", [P, 2, 1])
        ostage = sb("ostage", [P, QT, HD])
        ps_s = pb("ps_s", [P, RING, CW])
        ps_t = pb("ps_t3", [P, 2, CB, P])
        ps_o = pb("ps_o3", [P, 2, CW])

        consts = tally("consts3b")
        rounded = tally("rounded")
        ones_set = tally("ones_set")
        q_ld = [tally("q_ld%d" % j) for j in range(4)]
        k_ld = tally("k_ld")
        q_ready = tally("q_ready", 4)
        k_ready = tally("k_ready")
        pool_seen = tally("pool_seen")
        s_done = tally("s_done", PER, 1)
        t_done = tally("t_done", PER, 1)
        pv_done = tally("pv_done", PER, 1)
        exp_done = tally("exp_done", PER, 1)
        ev = [tally("ev_dve", PER // 2, 1), tally("ev_act", PER // 2, 1)]
        cmax = tally("cmax", PER)
        m_done = tally("m_done", QT)
        r_done = tally("r_done", QT)
        o_done = tally("o_done", QT, 1)
        o_out = [tally("o_out0", 16, 1), tally("o_out1", 16, 1)]
        NCONST = 2 + KV

        def at_chunk(t, hx, u):
            return t.at(hx, u + 1)

        block = ctx.enter_context(nc.Block())

        @block.sync
        def _(sp):
            sp.dma_start(idn[:, :], ident).then_inc(consts.sem, 16)
            sp.dma_start(mask[:, :], causal).then_inc(consts.sem, 16)
            sp.dma_start(kstage[:, :, :], k_scr[0].rearrange("l p t -> p l t")).then_inc(k_ld.sem, 16)
            for j in range(4):
                sp.dma_start(qstage[:, 4 * j:4 * j + 4, :].rearrange("p n t -> p (n t)"),
                             q_scr[0, :, j * CW:(j + 1) * CW]).then_inc(q_ld[j].sem, 16)
            for kv in range(KV):
                with nc.allow_non_contiguous_dma(reason="values of a head, once"):
                    sp.dma_start(v1[:, :, kv, 0:HD],
                                 v_scr[:, kv * HD:(kv + 1) * HD].rearrange("(n p) d -> p n d", p=P)).then_inc(consts.sem, 16)
            for o in o_out:
                o.credit(sp)
            with sp.Fori(0, NGROUPS) as g:
                group = sp.snap((g + 1) % NGROUPS)
                sp.wait_ge(k_ready.sem, k_ready.at(g))
                sp.dma_start(kstage[:, :, :], k_scr[bass.ds(group, 1)].rearrange("g l p t -> p (g l) t")).then_inc(k_ld.sem, 16)
                with sp.Fori(0, GROUP) as j4:
                    hx = sp.snap(g * GROUP + j4)
                    nxt = sp.snap((hx + 1) % NHEADS)
                    first = sp.snap((hx // HEADS) * QT)
                    col = sp.snap((hx % HEADS) * HD)
                    for j in range(4):
                        sp.wait_ge(q_ready.sem, q_ready.at(hx, j + 1))
                        sp.dma_start(qstage[:, 4 * j:4 * j + 4, :].rearrange("p n t -> p (n t)"),
                                     q_scr[bass.ds(nxt, 1), :, j * CW:(j + 1) * CW].rearrange("o p t -> p (o t)"),
                                     ).then_inc(q_ld[j].sem, 16)
                        if j % 2:
                            half = j // 2
                            n = QT // 2
                            sp.wait_ge(o_done.sem, o_done.at(hx, (half + 1) * n))
                            sp.dma_start(attn_view[:, bass.ds(first + half * n, n), bass.ds(col, HD)],
                                         ostage[:, half * n:(half + 1) * n, :]).then_inc(o_out[half].sem, 16)
            for j in range(4):
                sp.wait_ge(q_ld[j].sem, 16 * (NHEADS + 1))
            sp.wait_ge(q_ready.sem, q_ready.at(NHEADS))
            sp.wait_ge(k_ready.sem, NGROUPS + 1)
            sp.wait_ge(k_ld.sem, 16 * (NGROUPS + 1))
            for half in range(2):
                sp.wait_ge(o_out[half].sem, o_out[half].at(NHEADS - 1))

        @block.tensor
        def _(pe):
            def scores(hx, kslot, r, c, head0):
                u = CUM[r] + c
                w = blocks(r, c) * P
                out = ps_s[:, u % RING, 0:w]
                pe.wait_ge(exp_done.sem, exp_done.at(head0, u - RING + 1))
                for part in range(2):
                    last = nc.tensor.matmul(out, qbuf[:, r, :],
                                            kbuf[:, bass.ds(kslot, 1), part, c * CW:c * CW + w],
                                            start=part == 0, stop=part == 1 and c < NCH[r] - 1)
                if c == NCH[r] - 1:
                    last = nc.tensor.matmul(ps_s[:, u % RING, w - P:w], idn_r[:, :], mask_r[:, :], start=False, stop=True)
                last.then_inc(s_done.sem, 1)

            def turn(hx, r, c):
                u = CUM[r] + c
                pe.wait_ge(exp_done.sem, at_chunk(exp_done, hx, u))
                pe.wait_ge(ev[u % 2].sem, ev[u % 2].at(hx, u // 2))
                for j in range(blocks(r, c)):
                    last = nc.tensor.transpose(ps_t[:, u % 2, j, :], probs[:, u % RING, j, :], idn[:, :])
                last.then_inc(t_done.sem, 1)

            def weigh(hx, first, kv, r, c):
                u = CUM[r] + c
                pe.wait_ge(ev[u % 2].sem, ev[u % 2].at(hx, u // 2 + 1))
                if c == 0:
                    pe.wait_ge(o_done.sem, o_done.at(hx, r - 1))
                for j in range(blocks(r, c)):
                    kb = c * CB + j
                    last = nc.tensor.matmul(ps_o[:, r % 2, 0:HD + 1], probsT[:, u % RING, j, :],
                                            v1[:, bass.ds(first + kb, 1), bass.ds(kv, 1), :],
                                            start=kb == 0, stop=kb == r)
                last.then_inc(pv_done.sem, 1)

            pe.wait_ge(consts.sem, 16 * NCONST)
            pe.wait_ge(rounded.sem, 2)
            pe.wait_ge(ones_set.sem, 1)
            s_done.credit(pe)
            t_done.credit(pe)
            pv_done.credit(pe)
            pe.wait_ge(k_ready.sem, 1)
            pe.wait_ge(q_ready.sem, 1)
            scores(0, 0, 0, 0, 0)
            with pe.Fori(0, NHEADS) as hx:
                kslot = pe.snap((hx // GROUP) % 2)
                kslot_next = pe.snap(((hx + 1) // GROUP) % 2)
                kv = pe.snap((hx // GROUP) % KV)
                first = pe.snap((hx // HEADS) * QT)
                for r in range(QT):
                    nxt = NCH[r + 1] if r + 1 < QT else 1
                    for c in range(max(nxt, NCH[r] + 1)):
                        if c < nxt:
                            if r + 1 < QT:
                                if (r + 1) % 4 == 0 and c == 0:
                                    pe.wait_ge(q_ready.sem, q_ready.at(hx, (r + 1) // 4 + 1))
                                scores(hx, kslot, r + 1, c, hx)
                            else:
                                pe.wait_ge(q_ready.sem, q_ready.at(hx + 1, 1))
                                pe.wait_ge(k_ready.sem, (hx + 1) // GROUP + 1)
                                scores(hx + 1, kslot_next, 0, 0, hx + 1)
                        if c < NCH[r]:
                            turn(hx, r, c)
                        if 1 <= c <= NCH[r]:
                            weigh(hx, first, kv, r, c - 1)

        @block.gpsimd
        def _(pool):
            def keys(g):
                pool.wait_ge(k_ld.sem, 16 * (g + 1))
                pool.sem_inc(pool_seen.sem)
                nc.gpsimd.tensor_copy(kbuf[:, bass.ds(g % 2, 1), :, :], kstage[:, :, :]).then_inc(k_ready.sem, 1)

            def queries(hx, j):
                pool.wait_ge(q_ld[j].sem, 16 * (hx + 1))
                pool.sem_inc(pool_seen.sem)
                nc.gpsimd.tensor_copy(qbuf[:, 4 * j:4 * j + 4, :], qstage[:, 4 * j:4 * j + 4, :]).then_inc(q_ready.sem, 1)

            keys(0)
            for j in range(4):
                queries(0, j)
            with pool.Fori(0, NGROUPS) as g:
                pool.wait_ge(s_done.sem, s_done.at(g * GROUP, 1))
                keys(g + 1)
                with pool.Fori(0, GROUP) as j4:
                    hx = pool.snap(g * GROUP + j4)
                    for j in range(4):
                        pool.wait_ge(s_done.sem, s_done.at(hx, CUM[4 * j + 4]))
                        queries(hx + 1, j)

        @block.scalar
        def _(act):
            def exps(hx, r, c):
                u = CUM[r] + c
                w = blocks(r, c) * P
                if c == 0:
                    act.wait_ge(m_done.sem, m_done.at(hx, r + 1))
                act.wait_ge(t_done.sem, t_done.at(hx, u - RING + 1))
                nc.scalar.activation(probs[:, u % RING, 0:blocks(r, c), :], ps_s[:, u % RING, 0:w], ACT.Exp,
                                     bias=negm[:, r % 2, :]).then_inc(exp_done.sem, 1)

            def take(hx, r, c):
                u = CUM[r] + c
                n = blocks(r, c)
                act.wait_ge(t_done.sem, at_chunk(t_done, hx, u))
                act.wait_ge(pv_done.sem, pv_done.at(hx, u - RING + 1))
                nc.scalar.activation(probsT[:, u % RING, 0:n, :], ps_t[:, 1, 0:n, :], ACT.Copy).then_inc(ev[1].sem, 1)

            act.wait_ge(consts.sem, 16 * NCONST)
            for dst, src in ((idn_r, idn), (mask_r, mask)):
                nc.scalar.activation(dst[:, :], src[:, :], ACT.Copy).then_inc(rounded.sem, 1)
            exp_done.credit(act)
            ev[1].credit(act)
            with act.Fori(0, NHEADS) as hx:
                for r in range(QT):
                    for c in range(NCH[r] + 1):
                        if c < NCH[r]:
                            exps(hx, r, c)
                        if c >= 1 and (CUM[r] + c - 1) % 2:
                            take(hx, r, c - 1)

        @block.vector
        def _(dve):
            def peak(hx, r, head0):
                several = NCH[r] > 1
                for c in range(NCH[r]):
                    u = CUM[r] + c
                    dve.wait_ge(s_done.sem, at_chunk(s_done, head0, u))
                    if not several:
                        dve.wait_ge(exp_done.sem, exp_done.at(head0, CUM[r - 1] if r >= 1 else CUM[QT - 1] - PER))
                        nc.vector.reduce_max(negm[:, r % 2, :], ps_s[:, u % RING, 0:blocks(r, c) * P],
                                             axis=mybir.AxisListType.X, negate=True).then_inc(m_done.sem, 1)
                        nc_inc = dve.sem_inc(cmax.sem, 1)
                    else:
                        nc.vector.reduce_max(pmax[:, r % 2, c:c + 1], ps_s[:, u % RING, 0:blocks(r, c) * P],
                                             axis=mybir.AxisListType.X).then_inc(cmax.sem, 1)
                if several:
                    dve.wait_ge(cmax.sem, cmax.at(head0, CUM[r + 1]))
                    dve.wait_ge(exp_done.sem, exp_done.at(head0, CUM[r - 1]))
                    nc.vector.reduce_max(negm[:, r % 2, :], pmax[:, r % 2, 0:NCH[r]], axis=mybir.AxisListType.X,
                                         negate=True).then_inc(m_done.sem, 1)

            def take(hx, r, c):
                u = CUM[r] + c
                n = blocks(r, c)
                dve.wait_ge(t_done.sem, at_chunk(t_done, hx, u))
                dve.wait_ge(pv_done.sem, pv_done.at(hx, u - RING + 1))
                nc.vector.tensor_copy(probsT[:, u % RING, 0:n, :], ps_t[:, 0, 0:n, :]).then_inc(ev[0].sem, 1)

            def normalise(hx, r):
                dve.wait_ge(pv_done.sem, pv_done.at(hx, CUM[r + 1]))
                nc.vector.reciprocal(rinv[:, r % 2, :], ps_o[:, r % 2, HD:HD + 1]).then_inc(r_done.sem, 1)
                dve.wait_ge(r_done.sem, r_done.at(hx, r + 1))
                if r % (QT // 2) == 0:
                    dve.wait_ge(o_out[r // (QT // 2)].sem, o_out[r // (QT // 2)].at(hx - 1))
                nc.vector.tensor_scalar(ostage[:, r, :], ps_o[:, r % 2, 0:HD], rinv[:, r % 2, :], None,
                                        ALU.mult).then_inc(o_done.sem, 1)

            nc.vector.memset(v1[:, :, :, HD:HD + 1], 1.0).then_inc(ones_set.sem, 1)
            ev[0].credit(dve)
            o_done.credit(dve)
            peak(0, 0, 0)
            with dve.Fori(0, NHEADS) as hx:
                for r in range(QT):
                    for c in range(NCH[r]):
                        if (CUM[r] + c) % 2 == 0:
                            take(hx, r, c)
                    if r + 1 < QT:
                        peak(hx, r + 1, hx)
                    else:
                        peak(hx + 1, 0, hx + 1)
                    normalise(hx, r)
    nc.clear_and_free_semaphores(sems)
    nc.all_engine_barrier()


I32 = mybir.dt.int32
U32 = mybir.dt.uint32
EXPERTS, TOPK, FF = 64, 8, 192
VMAX = TOKENS * TOPK
SPARE = 8
MAXG = TOKENS * TOPK // P + EXPERTS + SPARE
COLS = EXPERTS * NT + SPARE


def route(nc, attn, x2_rows, Wo, gate_wT, ident, before, iota_e, v_first, base, e_base, iota_g, incl, no_place,
          x3_rows, table, plan):
    AD = HEADS * HD
    AB = AD // P
    STEPS = 9

    sems = []
    with ExitStack() as ctx:
        def sb(name, shape, dt=F32):
            return ctx.enter_context(nc.sbuf_tensor(name, shape, dt))

        def pb(name, shape):
            return ctx.enter_context(nc.psum_tensor(name, shape, F32))

        def tally(name, per=1, ahead=0):
            sems.append(nc.alloc_semaphore(name))
            return Tally(sems[-1], per, ahead)

        w_o = sb("w_o", [P, AB, DM])
        w_g = sb("w_g", [P, KD, EXPERTS])
        idn = sb("idn4", [P, P])
        before_sb = sb("before_sb", [P, P])
        iota_sb = sb("iota_sb", [P, EXPERTS])
        ones = sb("ones4", [P, P])
        at = sb("at", [P, 2, AD])
        x2t = sb("x2t", [P, 2, DM])
        aT = sb("aT", [P, AB, P])
        r3 = sb("r3", [P, DM])
        x3 = sb("x3", [P, 2, DM])
        idx_f = sb("idx_f", [P, TOPK])
        entry = sb("entry", [P, 2, TOPK, 2])
        xT = sb("xT4", [P, KD, P])
        stats = sb("stats4", [P, 6])
        mv = sb("mv4", [P, 2])
        rstd = sb("rstd4", [P, 1])
        nhalf = sb("nhalf4", [P, 1])
        eps_sb = sb("eps4", [P, 1])
        negm = sb("negm4", [P, 1])
        ex = sb("ex", [P, EXPERTS])
        esum = sb("esum", [P, 1])
        erec = sb("erec", [P, 1])
        sc = sb("sc", [P, EXPERTS])
        top = sb("top", [P, TOPK])
        idx = sb("idx", [P, TOPK], U32)
        rest = sb("rest", [P, EXPERTS])
        chosen = sb("chosen", [P, EXPERTS])
        tsum = sb("tsum", [P, 1])
        macc = sb("macc", [P, EXPERTS])
        junk = sb("junk4", [P, TOPK, EXPERTS])
        dest_f = sb("dest_f", [P, TOPK])
        dest_i = sb("dest_i", [P, TOPK], I32)
        col = sb("col", [P, TOPK], I32)
        dest = sb("dest", [P, 2, TOPK], I32)
        e_base_sb = sb("e_base_sb", [EXPERTS, 1])
        g_sb = sb("g_sb", [EXPERTS, MAXG])
        incl_sb = sb("incl_sb", [EXPERTS, 2, EXPERTS])
        n_i = sb("n_i", [EXPERTS, 1], I32)
        n_f = sb("n_f", [EXPERTS, 1])
        ends = sb("ends", [EXPERTS, 1])
        past = sb("past", [EXPERTS, MAXG])
        first_f = sb("first_f", [1, MAXG])
        plan_sb = sb("plan_sb", [1, 2 * MAXG + EXPERTS + 1], I32)
        ps_t = pb("ps_t4", [P, 2, 4, P])
        ps_o = pb("ps_o4", [P, 512])
        ps_x = pb("ps_x4", [P, 4, P])
        ps_g = pb("ps_g4", [P, 512])
        ps_p = pb("ps_p4", [P, 512])

        consts = tally("consts4")
        nh_set = tally("nh_set4")
        in_ld = [tally("in4_ld0", 32), tally("in4_ld1", 32)]
        at_tr = tally("at_tr", 2)
        at_ev = tally("at_ev", 2, 1)
        op_ps = tally("op_ps4", 1, 1)
        sum3 = tally("sum3", 1, 1)
        stat = tally("stat4")
        stat_seen = tally("stat_seen4")
        aggr = tally("aggr4")
        add = tally("add4")
        pw = tally("pow4")
        x3_ready = tally("x3_ready")
        x3_out = [tally("x3_out0", 16, 1), tally("x3_out1", 16, 1)]
        tx = tally("tx4")
        xT_ev = tally("xT4_ev", 1, 1)
        lg = tally("lg4", 1, 1)
        nm = tally("nm4")
        ex_done = tally("ex_done", 1, 1)
        step = tally("step4", STEPS)
        seen = tally("seen4")
        mask_ready = tally("mask_ready")
        pos_ps = tally("pos_ps")
        counted = tally("counted", 1, 1)
        picked = tally("picked", 4)
        dest_ready = tally("dest_ready", 1, 1)
        sent = [tally("sent0", 16 * TOPK), tally("sent1", 16 * TOPK)]
        plan_step = tally("plan_step")
        plan_ps = tally("plan_ps")
        plan_out = tally("plan_out")
        NCONST = 10

        block = ctx.enter_context(nc.Block())

        @block.sync
        def _(sp):
            with nc.allow_non_contiguous_dma(reason="small, once"):
                for dst, src in (
                    (w_o[:, :, :], Wo.rearrange("(k p) n -> p k n", p=P)),
                    (w_g[:, :, :], gate_wT.rearrange("(k p) n -> p k n", p=P)),
                    (idn[:, :], ident),
                    (before_sb[:, :], before),
                    (iota_sb[:, :], iota_e),
                    (entry[:, 1, :, 0], v_first),
                    (macc[:, :], base),
                    (e_base_sb[:, :], e_base),
                    (g_sb[:, :], iota_g),
                    (incl_sb[:, :, :], incl),
                ):
                    sp.dma_start(dst, src).then_inc(consts.sem, 16)

            def load(slot, rows):
                sp.dma_start(at[:, slot, :], attn[rows, :]).then_inc(in_ld[slot].sem, 16)
                sp.dma_start(x2t[:, slot, :], x2_rows[rows, :]).then_inc(in_ld[slot].sem, 16)

            for s in range(2):
                load(s, slice(s * P, (s + 1) * P))
            for o in x3_out:
                o.credit(sp)
            with sp.Fori(0, NT // 2) as i:
                ahead = [sp.snap(((2 * i + s + 2) % NT) * P) for s in range(2)]
                here = [sp.snap((2 * i + s) * P) for s in range(2)]
                for s in range(2):
                    t = 2 * i + s
                    sp.wait_ge(sum3.sem, sum3.at(t))
                    load(s, bass.ds(ahead[s], P))
                    sp.wait_ge(x3_ready.sem, x3_ready.at(t))
                    sp.dma_start(x3_rows[bass.ds(here[s], P), :], x3[:, s, :]).then_inc(x3_out[s].sem, 16)
            for s in range(2):
                sp.wait_ge(in_ld[s].sem, 32 * (NT // 2 + 1))
                sp.wait_ge(x3_out[s].sem, x3_out[s].at(NT // 2 - 1))
            sp.wait_ge(plan_step.sem, 10)
            sp.dma_start(plan, plan_sb[:, :]).then_inc(plan_out.sem, 16)
            sp.wait_ge(plan_out.sem, 16)

        @block.tensor
        def _(pe):
            def out_proj(t, s, loads):
                pe.wait_ge(in_ld[s].sem, 32 * loads)
                for g in range(2):
                    pe.wait_ge(at_ev.sem, at_ev.at(t - 1, g + 1))
                    for j in range(4):
                        b = 4 * g + j
                        last = nc.tensor.transpose(ps_t[:, g, j, :], at[:, s, b * P:(b + 1) * P], idn[:, :])
                    last.then_inc(at_tr.sem, 1)
                pe.wait_ge(at_ev.sem, at_ev.at(t))
                pe.wait_ge(sum3.sem, sum3.at(t - 1))
                for b in range(AB):
                    last = nc.tensor.matmul(ps_o[:, 0:DM], aT[:, b, :], w_o[:, b, :], start=b == 0, stop=b == AB - 1)
                last.then_inc(op_ps.sem, 1)

            def logits(t, s):
                pe.wait_ge(x3_ready.sem, x3_ready.at(t))
                for k in range(KD):
                    last = nc.tensor.transpose(ps_x[:, k, :], x3[:, s, k * P:(k + 1) * P], idn[:, :])
                last.then_inc(tx.sem, 1)
                pe.wait_ge(xT_ev.sem, xT_ev.at(t))
                pe.wait_ge(ex_done.sem, ex_done.at(t - 1))
                for k in range(KD):
                    last = nc.tensor.matmul(ps_g[:, 0:EXPERTS], xT[:, k, :], w_g[:, k, :], start=k == 0, stop=k == KD - 1)
                last.then_inc(lg.sem, 1)

            def places(t):
                pe.wait_ge(mask_ready.sem, mask_ready.at(t))
                pe.wait_ge(dest_ready.sem, dest_ready.at(t - 1))
                pe.wait_ge(counted.sem, counted.at(t - 1))
                nc.tensor.matmul(ps_p[:, 0:EXPERTS], before_sb[:, :], chosen[:, :], start=True, stop=False)
                nc.tensor.matmul(ps_p[:, 0:EXPERTS], ones[:, :], macc[:, :], start=False, stop=True).then_inc(pos_ps.sem, 1)

            pe.wait_ge(consts.sem, 16 * NCONST)
            pe.wait_ge(nh_set.sem, 3)
            out_proj(0, 0, 1)
            with pe.Fori(0, NT // 2) as i:
                for s in range(2):
                    t = 2 * i + s
                    logits(t, s)
                    out_proj(t + 1, 1 - s, i + 1 + s)
                    places(t)
            pe.wait_ge(counted.sem, counted.at(NT - 1))
            pe.wait_ge(dest_ready.sem, dest_ready.at(NT - 1))
            pe.wait_ge(ex_done.sem, ex_done.at(NT - 1))
            nc.tensor.matmul(ps_g[0:EXPERTS, 0:1], macc[:, :], ones[:, 0:1], start=True, stop=True).then_inc(plan_ps.sem, 1)
            pe.wait_ge(plan_step.sem, 3)
            pe.wait_ge(sum3.sem, sum3.at(NT))
            nc.tensor.matmul(ps_o[0:EXPERTS, 0:1], incl_sb[:, 0, :], n_f[:, :], start=True, stop=True).then_inc(plan_ps.sem, 1)
            nc.tensor.matmul(ps_g[0:1, 0:EXPERTS], n_f[:, :], incl_sb[:, 1, :], start=True, stop=True).then_inc(plan_ps.sem, 1)
            pe.wait_ge(plan_step.sem, 6)
            nc.tensor.matmul(ps_p[0:1, 0:MAXG], ones[0:EXPERTS, 0:1], past[:, :], start=True, stop=True).then_inc(plan_ps.sem, 1)
            nc.tensor.matmul(ps_o[0:1, 0:MAXG], n_f[:, :], past[:, :], start=True, stop=True).then_inc(plan_ps.sem, 1)

        @block.scalar
        def _(act):
            def take_attn(t):
                act.wait_ge(op_ps.sem, op_ps.at(t - 1))
                for g in range(2):
                    act.wait_ge(at_tr.sem, at_tr.at(t, g + 1))
                    nc.scalar.activation(aT[:, 4 * g:4 * g + 4, :], ps_t[:, g, :, :], ACT.Copy).then_inc(at_ev.sem, 1)

            at_ev.credit(act)
            op_ps.credit(act)
            xT_ev.credit(act)
            lg.credit(act)
            ex_done.credit(act)
            take_attn(0)
            with act.Fori(0, NT // 2) as i:
                for s in range(2):
                    t = 2 * i + s
                    act.wait_ge(tx.sem, tx.at(t))
                    act.wait_ge(lg.sem, lg.at(t - 1))
                    nc.scalar.activation(xT[:, :, :], ps_x[:, 0:KD, :], ACT.Copy).then_inc(xT_ev.sem, 1)
                    act.wait_ge(nm.sem, nm.at(t))
                    nc.scalar.activation(ex[:, :], ps_g[:, 0:EXPERTS], ACT.Exp, bias=negm[:, :],
                                         accum_out=esum[:, :]).then_inc(ex_done.sem, 1)
                    take_attn(t + 1)

        @block.gpsimd
        def _(pool):
            def inv_std(t):
                pool.wait_ge(aggr.sem, aggr.at(t))
                nc.gpsimd.tensor_tensor(rstd[:, :], mv[:, 1:2], eps_sb[:, :], ALU.add).then_inc(add.sem, 1)
                pool.wait_ge(add.sem, add.at(t))
                nc.gpsimd.tensor_tensor(rstd[:, :], rstd[:, :], nhalf[:, :], ALU.pow).then_inc(pw.sem, 1)

            nc.gpsimd.memset(nhalf[:, :], -0.5).then_inc(nh_set.sem, 1)
            nc.gpsimd.memset(eps_sb[:, :], EPS).then_inc(nh_set.sem, 1)
            nc.gpsimd.memset(ones[:, :], 1.0).then_inc(nh_set.sem, 1)
            for s in range(2):
                half = slice(s * P // 2, (s + 1) * P // 2)
                pool.dma_start(table.rearrange("(p c) n -> p (c n)", p=P)[half, :], no_place[half, :]).then_inc(sent[s].sem, 16)
            for s in range(2):
                pool.wait_ge(sent[s].sem, 16)
            pool.wait_ge(nh_set.sem, 3)
            pool.wait_ge(consts.sem, 16 * NCONST)
            inv_std(0)
            with pool.Fori(0, NT // 2) as i:
                for s in range(2):
                    t = 2 * i + s
                    inv_std(t + 1)
                    pool.wait_ge(dest_ready.sem, dest_ready.at(t))
                    pool.sem_inc(seen.sem)
                    for k in range(TOPK):
                        pool.indirect_dma_start(out=table, out_offset=bass.IndirectOffsetOnAxis(ap=dest[:, s, k:k + 1], axis=0),
                                                in_=entry[:, s, k, :], in_offset=None).then_inc(sent[s].sem, 16)
            for s in range(2):
                pool.wait_ge(sent[s].sem, 16 + sent[s].at(NT // 2 - 1))

        @block.vector
        def _(dve):
            def norm(t, s, prev):
                dve.wait_ge(op_ps.sem, op_ps.at(t))
                nc.vector.tensor_tensor(r3[:, :], ps_o[:, 0:DM], x2t[:, s, :], ALU.add).then_inc(sum3.sem, 1)
                dve.wait_ge(sum3.sem, sum3.at(t))
                nc.vector.bn_stats(stats[:, :], r3[:, :]).then_inc(stat.sem, 1)
                dve.wait_ge(stat.sem, stat.at(t))
                dve.sem_inc(stat_seen.sem)
                nc.vector.bn_aggr(mv[:, :], stats[:, :]).then_inc(aggr.sem, 1)
                dve.wait_ge(pw.sem, pw.at(t))
                dve.wait_ge(x3_out[s].sem, x3_out[s].at(prev))
                nc.vector.tensor_scalar(x3[:, s, :], r3[:, :], mv[:, 0:1], rstd[:, :], ALU.subtract,
                                        ALU.mult).then_inc(x3_ready.sem, 1)

            def after(t, n):
                dve.wait_ge(step.sem, step.at(t, n))

            def choose(i, t, s):
                dve.wait_ge(lg.sem, lg.at(t))
                nc.vector.reduce_max(negm[:, :], ps_g[:, 0:EXPERTS], axis=mybir.AxisListType.X,
                                     negate=True).then_inc(nm.sem, 1)
                dve.wait_ge(ex_done.sem, ex_done.at(t))
                nc.vector.reciprocal(erec[:, :], esum[:, :]).then_inc(step.sem, 1)
                after(t, 1)
                nc.vector.tensor_scalar(sc[:, :], ex[:, :], erec[:, :], None, ALU.mult).then_inc(step.sem, 1)
                after(t, 2)
                dve.sem_inc(stat_seen.sem)
                nc.vector.max(top[:, :], sc[:, :]).then_inc(step.sem, 1)
                after(t, 3)
                dve.sem_inc(stat_seen.sem)
                nc.vector.match_replace(rest[:, :], top[:, :], sc[:, :], -1.0).then_inc(step.sem, 1)
                nc.vector.max_index(idx[:, :], top[:, :], sc[:, :]).then_inc(step.sem, 1)
                after(t, 4)
                nc.vector.tensor_scalar(chosen[:, :], rest[:, :], -1.0, None, ALU.is_equal).then_inc(mask_ready.sem, 1)
                nc.vector.reduce_sum(tsum[:, :], top[:, :], axis=mybir.AxisListType.X).then_inc(step.sem, 1)
                after(t, 6)
                nc.vector.tensor_scalar(tsum[:, :], tsum[:, :], 1e-20, None, ALU.add).then_inc(step.sem, 1)
                after(t, 7)
                nc.vector.reciprocal(tsum[:, :], tsum[:, :]).then_inc(step.sem, 1)
                nc.vector.tensor_copy(idx_f[:, :], idx[:, :])
                dve.wait_ge(sent[s].sem, 16 + 16 * TOPK * i)
                nc.vector.tensor_scalar(entry[:, s, :, 0], entry[:, 1 - s, :, 0], float(P * TOPK), None, ALU.add)
                after(t, 8)
                nc.vector.tensor_scalar(entry[:, s, :, 1], top[:, :], tsum[:, :], None, ALU.mult).then_inc(step.sem, 1)

            def send(t, s):
                dve.wait_ge(step.sem, step.at(t))
                dve.wait_ge(pos_ps.sem, pos_ps.at(t))
                for k in range(TOPK):
                    ins = nc.vector.scalar_tensor_tensor(junk[:, k, :], iota_sb[:, :], idx_f[:, k:k + 1],
                                                         ps_p[:, 0:EXPERTS], ALU.is_equal, ALU.mult,
                                                         accum_out=dest_f[:, k:k + 1])
                ins.then_inc(picked.sem, 1)
                dve.wait_ge(picked.sem, picked.at(t, 1))
                nc.vector.tensor_copy(dest_i[:, :], dest_f[:, :]).then_inc(picked.sem, 1)
                dve.wait_ge(picked.sem, picked.at(t, 2))
                nc.vector.tensor_scalar(col[:, :], dest_i[:, :], 7, None, ALU.arith_shift_right).then_inc(picked.sem, 1)
                nc.vector.tensor_scalar(dest_i[:, :], dest_i[:, :], P - 1, None, ALU.bitwise_and).then_inc(picked.sem, 1)
                dve.wait_ge(picked.sem, picked.at(t, 4))
                nc.vector.scalar_tensor_tensor(dest[:, s, :], dest_i[:, :], float(COLS), col[:, :], ALU.mult,
                                               ALU.add).then_inc(dest_ready.sem, 1)
                nc.vector.tensor_tensor(macc[:, :], macc[:, :], chosen[:, :], ALU.add).then_inc(counted.sem, 1)

            sum3.credit(dve)
            counted.credit(dve)
            dest_ready.credit(dve)
            dve.wait_ge(consts.sem, 16 * NCONST)
            norm(0, 0, -1)
            with dve.Fori(0, NT // 2) as i:
                for s in range(2):
                    t = 2 * i + s
                    choose(i, t, s)
                    norm(t + 1, 1 - s, i - 1 + s)
                    send(t, s)

            def plan_after(n):
                dve.wait_ge(plan_step.sem, n)

            dve.wait_ge(plan_ps.sem, 1)
            nc.vector.tensor_scalar(n_i[:, :], ps_g[0:EXPERTS, 0:1], e_base_sb[:, :], None, ALU.subtract).then_inc(plan_step.sem, 1)
            plan_after(1)
            nc.vector.tensor_scalar(n_i[:, :], n_i[:, :], 7, None, ALU.arith_shift_right).then_inc(plan_step.sem, 1)
            plan_after(2)
            nc.vector.tensor_scalar(n_f[:, :], n_i[:, :], 1.0, None, ALU.max).then_inc(plan_step.sem, 1)
            dve.wait_ge(plan_ps.sem, 3)
            nc.vector.tensor_copy(ends[:, :], ps_o[0:EXPERTS, 0:1]).then_inc(plan_step.sem, 1)
            plan_after(4)
            nc.vector.tensor_scalar(past[:, :], g_sb[:, :], ends[:, :], None, ALU.is_ge).then_inc(plan_step.sem, 1)
            nc.vector.tensor_copy(plan_sb[:, 2 * MAXG:2 * MAXG + EXPERTS], ps_g[0:1, 0:EXPERTS]).then_inc(plan_step.sem, 1)
            dve.wait_ge(plan_ps.sem, 5)
            nc.vector.tensor_scalar(plan_sb[:, 0:MAXG], ps_p[0:1, 0:MAXG], float(EXPERTS - 1), None, ALU.min).then_inc(plan_step.sem, 1)
            nc.vector.tensor_tensor(first_f[:, :], g_sb[0:1, :], ps_o[0:1, 0:MAXG], ALU.subtract)
            nc.vector.tensor_copy(plan_sb[:, 2 * MAXG + EXPERTS:], ps_o[0:1, MAXG - 1:MAXG]).then_inc(plan_step.sem, 1)
            plan_after(8)
            nc.vector.scalar_tensor_tensor(first_f[:, :], ps_p[0:1, 0:MAXG], float(NT), first_f[:, :], ALU.mult,
                                           ALU.add).then_inc(plan_step.sem, 1)
            plan_after(9)
            nc.vector.tensor_scalar(plan_sb[:, MAXG:2 * MAXG], first_f[:, :], float(COLS - 1), None,
                                    ALU.min).then_inc(plan_step.sem, 1)
    nc.clear_and_free_semaphores(sems)
    nc.all_engine_barrier()


def experts(nc, table, plan, x3_rows, W_guT, W_downT, ident, y8):
    H2 = FF // 2
    WLOADS = 32

    sems = []
    with ExitStack() as ctx:
        def sb(name, shape, dt=F32):
            return ctx.enter_context(nc.sbuf_tensor(name, shape, dt))

        def pb(name, shape):
            return ctx.enter_context(nc.psum_tensor(name, shape, F32))

        def tally(name, per=1, ahead=0):
            sems.append(nc.alloc_semaphore(name))
            return Tally(sems[-1], per, ahead)

        idn = sb("idn5", [P, P])
        entries = sb("entries", [P, COLS, 2])
        token_all = sb("token_all", [P, COLS, 1], I32)
        place_all = sb("place_all", [P, COLS, 1], I32)
        token = sb("token", [P, 2, 1], I32)
        place = sb("place", [P, 2, 1], I32)
        weight = sb("weight", [P, 2, 1])
        plan_sb = sb("plan5", [1, 2 * MAXG + EXPERTS + 1], I32)
        pairs_sb = sb("pairs5", [1, 1], I32)
        w_gu = sb("w_gu", [P, 2, KD, 2 * FF])
        w_d = sb("w_d", [H2, 2, 2, DM])
        xr = sb("xr", [P, 2, DM])
        xT = sb("xT5", [P, 2, KD, P])
        sg = sb("sg", [P, 2, FF])
        hid = sb("hid", [P, 2, FF])
        hT = sb("hT", [H2, 2, 2, P])
        y_sb = sb("y5", [P, 2, DM])
        ps_x = pb("ps_x5", [P, 2, 4, P])
        ps_gu = pb("ps_gu", [P, 2, 512])
        ps_h = pb("ps_h", [P, 2, 4, P])
        ps_y = pb("ps_y5", [P, 2, 512])

        consts = tally("consts5")
        pairs_step = tally("pairs_step")
        w_ld = [tally("w_ld0", WLOADS, 1), tally("w_ld1", WLOADS, 1)]
        x_ld = [tally("x5_ld0", 16), tally("x5_ld1", 16)]
        tx = tally("tx5")
        xT_ev = tally("xT5_ev")
        gu = tally("gu")
        gate = tally("gate")
        hid_ready = tally("hid_ready")
        th = tally("th")
        hT_ev = tally("hT_ev")
        down = tally("down", 1, 2)
        listed = tally("listed")
        token_ready = tally("token_ready")
        token_seen = tally("token_seen")
        weighed = tally("weighed")
        y_ready = tally("y5_ready", 1, 2)
        y_seen = tally("y5_seen")
        y_out = [tally("y5_out0", 16), tally("y5_out1", 16)]
        NCONST = 2

        def planned(row, g):
            return plan_sb[0:1, bass.ds(row * MAXG + g, 1)]

        def pair_count(eng):
            eng.wait_ge(pairs_step.sem, 2)
            return eng.value_load(pairs_sb[0:1, 0:1], min_val=1, max_val=MAXG // 2)

        block = ctx.enter_context(nc.Block())

        @block.sync
        def _(sp):
            def weights(slot, e):
                sp.dma_start(w_gu[:, slot, :, :], W_guT[bass.ds(e, 1)].rearrange("o (k p) n -> p (o k) n", p=P)
                             ).then_inc(w_ld[slot].sem, 16)
                sp.dma_start(w_d[:, slot, :, :], W_downT[bass.ds(e, 1)].rearrange("o (k p) n -> p (o k) n", p=H2)
                             ).then_inc(w_ld[slot].sem, 16)

            sp.dma_start(plan_sb[:, :], plan).then_inc(consts.sem, 16)
            sp.dma_start(idn[:, :], ident).then_inc(consts.sem, 16)
            for w in w_ld:
                w.credit(sp)
            for s in range(2):
                weights(s, s)
            sp.wait_ge(consts.sem, 16 * NCONST)
            with sp.Fori(1, EXPERTS // 2) as j:
                for s in range(2):
                    e = sp.snap(2 * j + s)
                    start = sp.value_load(plan_sb[0:1, bass.ds(2 * MAXG + 2 * j + s - 1, 1)], min_val=1, max_val=MAXG)
                    sp.wait_ge(down.sem, start + down.ahead)
                    weights(s, e)
            for s in range(2):
                sp.wait_ge(w_ld[s].sem, w_ld[s].at(EXPERTS // 2 - 1))

        @block.tensor
        def _(pe):
            def turn_x(g, s, loads):
                pe.wait_ge(x_ld[s].sem, 16 * loads)
                for k in range(KD):
                    last = nc.tensor.transpose(ps_x[:, s, k, :], xr[:, s, k * P:(k + 1) * P], idn[:, :])
                last.then_inc(tx.sem, 1)

            def gate_up(g, s):
                e = pe.value_load(planned(0, g), min_val=0, max_val=EXPERTS - 1)
                slot = pe.snap(e % 2)
                pe.wait_ge(w_ld[0].sem, w_ld[0].at(0) + (e // 2) * WLOADS)
                pe.wait_ge(w_ld[1].sem, w_ld[1].at(-1) + ((e + 1) // 2) * WLOADS)
                pe.wait_ge(xT_ev.sem, xT_ev.at(g))
                for k in range(KD):
                    last = nc.tensor.matmul(ps_gu[:, s, 0:2 * FF], xT[:, s, k, :], w_gu[:, bass.ds(slot, 1), k, :],
                                            start=k == 0, stop=k == KD - 1)
                last.then_inc(gu.sem, 1)
                return slot

            def turn_h(g, s):
                pe.wait_ge(hid_ready.sem, hid_ready.at(g))
                for b in range(2):
                    last = nc.tensor.transpose(ps_h[0:H2, s, b, :], hid[:, s, b * H2:(b + 1) * H2], idn[:, :])
                last.then_inc(th.sem, 1)

            def output(g, s, slot):
                pe.wait_ge(hT_ev.sem, hT_ev.at(g))
                pe.wait_ge(y_ready.sem, y_ready.at(g - 2))
                for b in range(2):
                    last = nc.tensor.matmul(ps_y[:, s, 0:DM], hT[:, s, b, :], w_d[:, bass.ds(slot, 1), b, :],
                                            start=b == 0, stop=b == 1)
                last.then_inc(down.sem, 1)

            pe.wait_ge(consts.sem, 16 * NCONST)
            pairs = pair_count(pe)
            down.credit(pe)
            turn_x(0, 0, 1)
            turn_x(1, 1, 1)
            with pe.Fori(0, pairs) as i:
                slots = [gate_up(2 * i + s, s) for s in range(2)]
                turn_h(2 * i, 0)
                turn_x(2 * i + 2, 0, i + 2)
                turn_x(2 * i + 3, 1, i + 2)
                output(2 * i, 0, slots[0])
                turn_h(2 * i + 1, 1)
                output(2 * i + 1, 1, slots[1])

        @block.scalar
        def _(act):
            def take_x(g, s):
                act.wait_ge(tx.sem, tx.at(g))
                nc.scalar.activation(xT[:, s, :, :], ps_x[:, s, 0:KD, :], ACT.Copy).then_inc(xT_ev.sem, 1)

            def take_h(g, s):
                act.wait_ge(th.sem, th.at(g))
                act.wait_ge(down.sem, down.at(g - 2))
                nc.scalar.activation(hT[:, s, :, :], ps_h[0:H2, s, 0:2, :], ACT.Copy).then_inc(hT_ev.sem, 1)

            act.wait_ge(consts.sem, 16 * NCONST)
            pairs = pair_count(act)
            for s in range(2):
                take_x(s, s)
            with act.Fori(0, pairs) as i:
                for s in range(2):
                    act.wait_ge(gu.sem, gu.at(2 * i + s))
                    nc.scalar.activation(sg[:, s, :], ps_gu[:, s, 0:FF], ACT.Silu).then_inc(gate.sem, 1)
                take_h(2 * i, 0)
                for s in range(2):
                    take_x(2 * i + 2 + s, s)
                take_h(2 * i + 1, 1)

        @block.gpsimd
        def _(pool):
            def gather(g, s, turned=True):
                pool.wait_ge(token_ready.sem, token_ready.at(g))
                if turned:
                    pool.wait_ge(tx.sem, tx.at(g - 2))
                pool.sem_inc(token_seen.sem)
                pool.indirect_dma_start(out=xr[:, s, :], out_offset=None, in_=x3_rows,
                                        in_offset=bass.IndirectOffsetOnAxis(ap=token[:, s, :], axis=0)
                                        ).then_inc(x_ld[s].sem, 16)

            for s in range(2):
                half = slice(s * P // 2, (s + 1) * P // 2)
                pool.dma_start(entries[half, :, :], table.rearrange("(p c) n -> p c n", p=P)[half, :, :]).then_inc(y_out[s].sem, 16)
            y_ready.credit(pool)
            pool.wait_ge(consts.sem, 16 * NCONST)
            pairs = pair_count(pool)
            for g in range(4):
                gather(g, g % 2, g >= 2)
            with pool.Fori(0, pairs) as i:
                for s in range(2):
                    gather(2 * i + 4 + s, s)
                for s in range(2):
                    pool.wait_ge(y_ready.sem, y_ready.at(2 * i + s))
                    pool.sem_inc(y_seen.sem)
                    pool.indirect_dma_start(out=y8, out_offset=bass.IndirectOffsetOnAxis(ap=place[:, s, :], axis=0),
                                            in_=y_sb[:, s, :], in_offset=None).then_inc(y_out[s].sem, 16)
            for s in range(2):
                pool.wait_ge(y_out[s].sem, 16 * (pairs + 1))
                pool.sem_inc(y_seen.sem)
                pool.wait_ge(x_ld[s].sem, 16 * (pairs + 2))
                pool.sem_inc(token_seen.sem)

        @block.vector
        def _(dve):
            def tokens(g, s, loads):
                c = dve.value_load(planned(1, g), min_val=0, max_val=COLS - 1)
                if loads is not None:
                    dve.wait_ge(x_ld[s].sem, 16 * loads)
                nc.vector.tensor_copy(token[:, s, :], token_all[:, bass.ds(c, 1), :]).then_inc(token_ready.sem, 1)

            def unit(g, s):
                dve.wait_ge(gate.sem, gate.at(g))
                nc.vector.tensor_tensor(hid[:, s, :], ps_gu[:, s, FF:2 * FF], sg[:, s, :], ALU.mult).then_inc(hid_ready.sem, 1)

            def scale(i, g, s):
                c = dve.value_load(planned(1, g), min_val=0, max_val=COLS - 1)
                dve.wait_ge(y_out[s].sem, 16 * (i + 1))
                dve.wait_ge(y_ready.sem, y_ready.at(g - 2))
                nc.vector.tensor_copy(place[:, s, :], place_all[:, bass.ds(c, 1), :])
                nc.vector.tensor_copy(weight[:, s, :], entries[:, bass.ds(c, 1), 1:2]).then_inc(weighed.sem, 1)
                dve.wait_ge(weighed.sem, weighed.at(g))
                dve.wait_ge(down.sem, down.at(g))
                nc.vector.tensor_scalar(y_sb[:, s, :], ps_y[:, s, 0:DM], weight[:, s, :], None, ALU.mult).then_inc(y_ready.sem, 1)

            dve.wait_ge(consts.sem, 16 * NCONST)
            nc.vector.tensor_scalar(pairs_sb[:, :], plan_sb[:, 2 * MAXG + EXPERTS:], 1, None, ALU.add).then_inc(pairs_step.sem, 1)
            dve.wait_ge(pairs_step.sem, 1)
            nc.vector.tensor_scalar(pairs_sb[:, :], pairs_sb[:, :], 1, None, ALU.arith_shift_right).then_inc(pairs_step.sem, 1)
            pairs = pair_count(dve)
            for s in range(2):
                dve.wait_ge(y_out[s].sem, 16)
            nc.vector.tensor_copy(place_all[:, :, :], entries[:, :, 0:1]).then_inc(listed.sem, 1)
            dve.wait_ge(listed.sem, 1)
            nc.vector.tensor_scalar(token_all[:, :, :], place_all[:, :, :], 3, None, ALU.arith_shift_right).then_inc(listed.sem, 1)
            dve.wait_ge(listed.sem, 2)
            nc.vector.tensor_scalar(token_all[:, :, :], token_all[:, :, :], TOKENS - 1, None, ALU.min).then_inc(listed.sem, 1)
            dve.wait_ge(listed.sem, 3)
            for g in range(4):
                tokens(g, g % 2, 1 if g >= 2 else None)
            with dve.Fori(0, pairs) as i:
                for s in range(2):
                    unit(2 * i + s, s)
                for s in range(2):
                    tokens(2 * i + 4 + s, s, i + 2)
                for s in range(2):
                    scale(i, 2 * i + s, s)
    nc.clear_and_free_semaphores(sems)
    nc.all_engine_barrier()


def combine(nc, y8, x3_rows, out):
    y_view = y8[0:VMAX, :].rearrange("(t k) d -> t k d", k=TOPK)

    sems = []
    with ExitStack() as ctx:
        def sb(name, shape, dt=F32):
            return ctx.enter_context(nc.sbuf_tensor(name, shape, dt))

        def tally(name, per=1, ahead=0):
            sems.append(nc.alloc_semaphore(name))
            return Tally(sems[-1], per, ahead)

        yk = sb("yk", [P, 2, TOPK, DM])
        x3 = sb("x3_6", [P, 2, DM])
        r4 = sb("r4", [P, 2, DM])
        o_sb = sb("o_sb", [P, 2, DM])
        stats = sb("stats6", [P, 6])
        mv = sb("mv6", [P, 2])
        rstd = sb("rstd6", [P, 1])
        nhalf = sb("nhalf6", [P, 1])
        eps_sb = sb("eps6", [P, 1])

        nh_set = tally("nh_set6")
        in_ld = [tally("in6_ld0", 32), tally("in6_ld1", 32)]
        ksum = tally("ksum")
        sum4 = tally("sum4")
        stat = tally("stat6")
        stat_seen = tally("stat_seen6")
        aggr = tally("aggr6")
        add = tally("add6")
        pw = tally("pow6")
        o_ready = tally("o_ready")
        o_out = [tally("o6_out0", 16, 1), tally("o6_out1", 16, 1)]

        block = ctx.enter_context(nc.Block())

        @block.sync
        def _(sp):
            def load(slot, rows):
                sp.dma_start(yk[:, slot, :, :], y_view[rows, :, :]).then_inc(in_ld[slot].sem, 16)
                sp.dma_start(x3[:, slot, :], x3_rows[rows, :]).then_inc(in_ld[slot].sem, 16)

            for s in range(2):
                load(s, slice(s * P, (s + 1) * P))
            for o in o_out:
                o.credit(sp)
            with sp.Fori(0, NT // 2) as i:
                ahead = [sp.snap(((2 * i + s + 2) % NT) * P) for s in range(2)]
                here = [sp.snap((2 * i + s) * P) for s in range(2)]
                for s in range(2):
                    t = 2 * i + s
                    sp.wait_ge(sum4.sem, sum4.at(t))
                    load(s, bass.ds(ahead[s], P))
                    sp.wait_ge(o_ready.sem, o_ready.at(t))
                    sp.dma_start(out[bass.ds(here[s], P), :], o_sb[:, s, :]).then_inc(o_out[s].sem, 16)
            for s in range(2):
                sp.wait_ge(in_ld[s].sem, 32 * (NT // 2 + 1))
                sp.wait_ge(o_out[s].sem, o_out[s].at(NT // 2 - 1))

        @block.gpsimd
        def _(pool):
            nc.gpsimd.memset(nhalf[:, :], -0.5).then_inc(nh_set.sem, 1)
            nc.gpsimd.memset(eps_sb[:, :], EPS).then_inc(nh_set.sem, 1)
            pool.wait_ge(nh_set.sem, 2)
            with pool.Fori(0, NT) as t:
                pool.wait_ge(aggr.sem, aggr.at(t))
                nc.gpsimd.tensor_tensor(rstd[:, :], mv[:, 1:2], eps_sb[:, :], ALU.add).then_inc(add.sem, 1)
                pool.wait_ge(add.sem, add.at(t))
                nc.gpsimd.tensor_tensor(rstd[:, :], rstd[:, :], nhalf[:, :], ALU.pow).then_inc(pw.sem, 1)

        @block.vector
        def _(dve):
            def total(s, t, loads):
                dve.wait_ge(in_ld[s].sem, 32 * loads)
                nc.vector.reduce_sum(r4[:, s, :], yk[:, s, :, :].rearrange("p k d -> p d k"),
                                     axis=mybir.AxisListType.X).then_inc(ksum.sem, 1)

            total(0, 0, 1)
            with dve.Fori(0, NT // 2) as i:
                for s in range(2):
                    t = 2 * i + s
                    dve.wait_ge(ksum.sem, ksum.at(t))
                    nc.vector.tensor_tensor(r4[:, s, :], r4[:, s, :], x3[:, s, :], ALU.add).then_inc(sum4.sem, 1)
                    dve.wait_ge(sum4.sem, sum4.at(t))
                    nc.vector.bn_stats(stats[:, :], r4[:, s, :]).then_inc(stat.sem, 1)
                    dve.wait_ge(stat.sem, stat.at(t))
                    dve.sem_inc(stat_seen.sem)
                    nc.vector.bn_aggr(mv[:, :], stats[:, :]).then_inc(aggr.sem, 1)
                    total(1 - s, t + 1, i + 1 + s)
                    dve.wait_ge(pw.sem, pw.at(t))
                    dve.wait_ge(o_out[s].sem, o_out[s].at(i - 1))
                    nc.vector.tensor_scalar(o_sb[:, s, :], r4[:, s, :], mv[:, 0:1], rstd[:, :], ALU.subtract,
                                            ALU.mult).then_inc(o_ready.sem, 1)
    nc.clear_and_free_semaphores(sems)
    nc.all_engine_barrier()


def layers(nc, x_T, x_rows, W_inT, conv_w, W_xprojT, W_dtT, b_dt, A_log, D_skip, W_outT, F_inT, F_bias, F_outT, Wqk, Wv,
           Wo, gate_wT, W_guT, W_downT, sel_bc, keep, ident, rope_q, rope_k, causal, before, iota_e, v_first, base, e_base,
           iota_g, incl, no_place, out):
    def scratch(name, shape, dt=F32):
        return nc.dram_tensor(name, shape, dt).ap()

    y_scr = scratch("y_scr", (512, TOKENS))
    x2_rows = scratch("x2_rows", (TOKENS, DM))
    x2_T = scratch("x2_T", (DM, TOKENS))
    q_scr = scratch("q_scr", (BATCH * HEADS, P, LENGTH))
    k_scr = scratch("k_scr", (BATCH * KV, 2, P, LENGTH))
    v_scr = scratch("v_scr", (TOKENS, KV * HD))
    attn = scratch("attn", (TOKENS, HEADS * HD))
    x3_rows = scratch("x3_rows", (TOKENS, DM))
    table = scratch("table", (P * COLS, 2))
    plan = scratch("plan", (1, 2 * MAXG + EXPERTS + 1), I32)
    y8 = scratch("y8", (VMAX + 2 * P, DM))

    mamba(nc, x_T, W_inT, conv_w, W_xprojT, W_dtT, b_dt, A_log, D_skip, sel_bc, keep, ident, y_scr)
    tree_ffn(nc, y_scr, x_rows, W_outT, F_inT, F_bias, F_outT, ident, x2_rows, x2_T)
    qkv(nc, x2_T, Wqk, Wv, rope_q, rope_k, q_scr, k_scr, v_scr)
    attention(nc, q_scr, k_scr, v_scr, ident, causal, attn)
    route(nc, attn, x2_rows, Wo, gate_wT, ident, before, iota_e, v_first, base, e_base, iota_g, incl, no_place,
          x3_rows, table, plan)
    experts(nc, table, plan, x3_rows, W_guT, W_downT, ident, y8)
    combine(nc, y8, x3_rows, out)


def constants():
    import numpy as np
    f = np.float32
    i, e, k = np.arange(P), np.arange(EXPERTS), np.arange(TOPK)
    RANK, NST = 16, 16
    sel = np.zeros((RANK + 2 * NST, 2 * NST, P), f)
    sel[RANK + np.arange(2 * NST), np.arange(2 * NST), :] = 1
    keep = np.ones((P, 4), f)
    keep[:, 1::2] = 0
    inv = f(1) / np.power(f(10000), np.arange(0, HD, 2, dtype=f) / f(HD))
    freqs = np.arange(LENGTH, dtype=f)[:, None] * inv[None, :]
    emb = np.concatenate([freqs, freqs], -1)
    cos, sin = np.cos(emb)[:, 0::2].T, np.sin(emb)[:, 0::2].T
    rope = np.tile(np.stack([cos, sin, -sin, cos], 1).astype(f), (GROUP, 1, 1))
    base = np.zeros((P, EXPERTS), f)
    base[0] = e * TOKENS
    no_place = np.zeros((P, COLS, 2), f)
    no_place[:, :, 0] = VMAX + P * (np.arange(COLS) // NT % 2)[None, :] + i[:, None]
    return dict(
        sel_bc=sel, keep=keep, ident=np.eye(P, dtype=f), rope_q=rope * f(HD ** -0.5), rope_k=rope,
        causal=np.triu(np.full((P, P), -2.0 ** 100, f), 1), before=(i[:, None] < i[None, :]).astype(f),
        iota_e=np.tile(e.astype(f), (P, 1)), v_first=(i[:, None] * TOPK + k[None, :] - P * TOPK).astype(f), base=base,
        e_base=(e * TOKENS - (P - 1)).astype(f)[:, None], iota_g=np.tile(np.arange(MAXG, dtype=f), (EXPERTS, 1)),
        incl=np.stack([e[:, None] <= e[None, :], e[:, None] < e[None, :]], 1).astype(f), no_place=no_place.reshape(P, 2 * COLS))


def kernel(**inputs):
    import numpy as np
    import concourse.bacc as bacc
    from concourse.bass_utils import run_bass_kernel_spmd

    def a(name):
        return np.asarray(inputs[name])

    def heads(w, n):
        return w.reshape(DM, n, GROUP, HD // 2, 2).transpose(0, 1, 4, 2, 3).reshape(DM, 2 * n, P)

    x = a("L0_attn_x").reshape(TOKENS, DM)
    given = dict(
        x_T=x.T, x_rows=x, W_inT=a("L0_attn_W_in").T, conv_w=a("L0_attn_W_conv").reshape(512, 4),
        W_xprojT=a("L0_attn_W_xproj").T, W_dtT=a("L0_attn_W_dt").T, b_dt=a("L0_attn_b_dt"), A_log=a("L0_attn_A_log"),
        D_skip=a("L0_attn_D"), W_outT=a("L0_attn_W_out").T, F_inT=a("L0_ffn_W_in").T, F_bias=a("L0_ffn_b_in"),
        F_outT=a("L0_ffn_W_out").T,
        Wqk=np.concatenate([heads(a("L1_attn_Wq"), HEADS // GROUP), heads(a("L1_attn_Wk"), KV // GROUP)], 1),
        Wv=a("L1_attn_Wv"), Wo=a("L1_attn_Wo"), gate_wT=a("L1_ffn_gate_w").T,
        W_guT=np.concatenate([a("L1_ffn_w_gate").transpose(0, 2, 1), a("L1_ffn_w_up").transpose(0, 2, 1)], 2),
        W_downT=a("L1_ffn_w_down").transpose(0, 2, 1))
    nc = bacc.Bacc("TRN2", target_bir_lowering=False, num_devices=1)
    arrays, args = {}, {}
    for name, value in {**given, **constants()}.items():
        arrays[name] = np.ascontiguousarray(value)
        args[name] = nc.dram_tensor(name, arrays[name].shape, mybir.dt.from_np(arrays[name].dtype), kind="ExternalInput").ap()
    out = nc.dram_tensor("out", (TOKENS, DM), F32, kind="ExternalOutput").ap()
    layers(nc, out=out, **args)
    r = run_bass_kernel_spmd(nc, [arrays], core_ids=[0])
    return r.results[0]["out"].reshape(BATCH, LENGTH, DM)
```

```python
from contextlib import ExitStack

import concourse.bass as bass
from concourse import mybir
from concourse.alu_op_type import AluOpType as ALU

ACT = mybir.ActivationFunctionType
F32 = mybir.dt.float32
F32R = mybir.dt.float32r
P = 128
BATCH, LENGTH, DM = 2, 2048, 256
TOKENS = BATCH * LENGTH
KD = DM // P


class Tally:

    def __init__(self, sem, per=1, ahead=0):
        self.sem, self.per, self.ahead = sem, per, ahead

    def credit(self, eng):
        eng.sem_inc(self.sem, self.ahead * self.per)

    def at(self, rnd, k=None):
        return (rnd + self.ahead) * self.per + (self.per if k is None else k)


def mamba(nc, x_T, W_inT, conv_w, W_xprojT, W_dtT, b_dt, A_log, D_skip, sel_bc, keep, ident, y_scr):
    DI, NST, RANK, TAPS = 512, 16, 16, 4
    DB = DI // P
    TC = 512
    CHUNKS = TOKENS // TC
    NBC = RANK + 2 * NST
    ON_POOL = 2
    LOW = 64
    PARTS = LOW + NBC
    FRONT = 2 * DB + 1
    IN, XP, USES = 2 * DB, 2 * DB, 2 * DB + 1 + DB
    y_out_view = y_scr.rearrange("(d p) t -> p d t", p=P)
    xT_view = x_T.rearrange("(k p) t -> p k t", p=P)

    sems = []
    with ExitStack() as ctx:
        def sb(name, shape, dt=F32):
            return ctx.enter_context(nc.sbuf_tensor(name, shape, dt))

        def pb(name, shape):
            return ctx.enter_context(nc.psum_tensor(name, shape, F32))

        def tally(name, per=1, ahead=0):
            sems.append(nc.alloc_semaphore(name))
            return Tally(sems[-1], per, ahead)

        w_in = sb("w_in", [P, KD, 2 * DI])
        w_xp = sb("w_xp", [P, DB, PARTS])
        w_dt = sb("w_dt", [RANK, DI])
        taps = sb("taps", [P, DB, TAPS])
        dt_bias = sb("dt_bias", [P, DB])
        a_log = sb("a_log", [P, DB, NST])
        neg_a = sb("neg_a", [P, DB, NST])
        d_skip = sb("d_skip", [P, DB])
        sel = sb("sel", [PARTS, 2 * NST, P], F32R)
        idn = sb("idn1", [P, P])
        keep_sb = sb("keep_sb", [P, CHUNKS // 2])
        xt = sb("xt", [P, 2, KD, TC])
        xraw = sb("xraw", [P, DB, TC + TAPS - 1])
        tapped = sb("tapped", [P, 2, TAPS - 1, TC])
        xc = sb("xc", [P, 2, DB, TC])
        sz = sb("sz", [P, 2, DB, TC])
        dbc = sb("dbc", [PARTS, 2, TC], F32R)
        dt_in = sb("dt_in", [RANK, 2, TC])
        sp = sb("sp", [P, DB, TC])
        delta = sb("delta", [P, 2, DB, TC])
        u = sb("u", [P, 2, DB, TC])
        dA = sb("dA", [P, 2, DB, TC])
        dBx = sb("dBx", [P, 2, DB, TC])
        h = sb("h", [P, DB, TC])
        hc = sb("hc", [P, 2, DB, TC])
        b_sb = sb("b_sb", [P, 2, TC])
        yg = sb("yg", [P, DB, TC])
        h_in = sb("h_in", [P, NST, DB])
        sel_in = hc[0:PARTS, :, :, :].rearrange("p s d t -> p (s d t)").rearrange("p (n q) -> p n q", q=P)
        ps_y = pb("ps_y", [P, DB, TC])
        ps_b = pb("ps_b", [P, 2, TC])
        ps_c = pb("ps_c", [P, TC])
        ps_f = pb("ps_f", [P, TC])

        consts = tally("consts")
        xt_ld = [tally("xt_ld0"), tally("xt_ld1")]
        sel_ready = tally("sel_ready")
        high_done = tally("high_done")
        zeroed = tally("zeroed", 3)
        nega_step = tally("nega_step", 2)
        front_ps = tally("front_ps", USES)
        front_ev = tally("front_ev", USES)
        conv_step = tally("conv_step", DB * TAPS + 1, 1)
        tap_done = tally("tap_done", DB * TAPS)
        xc_ready = tally("xc_ready")
        sz_ready = tally("sz_ready")
        sp_step = tally("sp_step", 3)
        delta_ready = tally("delta_ready", 1, 1)
        u_ready = tally("u_ready")
        b_ready = tally("b_ready", NST)
        c_ready = tally("c_ready", NST)
        dA_ready = tally("dA_ready", NST)
        b_taken = tally("b_taken", NST, 1)
        dbx_pool = tally("dbx_pool", NST, 1)
        pool_seen = tally("pool_seen1")
        dbx_done = tally("dbx_done", NST, 1)
        scan_done = tally("scan_done", NST, 1)
        carry_done = tally("carry_done", NST, 1)
        hc_done = tally("hc_done", NST, 1)
        reduce_done = tally("reduce_done", NST, 1)
        y_taken = tally("y_taken", 1, 1)
        ygated = tally("ygated", 1, 2)
        y_out = tally("y_out", 16, 1)
        CONSTS = 12

        block = ctx.enter_context(nc.Block())

        @block.sync
        def _(sp_eng):
            for dst, src in (
                (w_in[:, :, :], W_inT.rearrange("(k p) n -> p k n", p=P)),
                (taps[:, :, :], conv_w.rearrange("(d p) t -> p d t", p=P)),
                (w_xp[:, :, 0:NBC], W_xprojT.rearrange("(d p) n -> p d n", p=P)),
                (w_xp[:, :, LOW:], W_xprojT.rearrange("(d p) n -> p d n", p=P)),
                (w_dt[:, :], W_dtT),
                (dt_bias[:, :], b_dt.rearrange("(d p) -> p d", p=P)),
                (a_log[:, :, :], A_log.rearrange("(d p) n -> p d n", p=P)),
                (d_skip[:, :], D_skip.rearrange("(d p) -> p d", p=P)),
                (sel_in, sel_bc),
                (idn[:, :], ident),
                (keep_sb[:, :], keep),
            ):
                with nc.allow_non_contiguous_dma(reason="small vectors, once"):
                    sp_eng.dma_start(dst, src).then_inc(consts.sem, 16)
            for k in range(2):
                sp_eng.dma_start(xt[:, k, :, :], xT_view[:, :, k * TC:(k + 1) * TC]).then_inc(xt_ld[k].sem, 16)
            y_out.credit(sp_eng)
            with sp_eng.Fori(0, CHUNKS // 2) as i:
                ahead = [sp_eng.snap(((2 * i + s + 2) % CHUNKS) * TC) for s in range(2)]
                here = [sp_eng.snap((2 * i + s) * TC) for s in range(2)]
                for s in range(2):
                    c = 2 * i + s
                    sp_eng.wait_ge(front_ps.sem, front_ps.at(c, IN))
                    sp_eng.dma_start(xt[:, s, :, :], xT_view[:, :, bass.ds(ahead[s], TC)]).then_inc(xt_ld[s].sem, 16)
                    sp_eng.wait_ge(ygated.sem, ygated.at(c))
                    sp_eng.dma_start(y_out_view[:, :, bass.ds(here[s], TC)], yg[:, :, :]).then_inc(y_out.sem, 16)
            sp_eng.wait_ge(y_out.sem, y_out.at(CHUNKS - 1))
            for k in range(2):
                sp_eng.wait_ge(xt_ld[k].sem, 16 * (CHUNKS // 2 + 1))

        @block.tensor
        def _(pe):
            def in_proj(k, slot, j, used=True):
                if used:
                    pe.wait_ge(front_ev.sem, front_ev.at(k, j))
                for kd in range(KD):
                    last = nc.tensor.matmul(ps_f[:, :], w_in[:, kd, j * P:(j + 1) * P], xt[:, slot, kd, :],
                                            start=kd == 0, stop=kd == KD - 1)
                last.then_inc(front_ps.sem, 1)

            def x_proj(k, slot):
                pe.wait_ge(front_ev.sem, front_ev.at(k, XP))
                pe.wait_ge(xc_ready.sem, xc_ready.at(k))
                for d in range(DB):
                    last = nc.tensor.matmul(ps_f[0:PARTS, :], w_xp[:, d, :], xc[:, slot, d, :],
                                            start=d == 0, stop=d == DB - 1)
                last.then_inc(front_ps.sem, 1)

            def dt_proj(k, slot, d):
                pe.wait_ge(front_ev.sem, front_ev.at(k, XP + 1 + d))
                nc.tensor.matmul(ps_f[:, :], w_dt[:, d * P:(d + 1) * P], dt_in[:, slot, :],
                                 start=True, stop=True).then_inc(front_ps.sem, 1)

            def spread_b(c, slot, n):
                pe.wait_ge(dbx_done.sem, dbx_done.at(c, n - 1))
                pe.wait_ge(b_taken.sem, b_taken.at(c, n - 1))
                if n == 0:
                    pe.wait_ge(front_ev.sem, front_ev.at(c, XP + 1))
                nc.tensor.matmul(ps_b[:, n % 2, :], sel[:, n, :], dbc[:, slot, :],
                                 start=True, stop=True).then_inc(b_ready.sem, 1)

            def spread_c(c, slot, n):
                if n:
                    pe.wait_ge(hc_done.sem, hc_done.at(c, n))
                nc.tensor.matmul(ps_c[:, :], sel[:, NST + n, :], dbc[:, slot, :],
                                 start=True, stop=True).then_inc(c_ready.sem, 1)

            def sum_states(c, n):
                pe.wait_ge(hc_done.sem, hc_done.at(c, n + 1))
                if n == 0:
                    pe.wait_ge(y_taken.sem, y_taken.at(c - 1))
                for d in range(DB):
                    last = nc.tensor.matmul(ps_y[:, d, :], idn[:, :], hc[:, n % 2, d, :],
                                            start=n == 0, stop=n == NST - 1)
                last.then_inc(reduce_done.sem, 1)

            pe.wait_ge(zeroed.sem, 3)
            pe.wait_ge(sel_ready.sem, 1)
            pe.wait_ge(consts.sem, 16 * (CONSTS - 1))
            pe.wait_ge(xt_ld[0].sem, 16)
            for j in range(IN):
                in_proj(0, 0, j, j > 0)
            x_proj(0, 0)
            for d in range(DB):
                dt_proj(0, 0, d)
            with pe.Fori(0, CHUNKS // 2) as i:
                for s in range(2):
                    c, k, f = 2 * i + s, 2 * i + s + 1, 1 - s
                    pe.wait_ge(xt_ld[f].sem, 16 * (i + 1 + s))
                    spread_b(c, s, 0)
                    spread_b(c, s, 1)
                    spread_c(c, s, 0)
                    for n in range(NST + 1):
                        if n + 2 < NST:
                            spread_b(c, s, n + 2)
                        if 1 <= n < NST:
                            spread_c(c, s, n)
                        if n >= 1:
                            sum_states(c, n - 1)
                        if n < IN:
                            in_proj(k, f, n)
                        elif n == FRONT + 1:
                            x_proj(k, f)
                        elif n in (FRONT + 2, FRONT + 3):
                            for d in range(2 * (n - FRONT - 2), 2 * (n - FRONT - 1)):
                                dt_proj(k, f, d)

        @block.scalar
        def _(act):
            def evac(k, slot, j):
                act.wait_ge(front_ps.sem, front_ps.at(k, j + 1))
                if j < DB:
                    ins = nc.scalar.activation(xraw[:, j, TAPS - 1:], ps_f[:, :], ACT.Copy)
                elif j < IN:
                    ins = nc.scalar.activation(sz[:, slot, j - DB, :], ps_f[:, :], ACT.Copy)
                elif j == XP:
                    nc.scalar.activation(dt_in[:, slot, :], ps_f[0:RANK, :], ACT.Copy)
                    nc.scalar.activation(dbc[:, slot, :], ps_f[0:PARTS, :], ACT.Copy).then_inc(high_done.sem, 1)
                    return
                else:
                    d = j - XP - 1
                    ins = nc.scalar.activation(delta[:, slot, d, :], ps_f[:, :], ACT.Identity,
                                               bias=dt_bias[:, d:d + 1])
                ins.then_inc(front_ev.sem, 1)

            def tap(k, slot, j, t):
                act.wait_ge(front_ev.sem, front_ev.at(k, j + 1))
                if j >= 2 and t == 1:
                    act.wait_ge(conv_step.sem, conv_step.at(k, (j - 1) * TAPS))
                nc.scalar.activation(tapped[:, j % 2, t - 1, :] if t else xc[:, slot, j, :], xraw[:, j, t:t + TC],
                                     ACT.Copy, scale=taps[:, j, t:t + 1]).then_inc(tap_done.sem, 1)

            def gates(k, slot):
                act.wait_ge(conv_step.sem, conv_step.at(k, DB * TAPS))
                nc.scalar.activation(xc[:, slot, :, :], xc[:, slot, :, :], ACT.Silu).then_inc(xc_ready.sem, 1)
                act.wait_ge(front_ev.sem, front_ev.at(k, IN))
                nc.scalar.activation(sz[:, slot, :, :], sz[:, slot, :, :], ACT.Silu).then_inc(sz_ready.sem, 1)

            def softplus(k, slot):
                act.wait_ge(front_ev.sem, front_ev.at(k, USES))
                act.wait_ge(delta_ready.sem, delta_ready.at(k - 1))
                nc.scalar.activation(sp[:, :, :], delta[:, slot, :, :], ACT.Abs).then_inc(sp_step.sem, 1)
                act.wait_ge(sp_step.sem, sp_step.at(k, 1))
                nc.scalar.activation(sp[:, :, :], sp[:, :, :], ACT.Exp, scale=-1.0).then_inc(sp_step.sem, 1)
                act.wait_ge(sp_step.sem, sp_step.at(k, 2))
                nc.scalar.activation(sp[:, :, :], sp[:, :, :], ACT.Ln, bias=1.0).then_inc(sp_step.sem, 1)

            def take_b(c, n):
                act.wait_ge(b_ready.sem, b_ready.at(c, n + 1))
                act.wait_ge(dbx_pool.sem, dbx_pool.at(c, n - 1))
                nc.scalar.activation(b_sb[:, n % 2, :], ps_b[:, n % 2, :], ACT.Copy).then_inc(b_taken.sem, 1)

            def decay(c, slot, n):
                if n == 0:
                    act.wait_ge(delta_ready.sem, delta_ready.at(c))
                act.wait_ge(scan_done.sem, scan_done.at(c, n - 1))
                for d in range(DB):
                    ins = nc.scalar.activation(dA[:, n % 2, d, :], delta[:, slot, d, :], ACT.Exp,
                                               scale=neg_a[:, d, n:n + 1])
                ins.then_inc(dA_ready.sem, 1)

            b_taken.credit(act)
            act.wait_ge(consts.sem, 16 * (CONSTS - 1))
            nc.scalar.activation(neg_a[:, :, :], a_log[:, :, :], ACT.Exp).then_inc(nega_step.sem, 1)
            act.wait_ge(nega_step.sem, 1)
            nc.scalar.activation(neg_a[:, :, :], neg_a[:, :, :], ACT.Copy, scale=-1.0).then_inc(nega_step.sem, 1)
            act.wait_ge(nega_step.sem, 2)
            act.wait_ge(zeroed.sem, 3)
            nc.scalar.activation(sel[:, :, :], sel_in, ACT.Copy).then_inc(sel_ready.sem, 1)
            for j in range(IN):
                evac(0, 0, j)
            gates(0, 0)
            for j in range(XP, USES):
                evac(0, 0, j)
            softplus(0, 0)
            with act.Fori(0, CHUNKS // 2) as i:
                for s in range(2):
                    c, k, f = 2 * i + s, 2 * i + s + 1, 1 - s
                    take_b(c, 0)
                    take_b(c, 1)
                    decay(c, s, 0)
                    act.wait_ge(ygated.sem, ygated.at(k - 2))
                    act.wait_ge(conv_step.sem, conv_step.at(k - 1))
                    for n in range(NST):
                        if n + 1 < NST:
                            decay(c, s, n + 1)
                        if n + 2 < NST:
                            take_b(c, n + 2)
                        if n < IN:
                            evac(k, f, n)
                        if 1 <= n <= 2 * DB:
                            for t in (0, 1) if n % 2 else (2, 3):
                                tap(k, f, (n - 1) // 2, t)
                        if n == FRONT:
                            gates(k, f)
                        elif n == FRONT + 1:
                            evac(k, f, XP)
                        elif n in (FRONT + 2, FRONT + 3):
                            for d in range(2 * (n - FRONT - 2), 2 * (n - FRONT - 1)):
                                evac(k, f, XP + 1 + d)
                        elif n == FRONT + 4:
                            softplus(k, f)

        @block.gpsimd
        def _(pool):
            def drive(c, slot, n):
                pool.wait_ge(b_taken.sem, b_taken.at(c, n + 1))
                if n == 0:
                    pool.wait_ge(u_ready.sem, u_ready.at(c))
                pool.wait_ge(scan_done.sem, scan_done.at(c, n - 1))
                for d in range(ON_POOL):
                    ins = nc.gpsimd.tensor_tensor(dBx[:, n % 2, d, :], u[:, slot, d, :], b_sb[:, n % 2, :], ALU.mult)
                ins.then_inc(dbx_pool.sem, 1)

            def carry(c, n, keep_col):
                pool.wait_ge(scan_done.sem, scan_done.at(c, n + 1))
                pool.sem_inc(pool_seen.sem)
                if keep_col is None:
                    ins = nc.gpsimd.tensor_copy(h_in[:, n, :], h[:, :, TC - 1])
                else:
                    ins = nc.gpsimd.tensor_tensor(h_in[:, n, :], h[:, :, TC - 1], keep_col.to_broadcast((P, DB)), ALU.mult)
                ins.then_inc(carry_done.sem, 1)

            def after(sem, value):
                pool.wait_ge(sem, value)
                pool.sem_inc(pool_seen.sem)

            def add_tap(k, slot, j, t):
                pool.wait_ge(tap_done.sem, tap_done.at(k - 1, j * TAPS + t + 1))
                if t > 1:
                    pool.wait_ge(conv_step.sem, conv_step.at(k, j * TAPS + t))
                nc.gpsimd.tensor_tensor(xc[:, slot, j, :], xc[:, slot, j, :], tapped[:, j % 2, t - 1, :],
                                        ALU.add).then_inc(conv_step.sem, 2 if t == 1 else 1)

            def halo(k, keep_col):
                after(conv_step.sem, conv_step.at(k, DB * TAPS))
                if keep_col is None:
                    ins = nc.gpsimd.tensor_copy(xraw[:, :, 0:TAPS - 1], xraw[:, :, TC:])
                else:
                    ins = nc.gpsimd.tensor_tensor(xraw[:, :, 0:TAPS - 1], xraw[:, :, TC:],
                                                  keep_col.rearrange("p (a b) -> p a b", a=1).to_broadcast((P, DB, TAPS - 1)), ALU.mult)
                ins.then_inc(conv_step.sem, 1)

            dbx_pool.credit(pool)
            carry_done.credit(pool)
            pool.wait_ge(consts.sem, 16 * (CONSTS - 1))
            pool.wait_ge(zeroed.sem, 3)
            with pool.Fori(0, CHUNKS // 2) as i:
                for s in range(2):
                    c, k, f = 2 * i + s, 2 * i + s + 1, 1 - s
                    keep_col = keep_sb[:, bass.ds(i, 1)]
                    drive(c, s, 0)
                    for n in range(NST):
                        if n + 1 < NST:
                            drive(c, s, n + 1)
                        carry(c, n, keep_col if s else None)
                        if 1 <= n <= 2 * DB:
                            for t in (1,) if n % 2 else (2, 3):
                                add_tap(k, f, (n - 1) // 2, t)
                        elif n == 2 * DB + 1:
                            halo(k, None if s else keep_col)

        @block.vector
        def _(dve):
            def conv_tap(k, slot, t):
                for j in range(DB):
                    if t == 0:
                        dve.wait_ge(front_ev.sem, front_ev.at(k, j + 1))
                        ins = nc.vector.tensor_scalar(xc[:, slot, j, :], xraw[:, j, 0:TC], taps[:, j, 0:1], None, ALU.mult)
                    else:
                        dve.wait_ge(conv_step.sem, conv_step.at(k, (t - 1) * DB + j + 1))
                        ins = nc.vector.scalar_tensor_tensor(xc[:, slot, j, :], xraw[:, j, t:t + TC], taps[:, j, t:t + 1],
                                                             xc[:, slot, j, :], ALU.mult, ALU.add)
                    ins.then_inc(conv_step.sem, 1)

            def low_parts(k, slot):
                dve.wait_ge(high_done.sem, high_done.at(k))
                nc.vector.tensor_tensor(dbc[LOW:PARTS, slot, :], ps_f[LOW:PARTS, :], dbc[LOW:PARTS, slot, :].bitcast(F32),
                                        ALU.subtract).then_inc(front_ev.sem, 1)

            def halo(k):
                dve.wait_ge(conv_step.sem, conv_step.at(k, DB * TAPS))
                nc.vector.tensor_copy(xraw[:, :, 0:TAPS - 1], xraw[:, :, TC:]).then_inc(conv_step.sem, 1)

            def make_delta(k, slot):
                dve.wait_ge(sp_step.sem, sp_step.at(k, 3))
                nc.vector.scalar_tensor_tensor(delta[:, slot, :, :], delta[:, slot, :, :], 0.0, sp[:, :, :],
                                               ALU.max, ALU.add).then_inc(delta_ready.sem, 1)

            def make_u(k, slot):
                dve.wait_ge(delta_ready.sem, delta_ready.at(k))
                dve.wait_ge(xc_ready.sem, xc_ready.at(k))
                nc.vector.tensor_tensor(u[:, slot, :, :], delta[:, slot, :, :], xc[:, slot, :, :],
                                        ALU.mult).then_inc(u_ready.sem, 1)

            def drive(c, slot, n):
                dve.wait_ge(b_taken.sem, b_taken.at(c, n + 1))
                if n == 0:
                    dve.wait_ge(u_ready.sem, u_ready.at(c))
                dve.wait_ge(scan_done.sem, scan_done.at(c, n - 1))
                nc.vector.tensor_tensor(dBx[:, n % 2, ON_POOL:, :], u[:, slot, ON_POOL:, :],
                                        ps_b[:, n % 2:n % 2 + 1, :].to_broadcast((P, DB - ON_POOL, TC)),
                                        ALU.mult).then_inc(dbx_done.sem, 1)

            def scan(c, n):
                dve.wait_ge(dA_ready.sem, dA_ready.at(c, n + 1))
                dve.wait_ge(dbx_pool.sem, dbx_pool.at(c, n + 1))
                dve.wait_ge(dbx_done.sem, dbx_done.at(c, n + 1))
                dve.wait_ge(hc_done.sem, hc_done.at(c, n))
                dve.wait_ge(carry_done.sem, carry_done.at(c, n))
                for d in range(DB):
                    ins = nc.vector.tensor_tensor_scan(h[:, d, :], dA[:, n % 2, d, :], dBx[:, n % 2, d, :],
                                                       h_in[:, n, d:d + 1], ALU.mult, ALU.add)
                ins.then_inc(scan_done.sem, 1)

            def weigh(c, n):
                dve.wait_ge(c_ready.sem, c_ready.at(c, n + 1))
                dve.wait_ge(scan_done.sem, scan_done.at(c, n + 1))
                dve.wait_ge(reduce_done.sem, reduce_done.at(c, n - 1))
                nc.vector.tensor_tensor(hc[:, n % 2, :, :], h[:, :, :],
                                        ps_c[:, :].rearrange("p (o t) -> p o t", o=1).to_broadcast((P, DB, TC)),
                                        ALU.mult).then_inc(hc_done.sem, 1)

            def gate_out(c, slot):
                dve.wait_ge(reduce_done.sem, reduce_done.at(c))
                dve.wait_ge(y_out.sem, y_out.at(c - 1))
                for d in range(DB):
                    ins = nc.vector.scalar_tensor_tensor(yg[:, d, :], xc[:, slot, d, :], d_skip[:, d:d + 1],
                                                         ps_y[:, d, :], ALU.mult, ALU.add)
                ins.then_inc(y_taken.sem, 1)
                dve.wait_ge(y_taken.sem, y_taken.at(c))
                dve.wait_ge(sz_ready.sem, sz_ready.at(c))
                nc.vector.tensor_tensor(yg[:, :, :], yg[:, :, :], sz[:, slot, :, :], ALU.mult).then_inc(ygated.sem, 1)

            for t in (conv_step, delta_ready, dbx_done, scan_done, hc_done, reduce_done, y_taken, ygated):
                t.credit(dve)
            nc.vector.memset(xraw[:, :, 0:TAPS - 1], 0.0).then_inc(zeroed.sem, 1)
            nc.vector.memset(h_in[:, :, :], 0.0).then_inc(zeroed.sem, 1)
            nc.vector.memset(w_xp[:, :, NBC:LOW], 0.0).then_inc(zeroed.sem, 1)
            dve.wait_ge(zeroed.sem, 3)
            dve.wait_ge(consts.sem, 16 * (CONSTS - 1))
            for t in range(TAPS):
                conv_tap(0, 0, t)
            halo(0)
            dve.wait_ge(sel_ready.sem, 1)
            low_parts(0, 0)
            make_delta(0, 0)
            make_u(0, 0)
            with dve.Fori(0, CHUNKS // 2) as i:
                for s in range(2):
                    c, k, f = 2 * i + s, 2 * i + s + 1, 1 - s
                    drive(c, s, 0)
                    for n in range(NST):
                        if n >= 1:
                            weigh(c, n - 1)
                        if n + 1 < NST:
                            drive(c, s, n + 1)
                        scan(c, n)
                        if n == FRONT + 2:
                            low_parts(k, f)
                        elif n == FRONT + 6:
                            make_delta(k, f)
                    weigh(c, NST - 1)
                    make_u(k, f)
                    gate_out(c, s)
    nc.clear_and_free_semaphores(sems)
    nc.all_engine_barrier()


EPS = 1e-5
NT = TOKENS // P


def tree_ffn(nc, y_scr, x_rows, W_outT, F_inT, F_bias, F_outT, ident, x2_rows, x2_T):
    DI, PAR, DEPTH = 512, 8, 7
    NODES = 2 ** (DEPTH + 1) - 1
    WIDTH = PAR * NODES
    DB = DI // P
    LB = 4
    LC = WIDTH // LB
    NB = -(-WIDTH // P)
    TAIL = WIDTH - (NB - 1) * P
    TG = NB // 4
    TR = TG + 2

    y_view = y_scr.rearrange("(d p) t -> p d t", p=P)
    x2T_view = x2_T.rearrange("(k p) t -> p k t", p=P)

    sems = []
    with ExitStack() as ctx:
        def sb(name, shape, dt=F32):
            return ctx.enter_context(nc.sbuf_tensor(name, shape, dt))

        def pb(name, shape):
            return ctx.enter_context(nc.psum_tensor(name, shape, F32))

        def tally(name, per=1, ahead=0):
            sems.append(nc.alloc_semaphore(name))
            return Tally(sems[-1], per, ahead)

        w_out = sb("w_out", [P, DB, DM])
        f_in = sb("f_in", [P, KD, WIDTH])
        f_bias = sb("f_bias", [P, WIDTH])
        f_out = sb("f_out", [P, NB, DM])
        idn = sb("idn2", [P, P])
        yt = sb("yt", [P, 2, DB, P])
        xin = sb("xin", [P, 2, DM])
        r1 = sb("r1", [P, 2, DM])
        x1 = sb("x1", [P, 2, DM])
        x1T = sb("x1T", [P, 2, KD, P])
        lg = sb("lg", [P, 2, PAR, NODES])
        acts = sb("acts", [P, 2, PAR, NODES])
        reach = sb("reach", [P, 2, PAR, NODES])
        mT = sb("mT", [P, NB, P])
        r2 = sb("r2", [P, DM])
        x2 = sb("x2", [P, 2, DM])
        x2T = sb("x2T", [P, 2, KD, P])
        stats = sb("stats2", [P, 2, 6])
        mv = sb("mv2", [P, 2, 2])
        rstd = sb("rstd2", [P, 2, 1])
        nhalf = sb("nhalf2", [P, 1])
        eps_sb = sb("eps2", [P, 1])
        ps_l = pb("ps_l", [P, LB, 512])
        ps_o = pb("ps_o", [P, 512])
        ps_d = pb("ps_d", [P, 512])
        ps_t = pb("ps_t", [P, 2, 4, P])

        consts = tally("consts2")
        in_ld = [tally("in_ld0", 32), tally("in_ld1", 32)]
        ready0 = tally("ready0", 3)
        nh_set = tally("nh_set")
        op_ps = tally("op_ps")
        lg_ps = tally("lg_ps")
        fo_ps = tally("fo_ps", 1, 1)
        tr_ps = tally("tr_ps", TR, 1)
        tr_ev = tally("tr_ev", TR, 1)
        sum1 = tally("sum1", 1, 1)
        stat_seen = tally("stat_seen")
        stat1 = tally("stat1")
        aggr1 = tally("aggr1")
        add1 = tally("add1")
        pow1 = tally("pow1")
        x1_ready = tally("x1_ready")
        kept = tally("kept")
        lg_ready = tally("lg_ready", 1, 1)
        silu_done = tally("silu_done")
        tree = tally("tree", 2 * DEPTH)
        masked = tally("masked", 1, 1)
        sum2 = tally("sum2", 1, 1)
        stat2 = tally("stat2")
        aggr2 = tally("aggr2")
        add2 = tally("add2")
        pow2 = tally("pow2")
        x2_ready = tally("x2_ready", 1, 1)
        x2_out = [tally("x2_out0", 16, 1), tally("x2_out1", 16, 1)]
        x2T_out = [tally("x2T_out0", 16, 1), tally("x2T_out1", 16, 1)]
        NCONST = 6

        block = ctx.enter_context(nc.Block())

        @block.sync
        def _(sp):
            for dst, src in (
                (w_out[:, :, :], W_outT.rearrange("(d p) n -> p d n", p=P)),
                (f_in[:, :, :], F_inT.rearrange("(k p) n -> p k n", p=P)),
                (f_bias[:, :], F_bias.rearrange("(o n) -> o n", o=1).to_broadcast((P, WIDTH))),
                (f_out[:, 0:NB - 1, :], F_outT[0:(NB - 1) * P, :].rearrange("(b p) n -> p b n", p=P)),
                (f_out[0:TAIL, NB - 1, :], F_outT[(NB - 1) * P:WIDTH, :]),
                (idn[:, :], ident),
            ):
                sp.dma_start(dst, src).then_inc(consts.sem, 16)

            def load(slot, col):
                sp.dma_start(yt[:, slot, :, :], y_view[:, :, col]).then_inc(in_ld[slot].sem, 16)
                sp.dma_start(xin[:, slot, :], x_rows[col, :]).then_inc(in_ld[slot].sem, 16)

            load(0, slice(0, P))
            load(1, slice(P, 2 * P))
            for o in x2_out + x2T_out:
                o.credit(sp)
            sp.wait_ge(sum1.sem, sum1.at(0))
            load(0, slice(2 * P, 3 * P))
            with sp.Fori(0, NT // 2) as i:
                ahead = [sp.snap(((2 * i + s + 3) % NT) * P) for s in range(2)]
                here = [sp.snap((2 * i + s) * P) for s in range(2)]
                prev = [sp.snap(((2 * i + s + NT - 1) % NT) * P) for s in range(2)]
                for s in range(2):
                    t = 2 * i + s
                    sp.wait_ge(sum1.sem, sum1.at(t + 1))
                    load(1 - s, bass.ds(ahead[s], P))
                    sp.wait_ge(tr_ev.sem, tr_ev.at(t))
                    sp.dma_start(x2T_view[:, :, bass.ds(prev[s], P)], x2T[:, 1 - s, :, :]).then_inc(x2T_out[1 - s].sem, 16)
                    sp.wait_ge(x2_ready.sem, x2_ready.at(t))
                    sp.dma_start(x2_rows[bass.ds(here[s], P), :], x2[:, s, :]).then_inc(x2_out[s].sem, 16)
            for s in range(2):
                sp.wait_ge(x2T_out[s].sem, x2T_out[s].at(NT // 2 - 1))
            sp.wait_ge(tr_ev.sem, tr_ev.at(NT, 1))
            sp.dma_start(x2T_view[:, :, TOKENS - P:], x2T[:, 1, :, :]).then_inc(x2T_out[1].sem, 16)
            sp.wait_ge(x2T_out[1].sem, x2T_out[1].at(NT // 2))
            for s in range(2):
                sp.wait_ge(x2_out[s].sem, x2_out[s].at(NT // 2 - 1))
            for s in range(2):
                sp.wait_ge(in_ld[s].sem, 32 * (NT // 2 + 2 - s))

        @block.tensor
        def _(pe):
            def out_proj(t, s, loads):
                pe.wait_ge(in_ld[s].sem, 32 * loads)
                pe.wait_ge(sum1.sem, sum1.at(t - 1))
                for d in range(DB):
                    last = nc.tensor.matmul(ps_o[:, 0:DM], yt[:, s, d, :], w_out[:, d, :], start=d == 0, stop=d == DB - 1)
                last.then_inc(op_ps.sem, 1)

            def turn(t, use, blocks):
                pe.wait_ge(tr_ev.sem, tr_ev.at(t, use - 1))
                for b, (rows, src) in enumerate(blocks):
                    last = nc.tensor.transpose(ps_t[0:rows, use % 2, b, :], src, idn[:, :])
                last.then_inc(tr_ps.sem, 1)

            def turn_x1(step, t, s):
                pe.wait_ge(x1_ready.sem, x1_ready.at(t))
                turn(step, 0, [(P, x1[:, s, k * P:(k + 1) * P]) for k in range(KD)])

            def logits(step, t, s, uses=1):
                pe.wait_ge(tr_ev.sem, tr_ev.at(step, uses))
                pe.wait_ge(lg_ready.sem, lg_ready.at(t - 1))
                for b in range(LB):
                    for k in range(KD):
                        last = nc.tensor.matmul(ps_l[:, b, 0:LC], x1T[:, s, k, :], f_in[:, k, b * LC:(b + 1) * LC],
                                                start=k == 0, stop=k == KD - 1)
                last.then_inc(lg_ps.sem, 1)

            def turn_nodes(t, s):
                pe.wait_ge(masked.sem, masked.at(t))
                flat = acts[:, s, :, :].rearrange("p a n -> p (a n)")
                for g in range(TG):
                    blocks = [(min(P, WIDTH - b * P), flat[:, b * P:min((b + 1) * P, WIDTH)]) for b in range(4 * g, 4 * g + 4)]
                    turn(t, 1 + g, blocks)

            def nodes_out(t, s):
                pe.wait_ge(tr_ev.sem, tr_ev.at(t, 1 + TG))
                pe.wait_ge(sum2.sem, sum2.at(t - 1))
                for b in range(NB):
                    rows = min(P, WIDTH - b * P)
                    last = nc.tensor.matmul(ps_d[:, 0:DM], mT[0:rows, b, :], f_out[0:rows, b, :], start=b == 0, stop=b == NB - 1)
                last.then_inc(fo_ps.sem, 1)

            def turn_x2(step, t, s):
                pe.wait_ge(x2_ready.sem, x2_ready.at(t))
                turn(step, 1 + TG, [(P, x2[:, s, k * P:(k + 1) * P]) for k in range(KD)])

            pe.sem_inc(tr_ps.sem, TR - 1)
            pe.wait_ge(consts.sem, 16 * NCONST)
            out_proj(0, 0, 1)
            out_proj(1, 1, 1)
            pe.wait_ge(x1_ready.sem, x1_ready.at(0))
            pe.wait_ge(ready0.sem, 3)
            for k in range(KD):
                last = nc.tensor.transpose(ps_t[:, 1, k, :], x1[:, 0, k * P:(k + 1) * P], idn[:, :])
            last.then_inc(tr_ps.sem, 1)
            logits(-1, 0, 0, TR)
            with pe.Fori(0, NT // 2) as i:
                for s in range(2):
                    t = 2 * i + s
                    turn_x1(t, t + 1, 1 - s)
                    out_proj(t + 2, s, i + 2)
                    logits(t, t + 1, 1 - s)
                    turn_nodes(t, s)
                    nodes_out(t, s)
                    turn_x2(t, t - 1, 1 - s)
            turn_x2_last = [(P, x2[:, 1, k * P:(k + 1) * P]) for k in range(KD)]
            pe.wait_ge(x2_ready.sem, x2_ready.at(NT - 1))
            turn(NT, 0, turn_x2_last)

        @block.scalar
        def _(act):
            def take(t, use, dst, src):
                act.wait_ge(tr_ps.sem, tr_ps.at(t, use + 1))
                return nc.scalar.activation(dst, src, ACT.Copy)

            def take_x(step, use, dst):
                take(step, use, dst, ps_t[:, use % 2, 0:KD, :]).then_inc(tr_ev.sem, 1)

            def gate(t, s, first=False):
                act.wait_ge(lg_ready.sem, lg_ready.at(t))
                if not first:
                    act.wait_ge(tr_ps.sem, tr_ps.at(t - 2, 1 + TG))
                nc.scalar.activation(acts[:, s, :, :], lg[:, s, :, :], ACT.Silu).then_inc(silu_done.sem, 1)

            def take_nodes(t, s):
                act.wait_ge(fo_ps.sem, fo_ps.at(t - 1))
                for g in range(TG):
                    whole = 4 if g < TG - 1 else 3
                    ins = take(t, 1 + g, mT[:, 4 * g:4 * g + whole, :], ps_t[:, (1 + g) % 2, 0:whole, :])
                    if whole < 4:
                        ins = nc.scalar.activation(mT[0:TAIL, NB - 1, :], ps_t[0:TAIL, (1 + g) % 2, 3, :], ACT.Copy)
                    ins.then_inc(tr_ev.sem, 1)

            fo_ps.credit(act)
            act.sem_inc(tr_ev.sem, TR - 1)
            act.wait_ge(tr_ps.sem, tr_ps.at(-1, TR))
            nc.scalar.activation(x1T[:, 0, :, :], ps_t[:, 1, 0:KD, :], ACT.Copy).then_inc(tr_ev.sem, 1)
            gate(0, 0, True)
            with act.Fori(0, NT // 2) as i:
                for s in range(2):
                    t = 2 * i + s
                    take_x(t, 0, x1T[:, 1 - s, :, :])
                    take_nodes(t, s)
                    gate(t + 1, 1 - s)
                    act.wait_ge(x2T_out[1 - s].sem, x2T_out[1 - s].at(i - 1))
                    take_x(t, 1 + TG, x2T[:, 1 - s, :, :])
            act.wait_ge(x2T_out[1].sem, x2T_out[1].at(NT // 2 - 1))
            take_x(NT, 0, x2T[:, 1, :, :])

        @block.gpsimd
        def _(pool):
            def inv_std(t, n, aggr, add, pw):
                pool.wait_ge(aggr.sem, aggr.at(t))
                nc.gpsimd.tensor_tensor(rstd[:, n, :], mv[:, n, 1:2], eps_sb[:, :], ALU.add).then_inc(add.sem, 1)
                pool.wait_ge(add.sem, add.at(t))
                nc.gpsimd.tensor_tensor(rstd[:, n, :], rstd[:, n, :], nhalf[:, :], ALU.pow).then_inc(pw.sem, 1)

            nc.gpsimd.memset(nhalf[:, :], -0.5).then_inc(nh_set.sem, 1)
            nc.gpsimd.memset(eps_sb[:, :], EPS).then_inc(nh_set.sem, 1)
            pool.wait_ge(nh_set.sem, 2)
            inv_std(0, 0, aggr1, add1, pow1)
            inv_std(1, 0, aggr1, add1, pow1)
            with pool.Fori(0, NT // 2) as i:
                for s in range(2):
                    t = 2 * i + s
                    inv_std(t + 2, 0, aggr1, add1, pow1)
                    inv_std(t, 1, aggr2, add2, pow2)

        @block.vector
        def _(dve):
            def moments(t, n, r, stat, aggr):
                nc.vector.bn_stats(stats[:, n, :], r).then_inc(stat.sem, 1)
                dve.wait_ge(stat.sem, stat.at(t))
                dve.sem_inc(stat_seen.sem)
                nc.vector.bn_aggr(mv[:, n, :], stats[:, n, :]).then_inc(aggr.sem, 1)

            def norm1(t, s, first=False):
                dve.wait_ge(op_ps.sem, op_ps.at(t))
                nc.vector.tensor_tensor(r1[:, s, :], ps_o[:, 0:DM], xin[:, s, :], ALU.add).then_inc(sum1.sem, 1)
                dve.wait_ge(sum1.sem, sum1.at(t))
                moments(t, 0, r1[:, s, :], stat1, aggr1)
                dve.wait_ge(pow1.sem, pow1.at(t))
                if not first:
                    dve.wait_ge(tr_ps.sem, tr_ps.at(t - 3, 1))
                    dve.wait_ge(kept.sem, kept.at(t - 2))
                nc.vector.tensor_scalar(x1[:, s, :], r1[:, s, :], mv[:, 0, 0:1], rstd[:, 0, :], ALU.subtract,
                                        ALU.mult).then_inc(x1_ready.sem, 1)
                dve.wait_ge(x1_ready.sem, x1_ready.at(t))

            def path(t, s):
                dve.wait_ge(lg_ps.sem, lg_ps.at(t))
                flat = lg[:, s, :, :].rearrange("p a n -> p (a n)").rearrange("p (b n) -> p b n", b=LB)
                nc.vector.tensor_tensor(flat, ps_l[:, :, 0:LC], f_bias[:, :].rearrange("p (b n) -> p b n", b=LB),
                                        ALU.add).then_inc(lg_ready.sem, 1)
                dve.wait_ge(lg_ready.sem, lg_ready.at(t))
                for d in range(DEPTH):
                    lo, n = 2 ** d - 1, 2 ** d
                    kids = reach[:, s, :, 2 * n - 1:4 * n - 1].rearrange("p a (n two) -> p a n two", two=2)
                    here = reach[:, s, :, lo:lo + n]
                    if d:
                        dve.wait_ge(tree.sem, tree.at(t, 2 * d))
                    nc.vector.scalar_tensor_tensor(kids[:, :, :, 1], lg[:, s, :, lo:lo + n], 0.0, here, ALU.is_gt,
                                                   ALU.mult).then_inc(tree.sem, 1)
                    dve.wait_ge(tree.sem, tree.at(t, 2 * d + 1))
                    nc.vector.tensor_tensor(kids[:, :, :, 0], here, kids[:, :, :, 1], ALU.subtract).then_inc(tree.sem, 1)
                dve.wait_ge(tree.sem, tree.at(t))
                dve.wait_ge(silu_done.sem, silu_done.at(t))
                nc.vector.tensor_tensor(acts[:, s, :, :], acts[:, s, :, :], reach[:, s, :, :], ALU.mult).then_inc(masked.sem, 1)

            def keep_x1(t, s):
                dve.wait_ge(x2_ready.sem, x2_ready.at(t - 1))
                nc.vector.tensor_copy(r2[:, :], x1[:, s, :]).then_inc(kept.sem, 1)

            def norm2(t, s, i):
                dve.wait_ge(fo_ps.sem, fo_ps.at(t))
                dve.wait_ge(kept.sem, kept.at(t))
                nc.vector.tensor_tensor(r2[:, :], ps_d[:, 0:DM], r2[:, :], ALU.add).then_inc(sum2.sem, 1)
                dve.wait_ge(sum2.sem, sum2.at(t))
                moments(t, 1, r2[:, :], stat2, aggr2)
                dve.wait_ge(pow2.sem, pow2.at(t))
                dve.wait_ge(x2_out[s].sem, x2_out[s].at(i - 1))
                dve.wait_ge(tr_ps.sem, tr_ps.at(t - 1))
                nc.vector.tensor_scalar(x2[:, s, :], r2[:, :], mv[:, 1, 0:1], rstd[:, 1, :], ALU.subtract,
                                        ALU.mult).then_inc(x2_ready.sem, 1)
                dve.wait_ge(x2_ready.sem, x2_ready.at(t))

            for t in (sum1, lg_ready, masked, sum2, x2_ready):
                t.credit(dve)
            nc.vector.memset(reach[:, 0, :, 0:1], 1.0).then_inc(ready0.sem, 1)
            nc.vector.memset(reach[:, 1, :, 0:1], 1.0).then_inc(ready0.sem, 1)
            nc.vector.memset(x2[:, 1, :], 0.0).then_inc(ready0.sem, 1)
            dve.wait_ge(ready0.sem, 3)
            dve.wait_ge(consts.sem, 16 * NCONST)
            norm1(0, 0, True)
            norm1(1, 1, True)
            path(0, 0)
            with dve.Fori(0, NT // 2) as i:
                for s in range(2):
                    t = 2 * i + s
                    keep_x1(t, s)
                    norm1(t + 2, s)
                    path(t + 1, 1 - s)
                    norm2(t, s, i)
    nc.clear_and_free_semaphores(sems)
    nc.all_engine_barrier()


HEADS, KV, HD = 16, 4, 64
GROUP = HEADS // KV


def qkv(nc, x2_T, Wqk, Wv, rope_q, rope_k, q_scr, k_scr, v_scr):
    TC = 512
    CHUNKS = TOKENS // TC
    PAIRS = KV + 1
    HALF = HD // 2
    PER = TC // P
    xT_view = x2_T.rearrange("(k p) t -> p k t", p=P)
    v_view = v_scr.rearrange("(n p) d -> p n d", p=P)

    sems = []
    with ExitStack() as ctx:
        def sb(name, shape, dt=F32):
            return ctx.enter_context(nc.sbuf_tensor(name, shape, dt))

        def pb(name, shape):
            return ctx.enter_context(nc.psum_tensor(name, shape, F32))

        def tally(name, per=1, ahead=0):
            sems.append(nc.alloc_semaphore(name))
            return Tally(sems[-1], per, ahead)

        w_qk = sb("w_qk", [P, KD, 2 * PAIRS, P])
        w_v = sb("w_v", [P, KD, KV * HD])
        rope = sb("rope", [P, 2, 4, LENGTH])
        xt = sb("xt3", [P, 2, KD, TC])
        even = sb("even", [P, 2, 2, TC])
        odd = sb("odd", [P, 2, 2, TC])
        rot = sb("rot", [P, 2, 2, TC])
        v_sb = sb("v_sb", [P, 2, PER, KV, HD + 1])
        ps_qk = pb("ps_qk", [P, 2, 2, TC])
        ps_v = pb("ps_v", [P, PER, KV * HD])

        consts = tally("consts3")
        xt_ld = [tally("xt3_ld0"), tally("xt3_ld1")]
        qk_ps = tally("qk_ps", PAIRS)
        v_ps = tally("v_ps")
        v_ev = tally("v_ev", 1, 1)
        even_done = tally("even_done", PAIRS)
        odd_done = tally("odd_done", PAIRS, 1)
        rot_done = tally("rot_done", PAIRS)
        qk_out = [tally("qk_out0", 32 * PAIRS, 1), tally("qk_out1", 32 * PAIRS, 1)]
        ones_set = tally("ones_set3")
        v_out = [tally("v_out0", 16, 1), tally("v_out1", 16, 1)]
        NCONST = 4

        block = ctx.enter_context(nc.Block())

        @block.sync
        def _(sp):
            for dst, src in (
                (w_qk[:, :, :, :], Wqk.rearrange("(k p) b n -> p k b n", p=P)),
                (w_v[:, :, :], Wv.rearrange("(k p) n -> p k n", p=P)),
                (rope[:, 0, :, :], rope_q),
                (rope[:, 1, :, :], rope_k),
            ):
                sp.dma_start(dst, src).then_inc(consts.sem, 16)
            for k in range(2):
                sp.dma_start(xt[:, k, :, :], xT_view[:, :, k * TC:(k + 1) * TC]).then_inc(xt_ld[k].sem, 16)
            for o in qk_out + v_out:
                o.credit(sp)
            with sp.Fori(0, CHUNKS // 2) as i:
                ahead = [sp.snap(((2 * i + s + 2) % CHUNKS) * TC) for s in range(2)]
                batch = sp.snap(i // (CHUNKS // 4))
                pos = [sp.snap(((2 * i + s) % (CHUNKS // 2)) * TC) for s in range(2)]
                first = [sp.snap((2 * i + s) * PER) for s in range(2)]
                q_row = [sp.snap(batch * HEADS + GROUP * g) for g in range(KV)]
                k_row = sp.snap(batch * KV)
                for s in range(2):
                    c = 2 * i + s
                    for p in range(PAIRS):
                        slot = (s * PAIRS + p) % 2
                        sp.wait_ge(rot_done.sem, rot_done.at(c, p + 1))
                        for eo in range(2):
                            rows = slice(eo * HALF, (eo + 1) * HALF)
                            to = (q_scr[bass.ds(q_row[p], GROUP), rows, bass.ds(pos[s], TC)] if p < KV
                                  else k_scr[bass.ds(k_row, KV), rows, bass.ds(pos[s], TC)])
                            sp.dma_start(to, rot[:, slot, eo, :]).then_inc(qk_out[slot].sem, 16)
                    sp.wait_ge(v_ev.sem, v_ev.at(c))
                    sp.dma_start(v_view[:, bass.ds(first[s], PER), :], v_sb[:, s, :, :, :].rearrange("p n h d -> p n (h d)")).then_inc(v_out[s].sem, 16)
                    sp.dma_start(xt[:, s, :, :], xT_view[:, :, bass.ds(ahead[s], TC)]).then_inc(xt_ld[s].sem, 16)
            for s in range(2):
                sp.wait_ge(xt_ld[s].sem, 16 * (CHUNKS // 2 + 1))
                sp.wait_ge(v_out[s].sem, v_out[s].at(CHUNKS // 2 - 1))
                sp.wait_ge(qk_out[s].sem, qk_out[s].at(CHUNKS // 2 - 1))

        @block.tensor
        def _(pe):
            pe.wait_ge(consts.sem, 16 * NCONST)
            with pe.Fori(0, CHUNKS // 2) as i:
                for s in range(2):
                    c = 2 * i + s
                    pe.wait_ge(xt_ld[s].sem, 16 * (i + 1))
                    for p in range(PAIRS):
                        slot = (s * PAIRS + p) % 2
                        pe.wait_ge(odd_done.sem, odd_done.at(c, p - 1))
                        for eo in range(2):
                            for k in range(KD):
                                last = nc.tensor.matmul(ps_qk[:, slot, eo, :], w_qk[:, k, 2 * p + eo, :], xt[:, s, k, :],
                                                        start=k == 0, stop=k == KD - 1)
                        last.then_inc(qk_ps.sem, 1)
                    pe.wait_ge(v_ev.sem, v_ev.at(c - 1))
                    for n in range(PER):
                        for k in range(KD):
                            last = nc.tensor.matmul(ps_v[:, n, :], xt[:, s, k, n * P:(n + 1) * P], w_v[:, k, :],
                                                    start=k == 0, stop=k == KD - 1)
                    last.then_inc(v_ps.sem, 1)

        @block.scalar
        def _(act):
            v_ev.credit(act)
            act.wait_ge(ones_set.sem, 1)
            with act.Fori(0, CHUNKS // 2) as i:
                for s in range(2):
                    c = 2 * i + s
                    act.wait_ge(v_ps.sem, v_ps.at(c))
                    act.wait_ge(v_out[s].sem, v_out[s].at(i - 1))
                    nc.scalar.activation(v_sb[:, s, :, :, 0:HD], ps_v[:, :, :].rearrange("p n (h d) -> p n h d", h=KV),
                                         ACT.Copy).then_inc(v_ev.sem, 1)

        @block.gpsimd
        def _(pool):
            nc.gpsimd.memset(v_sb[:, :, :, :, HD:HD + 1], 1.0).then_inc(ones_set.sem, 1)

        @block.vector
        def _(dve):
            odd_done.credit(dve)
            dve.wait_ge(consts.sem, 16 * NCONST)
            with dve.Fori(0, CHUNKS // 2) as i:
                pos = [dve.snap(((2 * i + s) % (CHUNKS // 2)) * TC) for s in range(2)]
                for s in range(2):
                    c = 2 * i + s
                    for p in range(PAIRS):
                        slot = (s * PAIRS + p) % 2
                        kind = p // KV
                        dve.wait_ge(qk_ps.sem, qk_ps.at(c, p + 1))
                        for eo, dst, done in ((0, even, even_done), (1, odd, odd_done)):
                            nc.vector.tensor_tensor(dst[:, slot, :, :],
                                                    ps_qk[:, slot, eo:eo + 1, :].to_broadcast((P, 2, TC)),
                                                    rope[:, kind, 2 * eo:2 * eo + 2, bass.ds(pos[s], TC)],
                                                    ALU.mult).then_inc(done.sem, 1)
                        dve.wait_ge(even_done.sem, even_done.at(c, p + 1))
                        dve.wait_ge(odd_done.sem, odd_done.at(c, p + 1))
                        dve.wait_ge(qk_out[slot].sem, qk_out[slot].at(i - 1, 32 * ((s * PAIRS + p) // 2) + 32 * PAIRS))
                        nc.vector.tensor_tensor(rot[:, slot, :, :], even[:, slot, :, :], odd[:, slot, :, :],
                                                ALU.add).then_inc(rot_done.sem, 1)
    nc.clear_and_free_semaphores(sems)
    nc.all_engine_barrier()


def attention(nc, q_scr, k_scr, v_scr, ident, causal, attn):
    QT = LENGTH // P
    CW = 512
    CB = CW // P
    UNITS = QT // 2
    NCH = [-(-(r + 1) // CB) for r in range(QT)]
    CHUNKS = [[(r, c) for r in (QT - 1 - k, k) for c in range(NCH[r])] for k in range(UNITS)]
    RING = len(CHUNKS[0])
    ON_DVE = (1,)
    AHEAD = 2
    PER = UNITS * RING
    QUEUE = (0, 3, 1, 2)
    NHEADS = BATCH * HEADS
    NGROUPS = BATCH * KV
    assert all(len(u) == RING for u in CHUNKS) and PER % 2 == 0
    attn_view = attn.rearrange("(n p) d -> p n d", p=P)

    def blocks(r, c):
        return min(CB, r + 1 - c * CB)

    sems = []
    with ExitStack() as ctx:
        def sb(name, shape, dt=F32):
            return ctx.enter_context(nc.sbuf_tensor(name, shape, dt))

        def pb(name, shape):
            return ctx.enter_context(nc.psum_tensor(name, shape, F32))

        def tally(name, per=1, ahead=0):
            sems.append(nc.alloc_semaphore(name))
            return Tally(sems[-1], per, ahead)

        idn = sb("idn3", [P, P])
        idn_r = sb("idn_r", [P, P], F32R)
        mask = sb("mask", [P, P])
        mask_r = sb("mask_r", [P, P], F32R)
        qbuf = sb("qbuf", [P, QT, P], F32R)
        kbuf = sb("kbuf", [P, 2, 2, LENGTH], F32R)
        qstage = sb("qstage", [P, QT, P])
        kstage = sb("kstage", [P, LENGTH])
        v1 = sb("v1", [P, BATCH * QT, KV, HD + 1])
        probs = sb("probs", [P, RING, CB, P])
        probsT = sb("probsT", [P, RING, CB, P])
        pmax = sb("pmax", [P, 2, 4])
        negm = sb("negm", [P, 2, 1])
        rinv = sb("rinv", [P, 2, 1])
        ostage = sb("ostage", [P, QT, HD])
        ps_s = pb("ps_s", [P, RING, CW])
        ps_t = pb("ps_t3", [P, 2, CB, P])
        ps_o = pb("ps_o3", [P, CW])

        consts = tally("consts3b")
        rounded = tally("rounded")
        q_ld = [tally("q_ld%d" % j, 32) for j in range(4)]
        k_ld = tally("k_ld", 32)
        high_k = tally("high_k")
        high_q = tally("high_q", 4)
        q_ready = tally("q_ready", 4)
        k_ready = tally("k_ready")
        pool_seen = tally("pool_seen")
        s_done = tally("s_done", PER, 1)
        t_done = tally("t_done", PER, 1)
        pv_done = tally("pv_done", PER, 1)
        exp_done = tally("exp_done", PER, 1)
        ev = [tally("ev0", PER // 2, 1), tally("ev1", PER // 2, 1)]
        cmax = tally("cmax", PER)
        m_done = tally("m_done", QT)
        r_done = tally("r_done", QT)
        o_done = tally("o_done", QT, 1)
        o_out = [tally("o_out0", 32, 1), tally("o_out1", 16, 1)]
        NCONST = 3

        def ends(k, r):
            return k * RING + max(v for v, (q, c) in enumerate(CHUNKS[k]) if q == r) + 1

        block = ctx.enter_context(nc.Block())

        @block.sync
        def _(sp):
            sp.dma_start(idn[:, :], ident).then_inc(consts.sem, 16)
            sp.dma_start(mask[:, :], causal).then_inc(consts.sem, 16)
            def load_keys(group):
                for half in range(2):
                    sp.dma_start(kstage[half * HD:(half + 1) * HD, :], k_scr[bass.ds(group, 1)].rearrange("g p t -> p (g t)")
                                 ).then_inc(k_ld.sem, 16)

            def load_queries(hx, j):
                for half in range(2):
                    sp.dma_start(qstage[half * HD:(half + 1) * HD, 4 * j:4 * j + 4, :].rearrange("p n t -> p (n t)"),
                                 q_scr[bass.ds(hx, 1), :, j * CW:(j + 1) * CW].rearrange("o p t -> p (o t)")
                                 ).then_inc(q_ld[j].sem, 16)

            load_keys(0)
            for j in QUEUE:
                load_queries(0, j)
            sp.dma_start(v1[:, :, :, :].rearrange("p n h d -> p n (h d)"), v_scr.rearrange("(n p) d -> p n d", p=P)
                         ).then_inc(consts.sem, 16)
            for o in o_out:
                o.credit(sp)
            with sp.Fori(0, NGROUPS) as g:
                group = sp.snap((g + 1) % NGROUPS)
                sp.wait_ge(k_ready.sem, k_ready.at(g))
                load_keys(group)
                with sp.Fori(0, GROUP) as j4:
                    hx = sp.snap(g * GROUP + j4)
                    nxt = sp.snap((hx + 1) % NHEADS)
                    first = sp.snap((hx // HEADS) * QT)
                    col = sp.snap((hx % HEADS) * HD)
                    for half in range(2):
                        for n in (2 * half, 2 * half + 1):
                            j = QUEUE[n]
                            sp.wait_ge(q_ready.sem, q_ready.at(hx, n + 1))
                            load_queries(nxt, j)
                        sp.wait_ge(o_done.sem, o_done.at(hx, (half + 1) * UNITS))
                        for lo, hi in ([(0, 4), (12, 16)], [(4, 12)])[half]:
                            sp.dma_start(attn_view[:, bass.ds(first + lo, hi - lo), bass.ds(col, HD)],
                                         ostage[:, lo:hi, :]).then_inc(o_out[half].sem, 16)
            for j in range(4):
                sp.wait_ge(q_ld[j].sem, q_ld[j].at(NHEADS))
            sp.wait_ge(q_ready.sem, q_ready.at(NHEADS))
            sp.wait_ge(k_ready.sem, NGROUPS + 1)
            sp.wait_ge(k_ld.sem, k_ld.at(NGROUPS))
            for half in range(2):
                sp.wait_ge(o_out[half].sem, o_out[half].at(NHEADS - 1))

        @block.tensor
        def _(pe):
            def scores(hx, kslot, k, v):
                r, c = CHUNKS[k][v]
                u = k * RING + v
                w = blocks(r, c) * P
                pe.wait_ge(exp_done.sem, exp_done.at(hx, u - RING + 1))
                for part in range(2):
                    last = nc.tensor.matmul(ps_s[:, v, 0:w], qbuf[:, r, :],
                                            kbuf[:, bass.ds(kslot, 1), part, c * CW:c * CW + w],
                                            start=part == 0, stop=part == 1 and c < NCH[r] - 1)
                if c == NCH[r] - 1:
                    last = nc.tensor.matmul(ps_s[:, v, w - P:w], idn_r[:, :], mask_r[:, :], start=False, stop=True)
                last.then_inc(s_done.sem, 1)

            def turn(hx, k, v):
                r, c = CHUNKS[k][v]
                u = k * RING + v
                pe.wait_ge(exp_done.sem, exp_done.at(hx, u + 1))
                pe.wait_ge(ev[u % 2].sem, ev[u % 2].at(hx, u // 2))
                for j in range(blocks(r, c)):
                    last = nc.tensor.transpose(ps_t[:, u % 2, j, :], probs[:, v, j, :], idn[:, :])
                last.then_inc(t_done.sem, 1)

            def weigh(hx, first, kv, k, v):
                r, c = CHUNKS[k][v]
                u = k * RING + v
                short = r < UNITS
                pe.wait_ge(ev[u % 2].sem, ev[u % 2].at(hx, u // 2 + 1))
                if c == 0:
                    pe.wait_ge(o_done.sem, o_done.at(hx, 2 * k + short))
                for j in range(blocks(r, c)):
                    kb = c * CB + j
                    last = nc.tensor.matmul(ps_o[:, 0:HD + 1], probsT[:, v, j, :],
                                            v1[:, bass.ds(first + kb, 1), bass.ds(kv, 1), :],
                                            start=kb == 0, stop=kb == r)
                last.then_inc(pv_done.sem, 1)

            pe.wait_ge(consts.sem, 16 * NCONST)
            pe.wait_ge(rounded.sem, 2)
            s_done.credit(pe)
            t_done.credit(pe)
            pv_done.credit(pe)
            pe.wait_ge(k_ready.sem, 1)
            pe.wait_ge(q_ready.sem, 2)
            for v in range(RING):
                scores(0, 0, 0, v)
            with pe.Fori(0, NHEADS) as hx:
                kslot = pe.snap((hx // GROUP) % 2)
                kslot_next = pe.snap(((hx + 1) // GROUP) % 2)
                kv = pe.snap((hx // GROUP) % KV)
                first = pe.snap((hx // HEADS) * QT)
                for k in range(UNITS):
                    if k == UNITS // 2 - 1:
                        pe.wait_ge(q_ready.sem, q_ready.at(hx, 4))
                    elif k == UNITS - 1:
                        pe.wait_ge(q_ready.sem, q_ready.at(hx + 1, 2))
                        pe.wait_ge(k_ready.sem, (hx + 1) // GROUP + 1)
                    for v in range(RING):
                        if k < UNITS - 1:
                            scores(hx, kslot, k + 1, v)
                        else:
                            scores(hx + 1, kslot_next, 0, v)
                        turn(hx, k, v)
                        if k or v:
                            weigh(hx, first, kv, k - (v == 0), (v - 1) % RING)
                weigh(hx, first, kv, UNITS - 1, RING - 1)

        @block.gpsimd
        def _(pool):
            def keys(g):
                pool.wait_ge(k_ld.sem, k_ld.at(g))
                pool.sem_inc(pool_seen.sem)
                slot = bass.ds(g % 2, 1)
                nc.gpsimd.tensor_copy(kbuf[:, slot, 0, :], kstage[:, :]).then_inc(high_k.sem, 1)
                pool.wait_ge(high_k.sem, high_k.at(g))
                pool.sem_inc(pool_seen.sem)
                nc.gpsimd.tensor_tensor(kbuf[:, slot, 1, :], kstage[:, :], kbuf[:, slot, 0, :].bitcast(F32),
                                        ALU.subtract).then_inc(k_ready.sem, 1)
                pool.wait_ge(k_ready.sem, g + 1)
                pool.sem_inc(pool_seen.sem)

            def queries(hx, n):
                j, low = QUEUE[n], slice(HD, P)
                pool.wait_ge(q_ld[j].sem, q_ld[j].at(hx))
                pool.sem_inc(pool_seen.sem)
                nc.gpsimd.tensor_copy(qbuf[:, 4 * j:4 * j + 4, :], qstage[:, 4 * j:4 * j + 4, :]).then_inc(high_q.sem, 1)
                pool.wait_ge(high_q.sem, high_q.at(hx, n + 1))
                pool.sem_inc(pool_seen.sem)
                nc.gpsimd.tensor_tensor(qbuf[low, 4 * j:4 * j + 4, :], qstage[low, 4 * j:4 * j + 4, :],
                                        qbuf[low, 4 * j:4 * j + 4, :].bitcast(F32), ALU.subtract).then_inc(q_ready.sem, 1)
                pool.wait_ge(q_ready.sem, q_ready.at(hx, n + 1))
                pool.sem_inc(pool_seen.sem)

            keys(0)
            for n in range(4):
                queries(0, n)
            with pool.Fori(0, NGROUPS) as g:
                pool.wait_ge(s_done.sem, s_done.at(g * GROUP, RING))
                keys(g + 1)
                with pool.Fori(0, GROUP) as j4:
                    hx = pool.snap(g * GROUP + j4)
                    for half in range(2):
                        pool.wait_ge(s_done.sem, s_done.at(hx, (half + 1) * PER // 2))
                        for n in (2 * half, 2 * half + 1):
                            queries(hx + 1, n)

        @block.scalar
        def _(act):
            def exps(hx, k, v):
                r, c = CHUNKS[k][v]
                u = k * RING + v
                short = r < UNITS
                if c == 0:
                    act.wait_ge(m_done.sem, m_done.at(hx, 2 * k + short + 1))
                act.wait_ge(t_done.sem, t_done.at(hx, u - RING + 1))
                nc.scalar.activation(probs[:, v, 0:blocks(r, c), :], ps_s[:, v, 0:blocks(r, c) * P], ACT.Exp,
                                     bias=negm[:, short, :]).then_inc(exp_done.sem, 1)

            def take(hx, k, v):
                r, c = CHUNKS[k][v]
                u = k * RING + v
                n = blocks(r, c)
                act.wait_ge(t_done.sem, t_done.at(hx, u + 1))
                act.wait_ge(pv_done.sem, pv_done.at(hx, u - RING + 1))
                nc.scalar.activation(probsT[:, v, 0:n, :], ps_t[:, u % 2, 0:n, :], ACT.Copy).then_inc(ev[u % 2].sem, 1)

            act.wait_ge(consts.sem, 16 * NCONST)
            for dst, src in ((idn_r, idn), (mask_r, mask)):
                nc.scalar.activation(dst[:, :], src[:, :], ACT.Copy).then_inc(rounded.sem, 1)
            exp_done.credit(act)
            ev[1].credit(act)
            for v in range(AHEAD):
                exps(0, 0, v)
            with act.Fori(0, NHEADS) as hx:
                for k in range(UNITS):
                    for v in range(RING):
                        if v not in ON_DVE:
                            take(hx, k, v)
                        ahead = k * RING + v + AHEAD
                        exps(hx + ahead // PER, ahead % PER // RING, ahead % RING)

        @block.vector
        def _(dve):
            def peak(hx, k, v):
                r, c = CHUNKS[k][v]
                u = k * RING + v
                short = r < UNITS
                n = 2 * k + short
                dve.wait_ge(s_done.sem, s_done.at(hx, u + 1))
                nc.vector.reduce_max(pmax[:, short, c:c + 1], ps_s[:, v, 0:blocks(r, c) * P],
                                     axis=mybir.AxisListType.X).then_inc(cmax.sem, 1)
                if c == NCH[r] - 1:
                    dve.wait_ge(cmax.sem, cmax.at(hx, u + 1))
                    before = k - 1 if k else UNITS - 1
                    dve.wait_ge(exp_done.sem, exp_done.at(hx, ends(before, before if short else QT - 1 - before) - (0 if k else PER)))
                    nc.vector.reduce_max(negm[:, short, :], pmax[:, short, 0:NCH[r]], axis=mybir.AxisListType.X,
                                         negate=True).then_inc(m_done.sem, 1)

            def take(hx, k, v):
                r, c = CHUNKS[k][v]
                u = k * RING + v
                n = blocks(r, c)
                dve.wait_ge(t_done.sem, t_done.at(hx, u + 1))
                dve.wait_ge(pv_done.sem, pv_done.at(hx, u - RING + 1))
                nc.vector.tensor_copy(probsT[:, v, 0:n, :], ps_t[:, u % 2, 0:n, :]).then_inc(ev[u % 2].sem, 1)

            def normalise(hx, k, r):
                short = r < UNITS
                n = 2 * k + short
                dve.wait_ge(pv_done.sem, pv_done.at(hx, ends(k, r)))
                nc.vector.reciprocal(rinv[:, short, :], ps_o[:, HD:HD + 1]).then_inc(r_done.sem, 1)
                dve.wait_ge(r_done.sem, r_done.at(hx, n + 1))
                if n % UNITS == 0:
                    dve.wait_ge(o_out[n // UNITS].sem, o_out[n // UNITS].at(hx - 1))
                nc.vector.tensor_scalar(ostage[:, r, :], ps_o[:, 0:HD], rinv[:, short, :], None,
                                        ALU.mult).then_inc(o_done.sem, 1)

            ev[0].credit(dve)
            o_done.credit(dve)
            for v in range(RING):
                peak(0, 0, v)
            with dve.Fori(0, NHEADS) as hx:
                for k in range(UNITS):
                    for v in range(RING):
                        peak(hx + (k + 1) // UNITS, (k + 1) % UNITS, v)
                        if v in ON_DVE:
                            take(hx, k, v)
                        if k and v == 0:
                            normalise(hx, k - 1, k - 1)
                        if v == NCH[QT - 1 - k]:
                            normalise(hx, k, QT - 1 - k)
                normalise(hx, UNITS - 1, UNITS - 1)
    nc.clear_and_free_semaphores(sems)
    nc.all_engine_barrier()


I32 = mybir.dt.int32
U32 = mybir.dt.uint32
EXPERTS, TOPK, FF = 64, 8, 192
VMAX = TOKENS * TOPK
SPARE = 8
MAXG = TOKENS * TOPK // P + EXPERTS + SPARE
COLS = EXPERTS * NT + SPARE


def route(nc, attn, x2_rows, Wo, gate_wT, ident, before, iota_e, v_first, base, e_base, iota_g, incl, no_place,
          x3_rows, table, plan):
    AD = HEADS * HD
    AB = AD // P
    STEPS = 9

    sems = []
    with ExitStack() as ctx:
        def sb(name, shape, dt=F32):
            return ctx.enter_context(nc.sbuf_tensor(name, shape, dt))

        def pb(name, shape):
            return ctx.enter_context(nc.psum_tensor(name, shape, F32))

        def tally(name, per=1, ahead=0):
            sems.append(nc.alloc_semaphore(name))
            return Tally(sems[-1], per, ahead)

        w_o = sb("w_o", [P, AB, DM])
        w_g = sb("w_g", [P, KD, EXPERTS])
        idn = sb("idn4", [P, P])
        before_sb = sb("before_sb", [P, P])
        iota_sb = sb("iota_sb", [P, EXPERTS])
        ones = sb("ones4", [P, P])
        at = sb("at", [P, 2, AD])
        x2t = sb("x2t", [P, 2, DM])
        aT = sb("aT", [P, AB, P])
        r3 = sb("r3", [P, DM])
        x3 = sb("x3", [P, 2, DM])
        idx_f = sb("idx_f", [P, TOPK])
        entry = sb("entry", [P, 2, TOPK, 2])
        xT = sb("xT4", [P, KD, P])
        stats = sb("stats4", [P, 6])
        mv = sb("mv4", [P, 2])
        rstd = sb("rstd4", [P, 1])
        nhalf = sb("nhalf4", [P, 1])
        eps_sb = sb("eps4", [P, 1])
        negm = sb("negm4", [P, 1])
        ex = sb("ex", [P, EXPERTS])
        esum = sb("esum", [P, 1])
        erec = sb("erec", [P, 1])
        sc = sb("sc", [P, EXPERTS])
        top = sb("top", [P, TOPK])
        idx = sb("idx", [P, TOPK], U32)
        rest = sb("rest", [P, EXPERTS])
        chosen = sb("chosen", [P, EXPERTS])
        tsum = sb("tsum", [P, 1])
        macc = sb("macc", [P, EXPERTS])
        junk = sb("junk4", [P, TOPK, EXPERTS])
        dest_f = sb("dest_f", [P, TOPK])
        dest_i = sb("dest_i", [P, TOPK], I32)
        col = sb("col", [P, TOPK], I32)
        dest = sb("dest", [P, 2, TOPK], I32)
        e_base_sb = sb("e_base_sb", [EXPERTS, 1])
        g_sb = sb("g_sb", [EXPERTS, MAXG])
        incl_sb = sb("incl_sb", [EXPERTS, 2, EXPERTS])
        n_i = sb("n_i", [EXPERTS, 1], I32)
        n_f = sb("n_f", [EXPERTS, 1])
        ends = sb("ends", [EXPERTS, 1])
        past = sb("past", [EXPERTS, MAXG])
        first_f = sb("first_f", [1, MAXG])
        plan_sb = sb("plan_sb", [1, 2 * MAXG + EXPERTS + 1], I32)
        ps_t = pb("ps_t4", [P, 2, 4, P])
        ps_o = pb("ps_o4", [P, 512])
        ps_x = pb("ps_x4", [P, 4, P])
        ps_g = pb("ps_g4", [P, 512])
        ps_p = pb("ps_p4", [P, 512])

        consts = tally("consts4")
        nh_set = tally("nh_set4")
        in_ld = [tally("in4_ld0", 32), tally("in4_ld1", 32)]
        at_tr = tally("at_tr", 2)
        at_ev = tally("at_ev", 2, 1)
        op_ps = tally("op_ps4", 1, 1)
        sum3 = tally("sum3", 1, 1)
        stat = tally("stat4")
        stat_seen = tally("stat_seen4")
        aggr = tally("aggr4")
        add = tally("add4")
        pw = tally("pow4")
        x3_ready = tally("x3_ready")
        x3_out = [tally("x3_out0", 16, 1), tally("x3_out1", 16, 1)]
        tx = tally("tx4")
        xT_ev = tally("xT4_ev", 1, 1)
        lg = tally("lg4", 1, 1)
        nm = tally("nm4")
        ex_done = tally("ex_done", 1, 1)
        step = tally("step4", STEPS)
        seen = tally("seen4")
        mask_ready = tally("mask_ready")
        pos_ps = tally("pos_ps")
        counted = tally("counted", 1, 1)
        picked = tally("picked", 4)
        dest_ready = tally("dest_ready", 1, 1)
        sent = [tally("sent0", 16 * TOPK), tally("sent1", 16 * TOPK)]
        plan_step = tally("plan_step")
        plan_ps = tally("plan_ps")
        plan_out = tally("plan_out")
        NCONST = 10

        block = ctx.enter_context(nc.Block())

        @block.sync
        def _(sp):
            with nc.allow_non_contiguous_dma(reason="small, once"):
                for dst, src in (
                    (w_o[:, :, :], Wo.rearrange("(k p) n -> p k n", p=P)),
                    (w_g[:, :, :], gate_wT.rearrange("(k p) n -> p k n", p=P)),
                    (idn[:, :], ident),
                    (before_sb[:, :], before),
                    (iota_sb[:, :], iota_e),
                    (entry[:, 1, :, 0], v_first),
                    (macc[:, :], base),
                    (e_base_sb[:, :], e_base),
                    (g_sb[:, :], iota_g),
                    (incl_sb[:, :, :], incl),
                ):
                    sp.dma_start(dst, src).then_inc(consts.sem, 16)

            def load(slot, rows):
                sp.dma_start(at[:, slot, :], attn[rows, :]).then_inc(in_ld[slot].sem, 16)
                sp.dma_start(x2t[:, slot, :], x2_rows[rows, :]).then_inc(in_ld[slot].sem, 16)

            for s in range(2):
                load(s, slice(s * P, (s + 1) * P))
            for o in x3_out:
                o.credit(sp)
            with sp.Fori(0, NT // 2) as i:
                ahead = [sp.snap(((2 * i + s + 2) % NT) * P) for s in range(2)]
                here = [sp.snap((2 * i + s) * P) for s in range(2)]
                for s in range(2):
                    t = 2 * i + s
                    sp.wait_ge(sum3.sem, sum3.at(t))
                    load(s, bass.ds(ahead[s], P))
                    sp.wait_ge(x3_ready.sem, x3_ready.at(t))
                    sp.dma_start(x3_rows[bass.ds(here[s], P), :], x3[:, s, :]).then_inc(x3_out[s].sem, 16)
            for s in range(2):
                sp.wait_ge(in_ld[s].sem, 32 * (NT // 2 + 1))
                sp.wait_ge(x3_out[s].sem, x3_out[s].at(NT // 2 - 1))
            sp.wait_ge(plan_step.sem, 10)
            sp.dma_start(plan, plan_sb[:, :]).then_inc(plan_out.sem, 16)
            sp.wait_ge(plan_out.sem, 16)

        @block.tensor
        def _(pe):
            def out_proj(t, s, loads, between=None):
                pe.wait_ge(in_ld[s].sem, 32 * loads)
                for g in range(2):
                    pe.wait_ge(at_ev.sem, at_ev.at(t - 1, g + 1))
                    for j in range(4):
                        b = 4 * g + j
                        last = nc.tensor.transpose(ps_t[:, g, j, :], at[:, s, b * P:(b + 1) * P], idn[:, :])
                    last.then_inc(at_tr.sem, 1)
                pe.wait_ge(at_ev.sem, at_ev.at(t))
                pe.wait_ge(sum3.sem, sum3.at(t - 1))
                for b in range(AB):
                    if b == AB // 2 and between:
                        between()
                    last = nc.tensor.matmul(ps_o[:, 0:DM], aT[:, b, :], w_o[:, b, :], start=b == 0, stop=b == AB - 1)
                last.then_inc(op_ps.sem, 1)

            def logits(t, s):
                pe.wait_ge(x3_ready.sem, x3_ready.at(t))
                for k in range(KD):
                    last = nc.tensor.transpose(ps_x[:, k, :], x3[:, s, k * P:(k + 1) * P], idn[:, :])
                last.then_inc(tx.sem, 1)
                pe.wait_ge(xT_ev.sem, xT_ev.at(t))
                pe.wait_ge(ex_done.sem, ex_done.at(t - 1))
                for k in range(KD):
                    last = nc.tensor.matmul(ps_g[:, 0:EXPERTS], xT[:, k, :], w_g[:, k, :], start=k == 0, stop=k == KD - 1)
                last.then_inc(lg.sem, 1)

            def places(t):
                pe.wait_ge(mask_ready.sem, mask_ready.at(t))
                pe.wait_ge(dest_ready.sem, dest_ready.at(t - 1))
                pe.wait_ge(counted.sem, counted.at(t - 1))
                nc.tensor.matmul(ps_p[:, 0:EXPERTS], before_sb[:, :], chosen[:, :], start=True, stop=False)
                nc.tensor.matmul(ps_p[:, 0:EXPERTS], ones[:, :], macc[:, :], start=False, stop=True).then_inc(pos_ps.sem, 1)

            pe.wait_ge(consts.sem, 16 * NCONST)
            pe.wait_ge(nh_set.sem, 3)
            out_proj(0, 0, 1)
            out_proj(1, 1, 1)
            with pe.Fori(0, NT // 2) as i:
                for s in range(2):
                    t = 2 * i + s
                    logits(t, s)
                    out_proj(t + 2, s, i + 2, lambda: places(t))
            pe.wait_ge(counted.sem, counted.at(NT - 1))
            pe.wait_ge(dest_ready.sem, dest_ready.at(NT - 1))
            pe.wait_ge(ex_done.sem, ex_done.at(NT - 1))
            nc.tensor.matmul(ps_g[0:EXPERTS, 0:1], macc[:, :], ones[:, 0:1], start=True, stop=True).then_inc(plan_ps.sem, 1)
            pe.wait_ge(plan_step.sem, 3)
            pe.wait_ge(sum3.sem, sum3.at(NT + 1))
            nc.tensor.matmul(ps_o[0:EXPERTS, 0:1], incl_sb[:, 0, :], n_f[:, :], start=True, stop=True).then_inc(plan_ps.sem, 1)
            nc.tensor.matmul(ps_g[0:1, 0:EXPERTS], n_f[:, :], incl_sb[:, 1, :], start=True, stop=True).then_inc(plan_ps.sem, 1)
            pe.wait_ge(plan_step.sem, 6)
            nc.tensor.matmul(ps_p[0:1, 0:MAXG], ones[0:EXPERTS, 0:1], past[:, :], start=True, stop=True).then_inc(plan_ps.sem, 1)
            nc.tensor.matmul(ps_o[0:1, 0:MAXG], n_f[:, :], past[:, :], start=True, stop=True).then_inc(plan_ps.sem, 1)

        @block.scalar
        def _(act):
            def take_attn(t):
                act.wait_ge(op_ps.sem, op_ps.at(t - 1))
                for g in range(2):
                    act.wait_ge(at_tr.sem, at_tr.at(t, g + 1))
                    nc.scalar.activation(aT[:, 4 * g:4 * g + 4, :], ps_t[:, g, :, :], ACT.Copy).then_inc(at_ev.sem, 1)

            at_ev.credit(act)
            op_ps.credit(act)
            xT_ev.credit(act)
            lg.credit(act)
            ex_done.credit(act)
            take_attn(0)
            take_attn(1)
            with act.Fori(0, NT // 2) as i:
                for s in range(2):
                    t = 2 * i + s
                    act.wait_ge(tx.sem, tx.at(t))
                    act.wait_ge(lg.sem, lg.at(t - 1))
                    nc.scalar.activation(xT[:, :, :], ps_x[:, 0:KD, :], ACT.Copy).then_inc(xT_ev.sem, 1)
                    act.wait_ge(nm.sem, nm.at(t))
                    nc.scalar.activation(ex[:, :], ps_g[:, 0:EXPERTS], ACT.Exp, bias=negm[:, :],
                                         accum_out=esum[:, :]).then_inc(ex_done.sem, 1)
                    take_attn(t + 2)

        @block.gpsimd
        def _(pool):
            def inv_std(t):
                pool.wait_ge(aggr.sem, aggr.at(t))
                nc.gpsimd.tensor_tensor(rstd[:, :], mv[:, 1:2], eps_sb[:, :], ALU.add).then_inc(add.sem, 1)
                pool.wait_ge(add.sem, add.at(t))
                nc.gpsimd.tensor_tensor(rstd[:, :], rstd[:, :], nhalf[:, :], ALU.pow).then_inc(pw.sem, 1)

            nc.gpsimd.memset(nhalf[:, :], -0.5).then_inc(nh_set.sem, 1)
            nc.gpsimd.memset(eps_sb[:, :], EPS).then_inc(nh_set.sem, 1)
            nc.gpsimd.memset(ones[:, :], 1.0).then_inc(nh_set.sem, 1)
            for s in range(2):
                half = slice(s * P // 2, (s + 1) * P // 2)
                pool.dma_start(table.rearrange("(p c) n -> p (c n)", p=P)[half, :], no_place[half, :]).then_inc(sent[s].sem, 16)
            for s in range(2):
                pool.wait_ge(sent[s].sem, 16)
            pool.wait_ge(nh_set.sem, 3)
            pool.wait_ge(consts.sem, 16 * NCONST)
            inv_std(0)
            inv_std(1)
            with pool.Fori(0, NT // 2) as i:
                for s in range(2):
                    t = 2 * i + s
                    pool.wait_ge(dest_ready.sem, dest_ready.at(t))
                    pool.sem_inc(seen.sem)
                    for k in range(TOPK):
                        pool.indirect_dma_start(out=table, out_offset=bass.IndirectOffsetOnAxis(ap=dest[:, s, k:k + 1], axis=0),
                                                in_=entry[:, s, k, :], in_offset=None).then_inc(sent[s].sem, 16)
                        if k == 0:
                            inv_std(t + 2)
            for s in range(2):
                pool.wait_ge(sent[s].sem, 16 + sent[s].at(NT // 2 - 1))

        @block.vector
        def _(dve):
            def moments(t, s, first=False):
                dve.wait_ge(op_ps.sem, op_ps.at(t))
                if not first:
                    dve.wait_ge(x3_ready.sem, x3_ready.at(t - 1))
                nc.vector.tensor_tensor(r3[:, :], ps_o[:, 0:DM], x2t[:, s, :], ALU.add).then_inc(sum3.sem, 1)
                dve.wait_ge(sum3.sem, sum3.at(t))
                nc.vector.bn_stats(stats[:, :], r3[:, :]).then_inc(stat.sem, 1)
                dve.wait_ge(stat.sem, stat.at(t))
                dve.sem_inc(stat_seen.sem)
                nc.vector.bn_aggr(mv[:, :], stats[:, :]).then_inc(aggr.sem, 1)

            def norm(t, s, prev):
                dve.wait_ge(pw.sem, pw.at(t))
                dve.wait_ge(x3_out[s].sem, x3_out[s].at(prev))
                nc.vector.tensor_scalar(x3[:, s, :], r3[:, :], mv[:, 0:1], rstd[:, :], ALU.subtract,
                                        ALU.mult).then_inc(x3_ready.sem, 1)

            def after(t, n):
                dve.wait_ge(step.sem, step.at(t, n))

            def choose(i, t, s):
                dve.wait_ge(lg.sem, lg.at(t))
                nc.vector.reduce_max(negm[:, :], ps_g[:, 0:EXPERTS], axis=mybir.AxisListType.X,
                                     negate=True).then_inc(nm.sem, 1)
                dve.wait_ge(ex_done.sem, ex_done.at(t))
                nc.vector.reciprocal(erec[:, :], esum[:, :]).then_inc(step.sem, 1)
                after(t, 1)
                nc.vector.tensor_scalar(sc[:, :], ex[:, :], erec[:, :], None, ALU.mult).then_inc(step.sem, 1)
                after(t, 2)
                dve.sem_inc(stat_seen.sem)
                nc.vector.max(top[:, :], sc[:, :]).then_inc(step.sem, 1)
                after(t, 3)
                dve.sem_inc(stat_seen.sem)
                nc.vector.match_replace(rest[:, :], top[:, :], sc[:, :], -1.0).then_inc(step.sem, 1)
                nc.vector.max_index(idx[:, :], top[:, :], sc[:, :]).then_inc(step.sem, 1)
                after(t, 4)
                nc.vector.tensor_scalar(chosen[:, :], rest[:, :], -1.0, None, ALU.is_equal).then_inc(mask_ready.sem, 1)
                nc.vector.reduce_sum(tsum[:, :], top[:, :], axis=mybir.AxisListType.X).then_inc(step.sem, 1)
                after(t, 6)
                nc.vector.tensor_scalar(tsum[:, :], tsum[:, :], 1e-20, None, ALU.add).then_inc(step.sem, 1)
                after(t, 7)
                nc.vector.reciprocal(tsum[:, :], tsum[:, :]).then_inc(step.sem, 1)
                nc.vector.tensor_copy(idx_f[:, :], idx[:, :])
                dve.wait_ge(sent[s].sem, 16 + 16 * TOPK * i)
                nc.vector.tensor_scalar(entry[:, s, :, 0], entry[:, 1 - s, :, 0], float(P * TOPK), None, ALU.add)
                after(t, 8)
                nc.vector.tensor_scalar(entry[:, s, :, 1], top[:, :], tsum[:, :], None, ALU.mult).then_inc(step.sem, 1)

            def send(t, s):
                dve.wait_ge(step.sem, step.at(t))
                dve.wait_ge(pos_ps.sem, pos_ps.at(t))
                for k in range(TOPK):
                    ins = nc.vector.scalar_tensor_tensor(junk[:, k, :], iota_sb[:, :], idx_f[:, k:k + 1],
                                                         ps_p[:, 0:EXPERTS], ALU.is_equal, ALU.mult,
                                                         accum_out=dest_f[:, k:k + 1])
                ins.then_inc(picked.sem, 1)
                dve.wait_ge(picked.sem, picked.at(t, 1))
                nc.vector.tensor_copy(dest_i[:, :], dest_f[:, :]).then_inc(picked.sem, 1)
                dve.wait_ge(picked.sem, picked.at(t, 2))
                nc.vector.tensor_scalar(col[:, :], dest_i[:, :], 7, None, ALU.arith_shift_right).then_inc(picked.sem, 1)
                nc.vector.tensor_scalar(dest_i[:, :], dest_i[:, :], P - 1, None, ALU.bitwise_and).then_inc(picked.sem, 1)
                dve.wait_ge(picked.sem, picked.at(t, 4))
                nc.vector.scalar_tensor_tensor(dest[:, s, :], dest_i[:, :], float(COLS), col[:, :], ALU.mult,
                                               ALU.add).then_inc(dest_ready.sem, 1)
                nc.vector.tensor_tensor(macc[:, :], macc[:, :], chosen[:, :], ALU.add).then_inc(counted.sem, 1)

            sum3.credit(dve)
            counted.credit(dve)
            dest_ready.credit(dve)
            dve.wait_ge(consts.sem, 16 * NCONST)
            moments(0, 0, True)
            norm(0, 0, -1)
            moments(1, 1)
            with dve.Fori(0, NT // 2) as i:
                for s in range(2):
                    t = 2 * i + s
                    choose(i, t, s)
                    send(t, s)
                    norm(t + 1, 1 - s, i - 1 + s)
                    moments(t + 2, s)

            def plan_after(n):
                dve.wait_ge(plan_step.sem, n)

            dve.wait_ge(plan_ps.sem, 1)
            nc.vector.tensor_scalar(n_i[:, :], ps_g[0:EXPERTS, 0:1], e_base_sb[:, :], None, ALU.subtract).then_inc(plan_step.sem, 1)
            plan_after(1)
            nc.vector.tensor_scalar(n_i[:, :], n_i[:, :], 7, None, ALU.arith_shift_right).then_inc(plan_step.sem, 1)
            plan_after(2)
            nc.vector.tensor_scalar(n_f[:, :], n_i[:, :], 1.0, None, ALU.max).then_inc(plan_step.sem, 1)
            dve.wait_ge(plan_ps.sem, 3)
            nc.vector.tensor_copy(ends[:, :], ps_o[0:EXPERTS, 0:1]).then_inc(plan_step.sem, 1)
            plan_after(4)
            nc.vector.tensor_scalar(past[:, :], g_sb[:, :], ends[:, :], None, ALU.is_ge).then_inc(plan_step.sem, 1)
            nc.vector.tensor_copy(plan_sb[:, 2 * MAXG:2 * MAXG + EXPERTS], ps_g[0:1, 0:EXPERTS]).then_inc(plan_step.sem, 1)
            dve.wait_ge(plan_ps.sem, 5)
            nc.vector.tensor_scalar(plan_sb[:, 0:MAXG], ps_p[0:1, 0:MAXG], float(EXPERTS - 1), None, ALU.min).then_inc(plan_step.sem, 1)
            nc.vector.tensor_tensor(first_f[:, :], g_sb[0:1, :], ps_o[0:1, 0:MAXG], ALU.subtract)
            nc.vector.tensor_copy(plan_sb[:, 2 * MAXG + EXPERTS:], ps_o[0:1, MAXG - 1:MAXG]).then_inc(plan_step.sem, 1)
            plan_after(8)
            nc.vector.scalar_tensor_tensor(first_f[:, :], ps_p[0:1, 0:MAXG], float(NT), first_f[:, :], ALU.mult,
                                           ALU.add).then_inc(plan_step.sem, 1)
            plan_after(9)
            nc.vector.tensor_scalar(plan_sb[:, MAXG:2 * MAXG], first_f[:, :], float(COLS - 1), None,
                                    ALU.min).then_inc(plan_step.sem, 1)
    nc.clear_and_free_semaphores(sems)
    nc.all_engine_barrier()


def experts(nc, table, plan, x3_rows, W_guT, W_downT, ident, y8):
    H2 = FF // 2
    WSLOTS = 4

    sems = []
    with ExitStack() as ctx:
        def sb(name, shape, dt=F32):
            return ctx.enter_context(nc.sbuf_tensor(name, shape, dt))

        def pb(name, shape):
            return ctx.enter_context(nc.psum_tensor(name, shape, F32))

        def tally(name, per=1, ahead=0):
            sems.append(nc.alloc_semaphore(name))
            return Tally(sems[-1], per, ahead)

        idn = sb("idn5", [P, P])
        entries = sb("entries", [P, COLS, 2])
        token_all = sb("token_all", [P, COLS, 1], I32)
        place_all = sb("place_all", [P, COLS, 1], I32)
        token = sb("token", [P, 2, 1], I32)
        place = sb("place", [P, 2, 1], I32)
        weight = sb("weight", [P, 2, 1])
        plan_sb = sb("plan5", [1, 2 * MAXG + EXPERTS + 1], I32)
        pairs_sb = sb("pairs5", [1, 1], I32)
        w_gu = sb("w_gu", [P, WSLOTS, KD, 2 * FF])
        w_d = sb("w_d", [H2, WSLOTS, 2, DM])
        xr = sb("xr", [P, 2, DM])
        xT = sb("xT5", [P, 2, KD, P])
        sg = sb("sg", [P, 2, FF])
        hid = sb("hid", [P, 2, FF])
        hT = sb("hT", [H2, 2, 2, P])
        y_sb = sb("y5", [P, 2, DM])
        ps_x = pb("ps_x5", [P, 2, 4, P])
        ps_gu = pb("ps_gu", [P, 2, 512])
        ps_h = pb("ps_h", [P, 2, 4, P])
        ps_y = pb("ps_y5", [P, 2, 512])

        consts = tally("consts5")
        pairs_step = tally("pairs_step")
        w_ld = [tally("w_ld%d" % q, 32, 1) for q in range(WSLOTS)]
        w_ready = tally("w_ready")
        x_ld = [tally("x5_ld0", 16), tally("x5_ld1", 16)]
        tx = tally("tx5")
        xT_ev = tally("xT5_ev")
        gu = tally("gu")
        gate = tally("gate")
        hid_ready = tally("hid_ready")
        th = tally("th")
        hT_ev = tally("hT_ev")
        down = tally("down", 1, 2)
        listed = tally("listed")
        token_ready = tally("token_ready")
        token_seen = tally("token_seen")
        weighed = tally("weighed")
        y_ready = tally("y5_ready", 1, 2)
        y_seen = tally("y5_seen")
        y_out = [tally("y5_out0", 16), tally("y5_out1", 16)]
        NCONST = 2

        def planned(row, g):
            return plan_sb[0:1, bass.ds(row * MAXG + g, 1)]

        def pair_count(eng):
            eng.wait_ge(pairs_step.sem, 2)
            return eng.value_load(pairs_sb[0:1, 0:1], min_val=1, max_val=MAXG // 2)

        block = ctx.enter_context(nc.Block())

        @block.sync
        def _(sp):
            def weights(slot, e):
                sp.dma_start(w_gu[:, slot, :, :], W_guT[bass.ds(e, 1)].rearrange("o (k p) n -> p (o k) n", p=P)
                             ).then_inc(w_ld[slot].sem, 16)
                sp.dma_start(w_d[:, slot, :, :], W_downT[bass.ds(e, 1)].rearrange("o (k p) n -> p (o k) n", p=H2)
                             ).then_inc(w_ld[slot].sem, 16)

            def arrived(q, load):
                sp.wait_ge(w_ld[q].sem, w_ld[q].at(load))
                sp.sem_inc(w_ready.sem)

            sp.dma_start(plan_sb[:, :], plan).then_inc(consts.sem, 16)
            sp.dma_start(idn[:, :], ident).then_inc(consts.sem, 16)
            for w in w_ld:
                w.credit(sp)
            for q in range(WSLOTS):
                weights(q, q)
            for q in range(WSLOTS - 1):
                arrived(q, 0)
            sp.wait_ge(consts.sem, 16 * NCONST)
            with sp.Fori(1, EXPERTS // WSLOTS) as j:
                for q in range(WSLOTS):
                    e = sp.snap(WSLOTS * j + q)
                    start = sp.value_load(plan_sb[0:1, bass.ds(2 * MAXG + WSLOTS * (j - 1) + q + 1, 1)], min_val=1, max_val=MAXG)
                    sp.wait_ge(down.sem, start + down.ahead)
                    weights(q, e)
                    arrived((q - 1) % WSLOTS, j if q else j - 1)
            arrived(WSLOTS - 1, EXPERTS // WSLOTS - 1)

        @block.tensor
        def _(pe):
            def expert(g):
                return pe.value_load(planned(0, g), min_val=0, max_val=EXPERTS - 1)

            def turn_x(g, s, loads):
                pe.wait_ge(x_ld[s].sem, 16 * loads)
                for k in range(KD):
                    last = nc.tensor.transpose(ps_x[:, s, k, :], xr[:, s, k * P:(k + 1) * P], idn[:, :])
                last.then_inc(tx.sem, 1)

            def gate_up(g, s, e):
                pe.wait_ge(w_ready.sem, e + 1)
                pe.wait_ge(xT_ev.sem, xT_ev.at(g))
                for k in range(KD):
                    last = nc.tensor.matmul(ps_gu[:, s, 0:2 * FF], xT[:, s, k, :], w_gu[:, bass.ds(e % WSLOTS, 1), k, :],
                                            start=k == 0, stop=k == KD - 1)
                last.then_inc(gu.sem, 1)

            def turn_h(g, s):
                pe.wait_ge(hid_ready.sem, hid_ready.at(g))
                for b in range(2):
                    last = nc.tensor.transpose(ps_h[0:H2, s, b, :], hid[:, s, b * H2:(b + 1) * H2], idn[:, :])
                last.then_inc(th.sem, 1)

            def output(g, s, e):
                pe.wait_ge(hT_ev.sem, hT_ev.at(g))
                pe.wait_ge(y_ready.sem, y_ready.at(g - 2))
                for b in range(2):
                    last = nc.tensor.matmul(ps_y[:, s, 0:DM], hT[:, s, b, :], w_d[:, bass.ds(e % WSLOTS, 1), b, :],
                                            start=b == 0, stop=b == 1)
                last.then_inc(down.sem, 1)

            pe.wait_ge(consts.sem, 16 * NCONST)
            pairs = pair_count(pe)
            down.credit(pe)
            turn_x(0, 0, 1)
            turn_x(1, 1, 1)
            for s in range(2):
                gate_up(s, s, expert(s))
            with pe.Fori(0, pairs) as i:
                here = [expert(2 * i + s) for s in range(2)]
                ahead = [expert(2 * i + 2 + s) for s in range(2)]
                for s in range(2):
                    turn_x(2 * i + 2 + s, s, i + 2)
                    turn_h(2 * i + s, s)
                gate_up(2 * i + 2, 0, ahead[0])
                output(2 * i, 0, here[0])
                gate_up(2 * i + 3, 1, ahead[1])
                output(2 * i + 1, 1, here[1])

        @block.scalar
        def _(act):
            def take_x(g, s):
                act.wait_ge(tx.sem, tx.at(g))
                nc.scalar.activation(xT[:, s, :, :], ps_x[:, s, 0:KD, :], ACT.Copy).then_inc(xT_ev.sem, 1)

            def take_h(g, s):
                act.wait_ge(th.sem, th.at(g))
                act.wait_ge(down.sem, down.at(g - 2))
                nc.scalar.activation(hT[:, s, :, :], ps_h[0:H2, s, 0:2, :], ACT.Copy).then_inc(hT_ev.sem, 1)

            act.wait_ge(consts.sem, 16 * NCONST)
            def silu(g, s):
                act.wait_ge(gu.sem, gu.at(g))
                nc.scalar.activation(sg[:, s, :], ps_gu[:, s, 0:FF], ACT.Silu).then_inc(gate.sem, 1)

            pairs = pair_count(act)
            for s in range(2):
                take_x(s, s)
            for s in range(2):
                silu(s, s)
            with act.Fori(0, pairs) as i:
                for s in range(2):
                    take_x(2 * i + 2 + s, s)
                    take_h(2 * i + s, s)
                for s in range(2):
                    silu(2 * i + 2 + s, s)

        @block.gpsimd
        def _(pool):
            def gather(g, s, turned=True):
                pool.wait_ge(token_ready.sem, token_ready.at(g))
                if turned:
                    pool.wait_ge(tx.sem, tx.at(g - 2))
                pool.sem_inc(token_seen.sem)
                pool.indirect_dma_start(out=xr[:, s, :], out_offset=None, in_=x3_rows,
                                        in_offset=bass.IndirectOffsetOnAxis(ap=token[:, s, :], axis=0)
                                        ).then_inc(x_ld[s].sem, 16)

            for s in range(2):
                half = slice(s * P // 2, (s + 1) * P // 2)
                pool.dma_start(entries[half, :, :], table.rearrange("(p c) n -> p c n", p=P)[half, :, :]).then_inc(y_out[s].sem, 16)
            y_ready.credit(pool)
            pool.wait_ge(consts.sem, 16 * NCONST)
            pairs = pair_count(pool)
            for g in range(4):
                gather(g, g % 2, g >= 2)
            with pool.Fori(0, pairs) as i:
                for s in range(2):
                    gather(2 * i + 4 + s, s)
                for s in range(2):
                    pool.wait_ge(y_ready.sem, y_ready.at(2 * i + s))
                    pool.sem_inc(y_seen.sem)
                    pool.indirect_dma_start(out=y8, out_offset=bass.IndirectOffsetOnAxis(ap=place[:, s, :], axis=0),
                                            in_=y_sb[:, s, :], in_offset=None).then_inc(y_out[s].sem, 16)
            for s in range(2):
                pool.wait_ge(y_out[s].sem, 16 * (pairs + 1))
                pool.sem_inc(y_seen.sem)
                pool.wait_ge(x_ld[s].sem, 16 * (pairs + 2))
                pool.sem_inc(token_seen.sem)

        @block.vector
        def _(dve):
            def tokens(g, s, loads):
                c = dve.value_load(planned(1, g), min_val=0, max_val=COLS - 1)
                if loads is not None:
                    dve.wait_ge(x_ld[s].sem, 16 * loads)
                nc.vector.tensor_copy(token[:, s, :], token_all[:, bass.ds(c, 1), :]).then_inc(token_ready.sem, 1)

            def unit(g, s):
                dve.wait_ge(gate.sem, gate.at(g))
                nc.vector.tensor_tensor(hid[:, s, :], ps_gu[:, s, FF:2 * FF], sg[:, s, :], ALU.mult).then_inc(hid_ready.sem, 1)

            def scale(i, g, s):
                c = dve.value_load(planned(1, g), min_val=0, max_val=COLS - 1)
                dve.wait_ge(y_out[s].sem, 16 * (i + 1))
                dve.wait_ge(y_ready.sem, y_ready.at(g - 2))
                nc.vector.tensor_copy(place[:, s, :], place_all[:, bass.ds(c, 1), :])
                nc.vector.tensor_copy(weight[:, s, :], entries[:, bass.ds(c, 1), 1:2]).then_inc(weighed.sem, 1)
                dve.wait_ge(weighed.sem, weighed.at(g))
                dve.wait_ge(down.sem, down.at(g))
                nc.vector.tensor_scalar(y_sb[:, s, :], ps_y[:, s, 0:DM], weight[:, s, :], None, ALU.mult).then_inc(y_ready.sem, 1)

            dve.wait_ge(consts.sem, 16 * NCONST)
            nc.vector.tensor_scalar(pairs_sb[:, :], plan_sb[:, 2 * MAXG + EXPERTS:], 1, None, ALU.add).then_inc(pairs_step.sem, 1)
            dve.wait_ge(pairs_step.sem, 1)
            nc.vector.tensor_scalar(pairs_sb[:, :], pairs_sb[:, :], 1, None, ALU.arith_shift_right).then_inc(pairs_step.sem, 1)
            pairs = pair_count(dve)
            for s in range(2):
                dve.wait_ge(y_out[s].sem, 16)
            nc.vector.tensor_copy(place_all[:, :, :], entries[:, :, 0:1]).then_inc(listed.sem, 1)
            dve.wait_ge(listed.sem, 1)
            nc.vector.tensor_scalar(token_all[:, :, :], place_all[:, :, :], 3, None, ALU.arith_shift_right).then_inc(listed.sem, 1)
            dve.wait_ge(listed.sem, 2)
            nc.vector.tensor_scalar(token_all[:, :, :], token_all[:, :, :], TOKENS - 1, None, ALU.min).then_inc(listed.sem, 1)
            dve.wait_ge(listed.sem, 3)
            for g in range(4):
                tokens(g, g % 2, 1 if g >= 2 else None)
            for s in range(2):
                unit(s, s)
            with dve.Fori(0, pairs) as i:
                for s in range(2):
                    tokens(2 * i + 4 + s, s, i + 2)
                for s in range(2):
                    unit(2 * i + 2 + s, s)
                    scale(i, 2 * i + s, s)
    nc.clear_and_free_semaphores(sems)
    nc.all_engine_barrier()


def combine(nc, y8, x3_rows, out):
    y_view = y8[0:VMAX, :].rearrange("(t k) d -> t k d", k=TOPK)

    sems = []
    with ExitStack() as ctx:
        def sb(name, shape, dt=F32):
            return ctx.enter_context(nc.sbuf_tensor(name, shape, dt))

        def tally(name, per=1, ahead=0):
            sems.append(nc.alloc_semaphore(name))
            return Tally(sems[-1], per, ahead)

        yk = sb("yk", [P, 2, TOPK, DM])
        x3 = sb("x3_6", [P, 2, DM])
        r4 = sb("r4", [P, 2, DM])
        o_sb = sb("o_sb", [P, 2, DM])
        stats = sb("stats6", [P, 6])
        mv = sb("mv6", [P, 2])
        rstd = sb("rstd6", [P, 1])
        nhalf = sb("nhalf6", [P, 1])
        eps_sb = sb("eps6", [P, 1])

        nh_set = tally("nh_set6")
        in_ld = [tally("in6_ld0", 32), tally("in6_ld1", 32)]
        ksum = tally("ksum")
        sum4 = tally("sum4")
        stat = tally("stat6")
        stat_seen = tally("stat_seen6")
        aggr = tally("aggr6")
        add = tally("add6")
        pw = tally("pow6")
        o_ready = tally("o_ready")
        o_out = [tally("o6_out0", 16, 1), tally("o6_out1", 16, 1)]

        block = ctx.enter_context(nc.Block())

        @block.sync
        def _(sp):
            def load(slot, rows):
                sp.dma_start(yk[:, slot, :, :], y_view[rows, :, :]).then_inc(in_ld[slot].sem, 16)
                sp.dma_start(x3[:, slot, :], x3_rows[rows, :]).then_inc(in_ld[slot].sem, 16)

            for s in range(2):
                load(s, slice(s * P, (s + 1) * P))
            for o in o_out:
                o.credit(sp)
            with sp.Fori(0, NT // 2) as i:
                ahead = [sp.snap(((2 * i + s + 2) % NT) * P) for s in range(2)]
                here = [sp.snap((2 * i + s) * P) for s in range(2)]
                for s in range(2):
                    t = 2 * i + s
                    sp.wait_ge(sum4.sem, sum4.at(t))
                    load(s, bass.ds(ahead[s], P))
                    sp.wait_ge(o_ready.sem, o_ready.at(t))
                    sp.dma_start(out[bass.ds(here[s], P), :], o_sb[:, s, :]).then_inc(o_out[s].sem, 16)
            for s in range(2):
                sp.wait_ge(in_ld[s].sem, 32 * (NT // 2 + 1))
                sp.wait_ge(o_out[s].sem, o_out[s].at(NT // 2 - 1))

        @block.gpsimd
        def _(pool):
            nc.gpsimd.memset(nhalf[:, :], -0.5).then_inc(nh_set.sem, 1)
            nc.gpsimd.memset(eps_sb[:, :], EPS).then_inc(nh_set.sem, 1)
            pool.wait_ge(nh_set.sem, 2)
            with pool.Fori(0, NT) as t:
                pool.wait_ge(aggr.sem, aggr.at(t))
                nc.gpsimd.tensor_tensor(rstd[:, :], mv[:, 1:2], eps_sb[:, :], ALU.add).then_inc(add.sem, 1)
                pool.wait_ge(add.sem, add.at(t))
                nc.gpsimd.tensor_tensor(rstd[:, :], rstd[:, :], nhalf[:, :], ALU.pow).then_inc(pw.sem, 1)

        @block.vector
        def _(dve):
            def total(s, t, loads):
                dve.wait_ge(in_ld[s].sem, 32 * loads)
                nc.vector.reduce_sum(r4[:, s, :], yk[:, s, :, :].rearrange("p k d -> p d k"),
                                     axis=mybir.AxisListType.X).then_inc(ksum.sem, 1)

            total(0, 0, 1)
            with dve.Fori(0, NT // 2) as i:
                for s in range(2):
                    t = 2 * i + s
                    dve.wait_ge(ksum.sem, ksum.at(t))
                    nc.vector.tensor_tensor(r4[:, s, :], r4[:, s, :], x3[:, s, :], ALU.add).then_inc(sum4.sem, 1)
                    dve.wait_ge(sum4.sem, sum4.at(t))
                    nc.vector.bn_stats(stats[:, :], r4[:, s, :]).then_inc(stat.sem, 1)
                    dve.wait_ge(stat.sem, stat.at(t))
                    dve.sem_inc(stat_seen.sem)
                    nc.vector.bn_aggr(mv[:, :], stats[:, :]).then_inc(aggr.sem, 1)
                    total(1 - s, t + 1, i + 1 + s)
                    dve.wait_ge(pw.sem, pw.at(t))
                    dve.wait_ge(o_out[s].sem, o_out[s].at(i - 1))
                    nc.vector.tensor_scalar(o_sb[:, s, :], r4[:, s, :], mv[:, 0:1], rstd[:, :], ALU.subtract,
                                            ALU.mult).then_inc(o_ready.sem, 1)
    nc.clear_and_free_semaphores(sems)
    nc.all_engine_barrier()


def layers(nc, x_T, x_rows, W_inT, conv_w, W_xprojT, W_dtT, b_dt, A_log, D_skip, W_outT, F_inT, F_bias, F_outT, Wqk, Wv,
           Wo, gate_wT, W_guT, W_downT, sel_bc, keep, ident, rope_q, rope_k, causal, before, iota_e, v_first, base, e_base,
           iota_g, incl, no_place, out):
    def scratch(name, shape, dt=F32):
        return nc.dram_tensor(name, shape, dt).ap()

    y_scr = scratch("y_scr", (512, TOKENS))
    x2_rows = scratch("x2_rows", (TOKENS, DM))
    x2_T = scratch("x2_T", (DM, TOKENS))
    q_scr = scratch("q_scr", (BATCH * HEADS, HD, LENGTH))
    k_scr = scratch("k_scr", (BATCH * KV, HD, LENGTH))
    v_scr = scratch("v_scr", (TOKENS, KV * (HD + 1)))
    attn = scratch("attn", (TOKENS, HEADS * HD))
    x3_rows = scratch("x3_rows", (TOKENS, DM))
    table = scratch("table", (P * COLS, 2))
    plan = scratch("plan", (1, 2 * MAXG + EXPERTS + 1), I32)
    y8 = scratch("y8", (VMAX + 2 * P, DM))

    mamba(nc, x_T, W_inT, conv_w, W_xprojT, W_dtT, b_dt, A_log, D_skip, sel_bc, keep, ident, y_scr)
    tree_ffn(nc, y_scr, x_rows, W_outT, F_inT, F_bias, F_outT, ident, x2_rows, x2_T)
    qkv(nc, x2_T, Wqk, Wv, rope_q, rope_k, q_scr, k_scr, v_scr)
    attention(nc, q_scr, k_scr, v_scr, ident, causal, attn)
    route(nc, attn, x2_rows, Wo, gate_wT, ident, before, iota_e, v_first, base, e_base, iota_g, incl, no_place,
          x3_rows, table, plan)
    experts(nc, table, plan, x3_rows, W_guT, W_downT, ident, y8)
    combine(nc, y8, x3_rows, out)


def constants():
    import numpy as np
    f = np.float32
    i, e, k = np.arange(P), np.arange(EXPERTS), np.arange(TOPK)
    RANK, NST = 16, 16
    n = np.arange(2 * NST)
    sel = np.zeros((64 + RANK + 2 * NST, 2 * NST, P), f)
    sel[RANK + n, n, :] = 1
    sel[64 + RANK + n, n, :] = 1
    keep = np.ones((P, 4), f)
    keep[:, 1::2] = 0
    inv = f(1) / np.power(f(10000), np.arange(0, HD, 2, dtype=f) / f(HD))
    freqs = np.arange(LENGTH, dtype=f)[:, None] * inv[None, :]
    emb = np.concatenate([freqs, freqs], -1)
    cos, sin = np.cos(emb)[:, 0::2].T, np.sin(emb)[:, 0::2].T
    rope = np.tile(np.stack([cos, sin, -sin, cos], 1).astype(f), (GROUP, 1, 1))
    base = np.zeros((P, EXPERTS), f)
    base[0] = e * TOKENS
    no_place = np.zeros((P, COLS, 2), f)
    no_place[:, :, 0] = VMAX + P * (np.arange(COLS) // NT % 2)[None, :] + i[:, None]
    return dict(
        sel_bc=sel, keep=keep, ident=np.eye(P, dtype=f), rope_q=rope * f(HD ** -0.5), rope_k=rope,
        causal=np.triu(np.full((P, P), -2.0 ** 100, f), 1), before=(i[:, None] < i[None, :]).astype(f),
        iota_e=np.tile(e.astype(f), (P, 1)), v_first=(i[:, None] * TOPK + k[None, :] - P * TOPK).astype(f), base=base,
        e_base=(e * TOKENS - (P - 1)).astype(f)[:, None], iota_g=np.tile(np.arange(MAXG, dtype=f), (EXPERTS, 1)),
        incl=np.stack([e[:, None] <= e[None, :], e[:, None] < e[None, :]], 1).astype(f), no_place=no_place.reshape(P, 2 * COLS))


def kernel(**inputs):
    import numpy as np
    import concourse.bacc as bacc
    from concourse.bass_utils import run_bass_kernel_spmd

    def a(name):
        return np.asarray(inputs[name])

    def heads(w, n):
        return w.reshape(DM, n, GROUP, HD // 2, 2).transpose(0, 1, 4, 2, 3).reshape(DM, 2 * n, P)

    x = a("L0_attn_x").reshape(TOKENS, DM)
    given = dict(
        x_T=x.T, x_rows=x, W_inT=a("L0_attn_W_in").T, conv_w=a("L0_attn_W_conv").reshape(512, 4),
        W_xprojT=a("L0_attn_W_xproj").T, W_dtT=a("L0_attn_W_dt").T, b_dt=a("L0_attn_b_dt"), A_log=a("L0_attn_A_log"),
        D_skip=a("L0_attn_D"), W_outT=a("L0_attn_W_out").T, F_inT=a("L0_ffn_W_in").T, F_bias=a("L0_ffn_b_in"),
        F_outT=a("L0_ffn_W_out").T,
        Wqk=np.concatenate([heads(a("L1_attn_Wq"), HEADS // GROUP), heads(a("L1_attn_Wk"), KV // GROUP)], 1),
        Wv=a("L1_attn_Wv"), Wo=a("L1_attn_Wo"), gate_wT=a("L1_ffn_gate_w").T,
        W_guT=np.concatenate([a("L1_ffn_w_gate").transpose(0, 2, 1), a("L1_ffn_w_up").transpose(0, 2, 1)], 2),
        W_downT=a("L1_ffn_w_down").transpose(0, 2, 1))
    nc = bacc.Bacc("TRN2", target_bir_lowering=False, num_devices=1)
    arrays, args = {}, {}
    for name, value in {**given, **constants()}.items():
        arrays[name] = np.ascontiguousarray(value)
        args[name] = nc.dram_tensor(name, arrays[name].shape, mybir.dt.from_np(arrays[name].dtype), kind="ExternalInput").ap()
    out = nc.dram_tensor("out", (TOKENS, DM), F32, kind="ExternalOutput").ap()
    layers(nc, out=out, **args)
    r = run_bass_kernel_spmd(nc, [arrays], core_ids=[0])
    return r.results[0]["out"].reshape(BATCH, LENGTH, DM)
```

```python
from contextlib import ExitStack

import concourse.bass as bass
from concourse import mybir
from concourse.alu_op_type import AluOpType as ALU

ACT = mybir.ActivationFunctionType
F32 = mybir.dt.float32
F32R = mybir.dt.float32r
P = 128
BATCH, LENGTH, DM = 2, 2048, 256
TOKENS = BATCH * LENGTH
KD = DM // P


class Tally:

    def __init__(self, sem, per=1, ahead=0):
        self.sem, self.per, self.ahead = sem, per, ahead

    def credit(self, eng):
        eng.sem_inc(self.sem, self.ahead * self.per)

    def at(self, rnd, k=None):
        return (rnd + self.ahead) * self.per + (self.per if k is None else k)


def mamba(nc, x_T, W_inT, conv_w, W_xprojT, W_dtT, b_dt, A_log, D_skip, sel_bc, keep, ident, y_scr):
    DI, NST, RANK, TAPS = 512, 16, 16, 4
    DB = DI // P
    TC = 512
    CHUNKS = TOKENS // TC
    NBC = RANK + 2 * NST
    ON_POOL = 2
    LOW = 64
    PARTS = LOW + NBC
    FRONT = 2 * DB + 1
    IN, XP, USES = 2 * DB, 2 * DB, 2 * DB + 1 + DB
    y_out_view = y_scr.rearrange("(d p) t -> p d t", p=P)
    xT_view = x_T.rearrange("(k p) t -> p k t", p=P)

    sems = []
    with ExitStack() as ctx:
        def sb(name, shape, dt=F32):
            return ctx.enter_context(nc.sbuf_tensor(name, shape, dt))

        def pb(name, shape):
            return ctx.enter_context(nc.psum_tensor(name, shape, F32))

        def tally(name, per=1, ahead=0):
            sems.append(nc.alloc_semaphore(name))
            return Tally(sems[-1], per, ahead)

        w_in = sb("w_in", [P, KD, 2 * DI])
        w_xp = sb("w_xp", [P, DB, PARTS])
        w_dt = sb("w_dt", [RANK, DI])
        taps = sb("taps", [P, DB, TAPS])
        dt_bias = sb("dt_bias", [P, DB])
        a_log = sb("a_log", [P, DB, NST])
        neg_a = sb("neg_a", [P, DB, NST])
        d_skip = sb("d_skip", [P, DB])
        sel = sb("sel", [PARTS, 2 * NST, P], F32R)
        idn = sb("idn1", [P, P])
        skip = sb("skip", [P, DB, P])
        keep_sb = sb("keep_sb", [P, CHUNKS // 2])
        xt = sb("xt", [P, 2, KD, TC])
        xraw = sb("xraw", [P, DB, TC + TAPS - 1])
        tapped = sb("tapped", [P, 2, TAPS - 1, TC])
        xc = sb("xc", [P, 2, DB, TC])
        sz = sb("sz", [P, 2, DB, TC])
        dbc = sb("dbc", [PARTS, 2, TC], F32R)
        dt_in = sb("dt_in", [RANK, 2, TC])
        sp = sb("sp", [P, DB, TC])
        delta = sb("delta", [P, 2, DB, TC])
        u = sb("u", [P, 2, DB, TC])
        dA = sb("dA", [P, 2, DB, TC])
        dBx = sb("dBx", [P, 2, DB, TC])
        h = sb("h", [P, DB, TC])
        hc = sb("hc", [P, 2, DB, TC])
        b_sb = sb("b_sb", [P, 2, TC])
        yg = sb("yg", [P, DB, TC])
        h_in = sb("h_in", [P, NST, DB])
        sel_in = hc[0:PARTS, :, :, :].rearrange("p s d t -> p (s d t)").rearrange("p (n q) -> p n q", q=P)
        ps_y = pb("ps_y", [P, DB, TC])
        ps_b = pb("ps_b", [P, 2, TC])
        ps_c = pb("ps_c", [P, TC])
        ps_f = pb("ps_f", [P, TC])

        front_ld = tally("front_ld", 32)
        consts = tally("consts")
        xt_ld = [tally("xt_ld0"), tally("xt_ld1")]
        sel_ready = tally("sel_ready")
        high_done = tally("high_done")
        zeroed = tally("zeroed", 3)
        nega_step = tally("nega_step", 2)
        front_ps = tally("front_ps", USES)
        front_ev = tally("front_ev", USES)
        conv_step = tally("conv_step", DB * TAPS + 1, 1)
        tap_done = tally("tap_done", DB * TAPS)
        xc_ready = tally("xc_ready")
        sz_ready = tally("sz_ready")
        sp_step = tally("sp_step", 3)
        delta_ready = tally("delta_ready", 1, 1)
        u_ready = tally("u_ready")
        b_ready = tally("b_ready", NST)
        c_ready = tally("c_ready", NST)
        dA_ready = tally("dA_ready", NST)
        b_taken = tally("b_taken", NST, 1)
        dbx_pool = tally("dbx_pool", NST, 1)
        pool_seen = tally("pool_seen1")
        dbx_done = tally("dbx_done", NST, 1)
        scan_done = tally("scan_done", NST, 1)
        carry_done = tally("carry_done", NST, 1)
        hc_done = tally("hc_done", NST, 1)
        reduce_done = tally("reduce_done", NST, 1)
        skip_ready = tally("skip_ready")
        ygated = tally("ygated", 1, 2)
        y_out = tally("y_out", 16, 1)
        CONSTS = 9

        block = ctx.enter_context(nc.Block())

        @block.sync
        def _(sp_eng):
            def load(sem, *pairs):
                for dst, src in pairs:
                    with nc.allow_non_contiguous_dma(reason="small vectors, once"):
                        sp_eng.dma_start(dst, src).then_inc(sem, 16)

            load(front_ld.sem,
                 (w_in[:, :, :], W_inT.rearrange("(k p) n -> p k n", p=P)),
                 (taps[:, :, :], conv_w.rearrange("(d p) t -> p d t", p=P)))
            load(xt_ld[0].sem, (xt[:, 0, :, :], xT_view[:, :, 0:TC]))
            load(consts.sem,
                 (a_log[:, :, :], A_log.rearrange("(d p) n -> p d n", p=P)),
                 (w_xp[:, :, 0:NBC], W_xprojT.rearrange("(d p) n -> p d n", p=P)),
                 (w_xp[:, :, LOW:], W_xprojT.rearrange("(d p) n -> p d n", p=P)),
                 (w_dt[:, :], W_dtT),
                 (dt_bias[:, :], b_dt.rearrange("(d p) -> p d", p=P)),
                 (d_skip[:, :], D_skip.rearrange("(d p) -> p d", p=P)),
                 (idn[:, :], ident),
                 (keep_sb[:, :], keep),
                 (sel_in, sel_bc))
            load(xt_ld[1].sem, (xt[:, 1, :, :], xT_view[:, :, TC:2 * TC]))
            y_out.credit(sp_eng)
            with sp_eng.Fori(0, CHUNKS // 2) as i:
                ahead = [sp_eng.snap(((2 * i + s + 2) % CHUNKS) * TC) for s in range(2)]
                here = [sp_eng.snap((2 * i + s) * TC) for s in range(2)]
                for s in range(2):
                    c = 2 * i + s
                    sp_eng.wait_ge(front_ps.sem, front_ps.at(c, IN))
                    sp_eng.dma_start(xt[:, s, :, :], xT_view[:, :, bass.ds(ahead[s], TC)]).then_inc(xt_ld[s].sem, 16)
                    sp_eng.wait_ge(ygated.sem, ygated.at(c))
                    sp_eng.dma_start(y_out_view[:, :, bass.ds(here[s], TC)], yg[:, :, :]).then_inc(y_out.sem, 16)
            sp_eng.wait_ge(y_out.sem, y_out.at(CHUNKS - 1))
            for k in range(2):
                sp_eng.wait_ge(xt_ld[k].sem, 16 * (CHUNKS // 2 + 1))

        @block.tensor
        def _(pe):
            def in_proj(k, slot, j, used=True):
                if used:
                    pe.wait_ge(front_ev.sem, front_ev.at(k, j))
                for kd in range(KD):
                    last = nc.tensor.matmul(ps_f[:, :], w_in[:, kd, j * P:(j + 1) * P], xt[:, slot, kd, :],
                                            start=kd == 0, stop=kd == KD - 1)
                last.then_inc(front_ps.sem, 1)

            def x_proj(k, slot):
                pe.wait_ge(front_ev.sem, front_ev.at(k, XP))
                pe.wait_ge(xc_ready.sem, xc_ready.at(k))
                for d in range(DB):
                    last = nc.tensor.matmul(ps_f[0:PARTS, :], w_xp[:, d, :], xc[:, slot, d, :],
                                            start=d == 0, stop=d == DB - 1)
                last.then_inc(front_ps.sem, 1)

            def dt_proj(k, slot, d):
                pe.wait_ge(front_ev.sem, front_ev.at(k, XP + 1 + d))
                nc.tensor.matmul(ps_f[:, :], w_dt[:, d * P:(d + 1) * P], dt_in[:, slot, :],
                                 start=True, stop=True).then_inc(front_ps.sem, 1)

            def spread_b(c, slot, n):
                pe.wait_ge(dbx_done.sem, dbx_done.at(c, n - 1))
                pe.wait_ge(b_taken.sem, b_taken.at(c, n - 1))
                if n == 0:
                    pe.wait_ge(front_ev.sem, front_ev.at(c, XP + 1))
                nc.tensor.matmul(ps_b[:, n % 2, :], sel[:, n, :], dbc[:, slot, :],
                                 start=True, stop=True).then_inc(b_ready.sem, 1)

            def spread_c(c, slot, n):
                if n:
                    pe.wait_ge(hc_done.sem, hc_done.at(c, n))
                nc.tensor.matmul(ps_c[:, :], sel[:, NST + n, :], dbc[:, slot, :],
                                 start=True, stop=True).then_inc(c_ready.sem, 1)

            def sum_states(c, slot, n):
                if n == 0:
                    pe.wait_ge(ygated.sem, ygated.at(c - 1))
                elif n == IN:
                    for d in range(DB):
                        nc.tensor.matmul(ps_y[:, d, :], skip[:, d, :], xc[:, slot, d, :], start=False, stop=False)
                pe.wait_ge(hc_done.sem, hc_done.at(c, n + 1))
                for d in range(DB):
                    last = nc.tensor.matmul(ps_y[:, d, :], idn[:, :], hc[:, n % 2, d, :],
                                            start=n == 0, stop=n == NST - 1)
                last.then_inc(reduce_done.sem, 1)

            pe.wait_ge(front_ld.sem, 32)
            pe.wait_ge(xt_ld[0].sem, 16)
            for j in range(IN):
                in_proj(0, 0, j, j > 0)
            pe.wait_ge(zeroed.sem, 3)
            pe.wait_ge(consts.sem, 16 * CONSTS)
            pe.wait_ge(sel_ready.sem, 1)
            x_proj(0, 0)
            for d in range(DB):
                dt_proj(0, 0, d)
            pe.wait_ge(skip_ready.sem, DB)
            with pe.Fori(0, CHUNKS // 2) as i:
                for s in range(2):
                    c, k, f = 2 * i + s, 2 * i + s + 1, 1 - s
                    pe.wait_ge(xt_ld[f].sem, 16 * (i + 1 + s))
                    spread_b(c, s, 0)
                    spread_b(c, s, 1)
                    spread_c(c, s, 0)
                    for n in range(NST + 1):
                        if n + 2 < NST:
                            spread_b(c, s, n + 2)
                        if 1 <= n < NST:
                            spread_c(c, s, n)
                        if n >= 1:
                            sum_states(c, s, n - 1)
                        if n < IN:
                            in_proj(k, f, n)
                        elif n == FRONT + 1:
                            x_proj(k, f)
                        elif n in (FRONT + 2, FRONT + 3):
                            for d in range(2 * (n - FRONT - 2), 2 * (n - FRONT - 1)):
                                dt_proj(k, f, d)

        @block.scalar
        def _(act):
            def evac(k, slot, j):
                act.wait_ge(front_ps.sem, front_ps.at(k, j + 1))
                if j < DB:
                    ins = nc.scalar.activation(xraw[:, j, TAPS - 1:], ps_f[:, :], ACT.Copy)
                elif j < IN:
                    ins = nc.scalar.activation(sz[:, slot, j - DB, :], ps_f[:, :], ACT.Copy)
                elif j == XP:
                    nc.scalar.activation(dt_in[:, slot, :], ps_f[0:RANK, :], ACT.Copy)
                    nc.scalar.activation(dbc[:, slot, :], ps_f[0:PARTS, :], ACT.Copy).then_inc(high_done.sem, 1)
                    return
                else:
                    d = j - XP - 1
                    ins = nc.scalar.activation(delta[:, slot, d, :], ps_f[:, :], ACT.Identity,
                                               bias=dt_bias[:, d:d + 1])
                ins.then_inc(front_ev.sem, 1)

            def tap(k, slot, j, t):
                act.wait_ge(front_ev.sem, front_ev.at(k, j + 1))
                if j >= 2 and t == 1:
                    act.wait_ge(conv_step.sem, conv_step.at(k, (j - 1) * TAPS))
                nc.scalar.activation(tapped[:, j % 2, t - 1, :] if t else xc[:, slot, j, :], xraw[:, j, t:t + TC],
                                     ACT.Copy, scale=taps[:, j, t:t + 1]).then_inc(tap_done.sem, 1)

            def gates(k, slot):
                act.wait_ge(conv_step.sem, conv_step.at(k, DB * TAPS))
                nc.scalar.activation(xc[:, slot, :, :], xc[:, slot, :, :], ACT.Silu).then_inc(xc_ready.sem, 1)
                act.wait_ge(front_ev.sem, front_ev.at(k, IN))
                nc.scalar.activation(sz[:, slot, :, :], sz[:, slot, :, :], ACT.Silu).then_inc(sz_ready.sem, 1)

            def softplus(k, slot):
                act.wait_ge(front_ev.sem, front_ev.at(k, USES))
                act.wait_ge(delta_ready.sem, delta_ready.at(k - 1))
                nc.scalar.activation(sp[:, :, :], delta[:, slot, :, :], ACT.Abs).then_inc(sp_step.sem, 1)
                act.wait_ge(sp_step.sem, sp_step.at(k, 1))
                nc.scalar.activation(sp[:, :, :], sp[:, :, :], ACT.Exp, scale=-1.0).then_inc(sp_step.sem, 1)
                act.wait_ge(sp_step.sem, sp_step.at(k, 2))
                nc.scalar.activation(sp[:, :, :], sp[:, :, :], ACT.Ln, bias=1.0).then_inc(sp_step.sem, 1)

            def take_b(c, n):
                act.wait_ge(b_ready.sem, b_ready.at(c, n + 1))
                act.wait_ge(dbx_pool.sem, dbx_pool.at(c, n - 1))
                nc.scalar.activation(b_sb[:, n % 2, :], ps_b[:, n % 2, :], ACT.Copy).then_inc(b_taken.sem, 1)

            def decay(c, slot, n):
                if n == 0:
                    act.wait_ge(delta_ready.sem, delta_ready.at(c))
                act.wait_ge(scan_done.sem, scan_done.at(c, n - 1))
                for d in range(DB):
                    ins = nc.scalar.activation(dA[:, n % 2, d, :], delta[:, slot, d, :], ACT.Exp,
                                               scale=neg_a[:, d, n:n + 1])
                ins.then_inc(dA_ready.sem, 1)

            b_taken.credit(act)
            act.wait_ge(zeroed.sem, 3)
            for j in range(IN):
                evac(0, 0, j)
            gates(0, 0)
            act.wait_ge(consts.sem, 16 * CONSTS)
            nc.scalar.activation(neg_a[:, :, :], a_log[:, :, :], ACT.Exp).then_inc(nega_step.sem, 1)
            act.wait_ge(nega_step.sem, 1)
            nc.scalar.activation(neg_a[:, :, :], neg_a[:, :, :], ACT.Copy, scale=-1.0).then_inc(nega_step.sem, 1)
            act.wait_ge(nega_step.sem, 2)
            for j in range(XP, USES):
                evac(0, 0, j)
            for d in range(DB):
                nc.scalar.activation(skip[:, d, :], idn[:, :], ACT.Copy, scale=d_skip[:, d:d + 1]).then_inc(skip_ready.sem, 1)
            softplus(0, 0)
            with act.Fori(0, CHUNKS // 2) as i:
                for s in range(2):
                    c, k, f = 2 * i + s, 2 * i + s + 1, 1 - s
                    take_b(c, 0)
                    take_b(c, 1)
                    decay(c, s, 0)
                    act.wait_ge(ygated.sem, ygated.at(k - 2))
                    act.wait_ge(conv_step.sem, conv_step.at(k - 1))
                    for n in range(NST):
                        if n + 1 < NST:
                            decay(c, s, n + 1)
                        if n + 2 < NST:
                            take_b(c, n + 2)
                        if n < IN:
                            evac(k, f, n)
                        if 1 <= n <= 2 * DB:
                            for t in (0, 1) if n % 2 else (2, 3):
                                tap(k, f, (n - 1) // 2, t)
                        if n == FRONT:
                            gates(k, f)
                        elif n == FRONT + 1:
                            evac(k, f, XP)
                        elif n in (FRONT + 2, FRONT + 3):
                            for d in range(2 * (n - FRONT - 2), 2 * (n - FRONT - 1)):
                                evac(k, f, XP + 1 + d)
                        elif n == FRONT + 5:
                            softplus(k, f)

        @block.gpsimd
        def _(pool):
            def drive(c, slot, n):
                pool.wait_ge(b_taken.sem, b_taken.at(c, n + 1))
                if n == 0:
                    pool.wait_ge(u_ready.sem, u_ready.at(c))
                pool.wait_ge(scan_done.sem, scan_done.at(c, n - 1))
                for d in range(ON_POOL):
                    ins = nc.gpsimd.tensor_tensor(dBx[:, n % 2, d, :], u[:, slot, d, :], b_sb[:, n % 2, :], ALU.mult)
                ins.then_inc(dbx_pool.sem, 1)

            def carry(c, n, keep_col):
                pool.wait_ge(scan_done.sem, scan_done.at(c, n + 1))
                pool.sem_inc(pool_seen.sem)
                if keep_col is None:
                    ins = nc.gpsimd.tensor_copy(h_in[:, n, :], h[:, :, TC - 1])
                else:
                    ins = nc.gpsimd.tensor_tensor(h_in[:, n, :], h[:, :, TC - 1], keep_col.to_broadcast((P, DB)), ALU.mult)
                ins.then_inc(carry_done.sem, 1)

            def after(sem, value):
                pool.wait_ge(sem, value)
                pool.sem_inc(pool_seen.sem)

            def add_tap(k, slot, j, t):
                pool.wait_ge(tap_done.sem, tap_done.at(k - 1, j * TAPS + t + 1))
                if t > 1:
                    pool.wait_ge(conv_step.sem, conv_step.at(k, j * TAPS + t))
                nc.gpsimd.tensor_tensor(xc[:, slot, j, :], xc[:, slot, j, :], tapped[:, j % 2, t - 1, :],
                                        ALU.add).then_inc(conv_step.sem, 2 if t == 1 else 1)

            def halo(k, keep_col):
                after(conv_step.sem, conv_step.at(k, DB * TAPS))
                if keep_col is None:
                    ins = nc.gpsimd.tensor_copy(xraw[:, :, 0:TAPS - 1], xraw[:, :, TC:])
                else:
                    ins = nc.gpsimd.tensor_tensor(xraw[:, :, 0:TAPS - 1], xraw[:, :, TC:],
                                                  keep_col.rearrange("p (a b) -> p a b", a=1).to_broadcast((P, DB, TAPS - 1)), ALU.mult)
                ins.then_inc(conv_step.sem, 1)

            dbx_pool.credit(pool)
            carry_done.credit(pool)
            pool.wait_ge(consts.sem, 16 * CONSTS)
            nc.gpsimd.tensor_copy(sel[:, :, :], sel_in).then_inc(sel_ready.sem, 1)
            pool.wait_ge(zeroed.sem, 3)
            with pool.Fori(0, CHUNKS // 2) as i:
                for s in range(2):
                    c, k, f = 2 * i + s, 2 * i + s + 1, 1 - s
                    keep_col = keep_sb[:, bass.ds(i, 1)]
                    drive(c, s, 0)
                    for n in range(NST):
                        if n + 1 < NST:
                            drive(c, s, n + 1)
                        carry(c, n, keep_col if s else None)
                        if 1 <= n <= 2 * DB:
                            for t in (1,) if n % 2 else (2, 3):
                                add_tap(k, f, (n - 1) // 2, t)
                        elif n == 2 * DB + 1:
                            halo(k, None if s else keep_col)

        @block.vector
        def _(dve):
            def conv_tap(k, slot, t):
                for j in range(DB):
                    if t == 0:
                        dve.wait_ge(front_ev.sem, front_ev.at(k, j + 1))
                        ins = nc.vector.tensor_scalar(xc[:, slot, j, :], xraw[:, j, 0:TC], taps[:, j, 0:1], None, ALU.mult)
                    else:
                        dve.wait_ge(conv_step.sem, conv_step.at(k, (t - 1) * DB + j + 1))
                        ins = nc.vector.scalar_tensor_tensor(xc[:, slot, j, :], xraw[:, j, t:t + TC], taps[:, j, t:t + 1],
                                                             xc[:, slot, j, :], ALU.mult, ALU.add)
                    ins.then_inc(conv_step.sem, 1)

            def low_parts(k, slot):
                dve.wait_ge(high_done.sem, high_done.at(k))
                nc.vector.tensor_tensor(dbc[LOW:PARTS, slot, :], ps_f[LOW:PARTS, :], dbc[LOW:PARTS, slot, :].bitcast(F32),
                                        ALU.subtract).then_inc(front_ev.sem, 1)

            def halo(k):
                dve.wait_ge(conv_step.sem, conv_step.at(k, DB * TAPS))
                nc.vector.tensor_copy(xraw[:, :, 0:TAPS - 1], xraw[:, :, TC:]).then_inc(conv_step.sem, 1)

            def make_delta(k, slot):
                dve.wait_ge(sp_step.sem, sp_step.at(k, 3))
                nc.vector.scalar_tensor_tensor(delta[:, slot, :, :], delta[:, slot, :, :], 0.0, sp[:, :, :],
                                               ALU.max, ALU.add).then_inc(delta_ready.sem, 1)

            def make_u(k, slot):
                dve.wait_ge(delta_ready.sem, delta_ready.at(k))
                dve.wait_ge(xc_ready.sem, xc_ready.at(k))
                nc.vector.tensor_tensor(u[:, slot, :, :], delta[:, slot, :, :], xc[:, slot, :, :],
                                        ALU.mult).then_inc(u_ready.sem, 1)

            def drive(c, slot, n):
                dve.wait_ge(b_taken.sem, b_taken.at(c, n + 1))
                if n == 0:
                    dve.wait_ge(u_ready.sem, u_ready.at(c))
                dve.wait_ge(scan_done.sem, scan_done.at(c, n - 1))
                nc.vector.tensor_tensor(dBx[:, n % 2, ON_POOL:, :], u[:, slot, ON_POOL:, :],
                                        ps_b[:, n % 2:n % 2 + 1, :].to_broadcast((P, DB - ON_POOL, TC)),
                                        ALU.mult).then_inc(dbx_done.sem, 1)

            def scan(c, n):
                dve.wait_ge(dA_ready.sem, dA_ready.at(c, n + 1))
                dve.wait_ge(dbx_pool.sem, dbx_pool.at(c, n + 1))
                dve.wait_ge(dbx_done.sem, dbx_done.at(c, n + 1))
                dve.wait_ge(hc_done.sem, hc_done.at(c, n))
                dve.wait_ge(carry_done.sem, carry_done.at(c, n))
                for d in range(DB):
                    ins = nc.vector.tensor_tensor_scan(h[:, d, :], dA[:, n % 2, d, :], dBx[:, n % 2, d, :],
                                                       h_in[:, n, d:d + 1], ALU.mult, ALU.add)
                ins.then_inc(scan_done.sem, 1)

            def weigh(c, n):
                dve.wait_ge(c_ready.sem, c_ready.at(c, n + 1))
                dve.wait_ge(scan_done.sem, scan_done.at(c, n + 1))
                dve.wait_ge(reduce_done.sem, reduce_done.at(c, n - 1))
                nc.vector.tensor_tensor(hc[:, n % 2, :, :], h[:, :, :],
                                        ps_c[:, :].rearrange("p (o t) -> p o t", o=1).to_broadcast((P, DB, TC)),
                                        ALU.mult).then_inc(hc_done.sem, 1)

            def gate_out(c, slot):
                dve.wait_ge(reduce_done.sem, reduce_done.at(c))
                dve.wait_ge(y_out.sem, y_out.at(c - 1))
                dve.wait_ge(sz_ready.sem, sz_ready.at(c))
                nc.vector.tensor_tensor(yg[:, :, :], ps_y[:, :, :], sz[:, slot, :, :], ALU.mult).then_inc(ygated.sem, 1)

            for t in (conv_step, delta_ready, dbx_done, scan_done, hc_done, reduce_done, ygated):
                t.credit(dve)
            nc.vector.memset(xraw[:, :, 0:TAPS - 1], 0.0).then_inc(zeroed.sem, 1)
            nc.vector.memset(h_in[:, :, :], 0.0).then_inc(zeroed.sem, 1)
            nc.vector.memset(w_xp[:, :, NBC:LOW], 0.0).then_inc(zeroed.sem, 1)
            dve.wait_ge(zeroed.sem, 3)
            dve.wait_ge(front_ld.sem, 32)
            for t in range(TAPS):
                conv_tap(0, 0, t)
            halo(0)
            dve.wait_ge(consts.sem, 16 * CONSTS)
            dve.wait_ge(sel_ready.sem, 1)
            low_parts(0, 0)
            make_delta(0, 0)
            make_u(0, 0)
            with dve.Fori(0, CHUNKS // 2) as i:
                for s in range(2):
                    c, k, f = 2 * i + s, 2 * i + s + 1, 1 - s
                    drive(c, s, 0)
                    for n in range(NST):
                        if n >= 1:
                            weigh(c, n - 1)
                        if n + 1 < NST:
                            drive(c, s, n + 1)
                        scan(c, n)
                        if n == FRONT + 2:
                            low_parts(k, f)
                    weigh(c, NST - 1)
                    make_delta(k, f)
                    make_u(k, f)
                    gate_out(c, s)
    nc.clear_and_free_semaphores(sems)
    nc.all_engine_barrier()


EPS = 1e-5
NT = TOKENS // P


def tree_ffn(nc, y_scr, x_rows, W_outT, F_inT, F_bias, F_outT, ident, x2_rows, x2_T):
    DI, PAR, DEPTH = 512, 8, 7
    NODES = 2 ** (DEPTH + 1) - 1
    WIDTH = PAR * NODES
    DB = DI // P
    LB = 4
    LC = WIDTH // LB
    NB = -(-WIDTH // P)
    TAIL = WIDTH - (NB - 1) * P
    TG = NB // 4
    TR = TG + 2

    y_view = y_scr.rearrange("(d p) t -> p d t", p=P)
    x2T_view = x2_T.rearrange("(k p) t -> p k t", p=P)

    sems = []
    with ExitStack() as ctx:
        def sb(name, shape, dt=F32):
            return ctx.enter_context(nc.sbuf_tensor(name, shape, dt))

        def pb(name, shape):
            return ctx.enter_context(nc.psum_tensor(name, shape, F32))

        def tally(name, per=1, ahead=0):
            sems.append(nc.alloc_semaphore(name))
            return Tally(sems[-1], per, ahead)

        w_out = sb("w_out", [P, DB, DM])
        f_in = sb("f_in", [P, KD, WIDTH])
        f_bias = sb("f_bias", [P, WIDTH])
        f_out = sb("f_out", [P, NB, DM])
        idn = sb("idn2", [P, P])
        yt = sb("yt", [P, 2, DB, P])
        xin = sb("xin", [P, 2, DM])
        r1 = sb("r1", [P, 2, DM])
        x1 = sb("x1", [P, 2, DM])
        x1T = sb("x1T", [P, 2, KD, P])
        lg = sb("lg", [P, 2, PAR, NODES])
        acts = sb("acts", [P, 2, PAR, NODES])
        reach = sb("reach", [P, 2, PAR, NODES])
        mT = sb("mT", [P, NB, P])
        r2 = sb("r2", [P, DM])
        x2 = sb("x2", [P, 2, DM])
        x2T = sb("x2T", [P, 2, KD, P])
        stats = sb("stats2", [P, 2, 6])
        mv = sb("mv2", [P, 2, 2])
        rstd = sb("rstd2", [P, 2, 1])
        nhalf = sb("nhalf2", [P, 1])
        eps_sb = sb("eps2", [P, 1])
        ps_l = pb("ps_l", [P, LB, 512])
        ps_o = pb("ps_o", [P, 512])
        ps_d = pb("ps_d", [P, 512])
        ps_t = pb("ps_t", [P, 2, 4, P])

        front_ld = tally("front_ld2")
        consts = tally("consts2")
        f_out_ld = tally("f_out_ld")
        in_ld = [tally("in_ld0", 32), tally("in_ld1", 32)]
        ready0 = tally("ready0", 3)
        nh_set = tally("nh_set")
        op_ps = tally("op_ps")
        lg_ps = tally("lg_ps")
        fo_ps = tally("fo_ps", 1, 1)
        tr_ps = tally("tr_ps", TR, 1)
        tr_ev = tally("tr_ev", TR, 1)
        sum1 = tally("sum1", 1, 1)
        stat_seen = tally("stat_seen")
        stat1 = tally("stat1")
        aggr1 = tally("aggr1")
        add1 = tally("add1")
        pow1 = tally("pow1")
        x1_ready = tally("x1_ready")
        kept = tally("kept")
        lg_ready = tally("lg_ready", 1, 1)
        silu_done = tally("silu_done")
        tree = tally("tree", 2 * DEPTH)
        masked = tally("masked", 1, 1)
        sum2 = tally("sum2", 1, 1)
        stat2 = tally("stat2")
        aggr2 = tally("aggr2")
        add2 = tally("add2")
        pow2 = tally("pow2")
        x2_ready = tally("x2_ready", 1, 1)
        x2_out = [tally("x2_out0", 16, 1), tally("x2_out1", 16, 1)]
        x2T_out = [tally("x2T_out0", 16, 1), tally("x2T_out1", 16, 1)]
        NCONST = 2

        block = ctx.enter_context(nc.Block())

        @block.sync
        def _(sp):
            def load(slot, col):
                sp.dma_start(yt[:, slot, :, :], y_view[:, :, col]).then_inc(in_ld[slot].sem, 16)
                sp.dma_start(xin[:, slot, :], x_rows[col, :]).then_inc(in_ld[slot].sem, 16)

            load(0, slice(0, P))
            for dst, src, ready in (
                (w_out[:, :, :], W_outT.rearrange("(d p) n -> p d n", p=P), front_ld),
                (idn[:, :], ident, front_ld),
                (f_in[:, :, :], F_inT.rearrange("(k p) n -> p k n", p=P), consts),
                (f_bias[:, :], F_bias.rearrange("(o n) -> o n", o=1).to_broadcast((P, WIDTH)), consts),
            ):
                sp.dma_start(dst, src).then_inc(ready.sem, 16)
            load(1, slice(P, 2 * P))
            for dst, src in (
                (f_out[:, 0:NB - 1, :], F_outT[0:(NB - 1) * P, :].rearrange("(b p) n -> p b n", p=P)),
                (f_out[0:TAIL, NB - 1, :], F_outT[(NB - 1) * P:WIDTH, :]),
            ):
                sp.dma_start(dst, src).then_inc(f_out_ld.sem, 16)
            for o in x2_out + x2T_out:
                o.credit(sp)
            sp.wait_ge(sum1.sem, sum1.at(0))
            load(0, slice(2 * P, 3 * P))
            with sp.Fori(0, NT // 2) as i:
                ahead = [sp.snap(((2 * i + s + 3) % NT) * P) for s in range(2)]
                here = [sp.snap((2 * i + s) * P) for s in range(2)]
                prev = [sp.snap(((2 * i + s + NT - 1) % NT) * P) for s in range(2)]
                for s in range(2):
                    t = 2 * i + s
                    sp.wait_ge(sum1.sem, sum1.at(t + 1))
                    load(1 - s, bass.ds(ahead[s], P))
                    sp.wait_ge(tr_ev.sem, tr_ev.at(t))
                    sp.dma_start(x2T_view[:, :, bass.ds(prev[s], P)], x2T[:, 1 - s, :, :]).then_inc(x2T_out[1 - s].sem, 16)
                    sp.wait_ge(x2_ready.sem, x2_ready.at(t))
                    sp.dma_start(x2_rows[bass.ds(here[s], P), :], x2[:, s, :]).then_inc(x2_out[s].sem, 16)
            for s in range(2):
                sp.wait_ge(x2T_out[s].sem, x2T_out[s].at(NT // 2 - 1))
            sp.wait_ge(tr_ev.sem, tr_ev.at(NT, 1))
            sp.dma_start(x2T_view[:, :, TOKENS - P:], x2T[:, 1, :, :]).then_inc(x2T_out[1].sem, 16)
            sp.wait_ge(x2T_out[1].sem, x2T_out[1].at(NT // 2))
            for s in range(2):
                sp.wait_ge(x2_out[s].sem, x2_out[s].at(NT // 2 - 1))
            for s in range(2):
                sp.wait_ge(in_ld[s].sem, 32 * (NT // 2 + 2 - s))

        @block.tensor
        def _(pe):
            def out_proj(t, s, loads):
                pe.wait_ge(in_ld[s].sem, 32 * loads)
                pe.wait_ge(sum1.sem, sum1.at(t - 1))
                for d in range(DB):
                    last = nc.tensor.matmul(ps_o[:, 0:DM], yt[:, s, d, :], w_out[:, d, :], start=d == 0, stop=d == DB - 1)
                last.then_inc(op_ps.sem, 1)

            def turn(t, use, blocks):
                pe.wait_ge(tr_ev.sem, tr_ev.at(t, use - 1))
                for b, (rows, src) in enumerate(blocks):
                    last = nc.tensor.transpose(ps_t[0:rows, use % 2, b, :], src, idn[:, :])
                last.then_inc(tr_ps.sem, 1)

            def turn_x1(step, t, s):
                pe.wait_ge(x1_ready.sem, x1_ready.at(t))
                turn(step, 0, [(P, x1[:, s, k * P:(k + 1) * P]) for k in range(KD)])

            def logits(step, t, s, uses=1):
                pe.wait_ge(tr_ev.sem, tr_ev.at(step, uses))
                pe.wait_ge(lg_ready.sem, lg_ready.at(t - 1))
                for b in range(LB):
                    for k in range(KD):
                        last = nc.tensor.matmul(ps_l[:, b, 0:LC], x1T[:, s, k, :], f_in[:, k, b * LC:(b + 1) * LC],
                                                start=k == 0, stop=k == KD - 1)
                last.then_inc(lg_ps.sem, 1)

            def nodes_out(t, s):
                pe.wait_ge(masked.sem, masked.at(t))
                flat = acts[:, s, :, :].rearrange("p a n -> p (a n)")
                for g in range(TG + 1):
                    if g < TG:
                        blocks = [(min(P, WIDTH - b * P), flat[:, b * P:min((b + 1) * P, WIDTH)]) for b in range(4 * g, 4 * g + 4)]
                        turn(t, 1 + g, blocks)
                    if g == 1:
                        pe.wait_ge(sum2.sem, sum2.at(t - 1))
                    if g:
                        pe.wait_ge(tr_ev.sem, tr_ev.at(t, 1 + g))
                        for b in range(4 * g - 4, 4 * g):
                            rows = min(P, WIDTH - b * P)
                            last = nc.tensor.matmul(ps_d[:, 0:DM], mT[0:rows, b, :], f_out[0:rows, b, :],
                                                    start=b == 0, stop=b == NB - 1)
                last.then_inc(fo_ps.sem, 1)

            def turn_x2(step, t, s):
                pe.wait_ge(x2_ready.sem, x2_ready.at(t))
                turn(step, 1 + TG, [(P, x2[:, s, k * P:(k + 1) * P]) for k in range(KD)])

            pe.sem_inc(tr_ps.sem, TR - 1)
            pe.wait_ge(front_ld.sem, 32)
            out_proj(0, 0, 1)
            out_proj(1, 1, 1)
            pe.wait_ge(x1_ready.sem, x1_ready.at(0))
            pe.wait_ge(ready0.sem, 3)
            for k in range(KD):
                last = nc.tensor.transpose(ps_t[:, 1, k, :], x1[:, 0, k * P:(k + 1) * P], idn[:, :])
            last.then_inc(tr_ps.sem, 1)
            pe.wait_ge(consts.sem, 16 * NCONST)
            logits(-1, 0, 0, TR)
            pe.wait_ge(f_out_ld.sem, 32)
            with pe.Fori(0, NT // 2) as i:
                for s in range(2):
                    t = 2 * i + s
                    turn_x1(t, t + 1, 1 - s)
                    out_proj(t + 2, s, i + 2)
                    logits(t, t + 1, 1 - s)
                    nodes_out(t, s)
                    turn_x2(t, t - 1, 1 - s)
            turn_x2_last = [(P, x2[:, 1, k * P:(k + 1) * P]) for k in range(KD)]
            pe.wait_ge(x2_ready.sem, x2_ready.at(NT - 1))
            turn(NT, 0, turn_x2_last)

        @block.scalar
        def _(act):
            def take(t, use, dst, src):
                act.wait_ge(tr_ps.sem, tr_ps.at(t, use + 1))
                return nc.scalar.activation(dst, src, ACT.Copy)

            def take_x(step, use, dst):
                take(step, use, dst, ps_t[:, use % 2, 0:KD, :]).then_inc(tr_ev.sem, 1)

            def gate(t, s, first=False):
                act.wait_ge(lg_ready.sem, lg_ready.at(t))
                if not first:
                    act.wait_ge(tr_ps.sem, tr_ps.at(t - 2, 1 + TG))
                nc.scalar.activation(acts[:, s, :, :], lg[:, s, :, :], ACT.Silu).then_inc(silu_done.sem, 1)

            def take_nodes(t, s):
                act.wait_ge(fo_ps.sem, fo_ps.at(t - 1))
                for g in range(TG):
                    whole = 4 if g < TG - 1 else 3
                    ins = take(t, 1 + g, mT[:, 4 * g:4 * g + whole, :], ps_t[:, (1 + g) % 2, 0:whole, :])
                    if whole < 4:
                        ins = nc.scalar.activation(mT[0:TAIL, NB - 1, :], ps_t[0:TAIL, (1 + g) % 2, 3, :], ACT.Copy)
                    ins.then_inc(tr_ev.sem, 1)

            fo_ps.credit(act)
            act.sem_inc(tr_ev.sem, TR - 1)
            act.wait_ge(tr_ps.sem, tr_ps.at(-1, TR))
            nc.scalar.activation(x1T[:, 0, :, :], ps_t[:, 1, 0:KD, :], ACT.Copy).then_inc(tr_ev.sem, 1)
            gate(0, 0, True)
            with act.Fori(0, NT // 2) as i:
                for s in range(2):
                    t = 2 * i + s
                    take_x(t, 0, x1T[:, 1 - s, :, :])
                    take_nodes(t, s)
                    gate(t + 1, 1 - s)
                    act.wait_ge(x2T_out[1 - s].sem, x2T_out[1 - s].at(i - 1))
                    take_x(t, 1 + TG, x2T[:, 1 - s, :, :])
            act.wait_ge(x2T_out[1].sem, x2T_out[1].at(NT // 2 - 1))
            take_x(NT, 0, x2T[:, 1, :, :])

        @block.gpsimd
        def _(pool):
            def inv_std(t, n, aggr, add, pw):
                pool.wait_ge(aggr.sem, aggr.at(t))
                nc.gpsimd.tensor_tensor(rstd[:, n, :], mv[:, n, 1:2], eps_sb[:, :], ALU.add).then_inc(add.sem, 1)
                pool.wait_ge(add.sem, add.at(t))
                nc.gpsimd.tensor_tensor(rstd[:, n, :], rstd[:, n, :], nhalf[:, :], ALU.pow).then_inc(pw.sem, 1)

            nc.gpsimd.memset(nhalf[:, :], -0.5).then_inc(nh_set.sem, 1)
            nc.gpsimd.memset(eps_sb[:, :], EPS).then_inc(nh_set.sem, 1)
            pool.wait_ge(nh_set.sem, 2)
            inv_std(0, 0, aggr1, add1, pow1)
            inv_std(1, 0, aggr1, add1, pow1)
            with pool.Fori(0, NT // 2) as i:
                for s in range(2):
                    t = 2 * i + s
                    inv_std(t + 2, 0, aggr1, add1, pow1)
                    inv_std(t, 1, aggr2, add2, pow2)

        @block.vector
        def _(dve):
            def moments(t, n, r, stat, aggr):
                nc.vector.bn_stats(stats[:, n, :], r).then_inc(stat.sem, 1)
                dve.wait_ge(stat.sem, stat.at(t))
                dve.sem_inc(stat_seen.sem)
                nc.vector.bn_aggr(mv[:, n, :], stats[:, n, :]).then_inc(aggr.sem, 1)

            def norm1(t, s, first=False):
                dve.wait_ge(op_ps.sem, op_ps.at(t))
                nc.vector.tensor_tensor(r1[:, s, :], ps_o[:, 0:DM], xin[:, s, :], ALU.add).then_inc(sum1.sem, 1)
                dve.wait_ge(sum1.sem, sum1.at(t))
                moments(t, 0, r1[:, s, :], stat1, aggr1)
                dve.wait_ge(pow1.sem, pow1.at(t))
                if not first:
                    dve.wait_ge(tr_ps.sem, tr_ps.at(t - 3, 1))
                    dve.wait_ge(kept.sem, kept.at(t - 2))
                nc.vector.tensor_scalar(x1[:, s, :], r1[:, s, :], mv[:, 0, 0:1], rstd[:, 0, :], ALU.subtract,
                                        ALU.mult).then_inc(x1_ready.sem, 1)
                dve.wait_ge(x1_ready.sem, x1_ready.at(t))

            def path(t, s):
                dve.wait_ge(lg_ps.sem, lg_ps.at(t))
                flat = lg[:, s, :, :].rearrange("p a n -> p (a n)").rearrange("p (b n) -> p b n", b=LB)
                nc.vector.tensor_tensor(flat, ps_l[:, :, 0:LC], f_bias[:, :].rearrange("p (b n) -> p b n", b=LB),
                                        ALU.add).then_inc(lg_ready.sem, 1)
                dve.wait_ge(lg_ready.sem, lg_ready.at(t))
                for d in range(DEPTH):
                    lo, n = 2 ** d - 1, 2 ** d
                    kids = reach[:, s, :, 2 * n - 1:4 * n - 1].rearrange("p a (n two) -> p a n two", two=2)
                    here = reach[:, s, :, lo:lo + n]
                    if d:
                        dve.wait_ge(tree.sem, tree.at(t, 2 * d))
                    nc.vector.scalar_tensor_tensor(kids[:, :, :, 1], lg[:, s, :, lo:lo + n], 0.0, here, ALU.is_gt,
                                                   ALU.mult).then_inc(tree.sem, 1)
                    dve.wait_ge(tree.sem, tree.at(t, 2 * d + 1))
                    nc.vector.tensor_tensor(kids[:, :, :, 0], here, kids[:, :, :, 1], ALU.subtract).then_inc(tree.sem, 1)
                dve.wait_ge(tree.sem, tree.at(t))
                dve.wait_ge(silu_done.sem, silu_done.at(t))
                nc.vector.tensor_tensor(acts[:, s, :, :], acts[:, s, :, :], reach[:, s, :, :], ALU.mult).then_inc(masked.sem, 1)

            def keep_x1(t, s):
                dve.wait_ge(x2_ready.sem, x2_ready.at(t - 1))
                nc.vector.tensor_copy(r2[:, :], x1[:, s, :]).then_inc(kept.sem, 1)

            def norm2(t, s, i):
                dve.wait_ge(fo_ps.sem, fo_ps.at(t))
                dve.wait_ge(kept.sem, kept.at(t))
                nc.vector.tensor_tensor(r2[:, :], ps_d[:, 0:DM], r2[:, :], ALU.add).then_inc(sum2.sem, 1)
                dve.wait_ge(sum2.sem, sum2.at(t))
                moments(t, 1, r2[:, :], stat2, aggr2)
                dve.wait_ge(pow2.sem, pow2.at(t))
                dve.wait_ge(x2_out[s].sem, x2_out[s].at(i - 1))
                dve.wait_ge(tr_ps.sem, tr_ps.at(t - 1))
                nc.vector.tensor_scalar(x2[:, s, :], r2[:, :], mv[:, 1, 0:1], rstd[:, 1, :], ALU.subtract,
                                        ALU.mult).then_inc(x2_ready.sem, 1)
                dve.wait_ge(x2_ready.sem, x2_ready.at(t))

            for t in (sum1, lg_ready, masked, sum2, x2_ready):
                t.credit(dve)
            nc.vector.memset(reach[:, 0, :, 0:1], 1.0).then_inc(ready0.sem, 1)
            nc.vector.memset(reach[:, 1, :, 0:1], 1.0).then_inc(ready0.sem, 1)
            nc.vector.memset(x2[:, 1, :], 0.0).then_inc(ready0.sem, 1)
            dve.wait_ge(ready0.sem, 3)
            norm1(0, 0, True)
            norm1(1, 1, True)
            dve.wait_ge(consts.sem, 16 * NCONST)
            path(0, 0)
            with dve.Fori(0, NT // 2) as i:
                for s in range(2):
                    t = 2 * i + s
                    keep_x1(t, s)
                    norm1(t + 2, s)
                    path(t + 1, 1 - s)
                    norm2(t, s, i)
    nc.clear_and_free_semaphores(sems)
    nc.all_engine_barrier()


HEADS, KV, HD = 16, 4, 64
GROUP = HEADS // KV


def qkv(nc, x2_T, Wqk, Wv, rope_q, rope_k, q_scr, k_scr, v_scr):
    TC = 512
    CHUNKS = TOKENS // TC
    PAIRS = KV + 1
    HALF = HD // 2
    PER = TC // P
    xT_view = x2_T.rearrange("(k p) t -> p k t", p=P)
    v_view = v_scr.rearrange("(n p) d -> p n d", p=P)

    sems = []
    with ExitStack() as ctx:
        def sb(name, shape, dt=F32):
            return ctx.enter_context(nc.sbuf_tensor(name, shape, dt))

        def pb(name, shape):
            return ctx.enter_context(nc.psum_tensor(name, shape, F32))

        def tally(name, per=1, ahead=0):
            sems.append(nc.alloc_semaphore(name))
            return Tally(sems[-1], per, ahead)

        w_qk = sb("w_qk", [P, KD, 2 * PAIRS, P])
        w_v = sb("w_v", [P, KD, KV * HD])
        rope = sb("rope", [P, 2, 4, LENGTH])
        xt = sb("xt3", [P, 2, KD, TC])
        even = sb("even", [P, 2, 2, TC])
        odd = sb("odd", [P, 2, 2, TC])
        rot = sb("rot", [P, 2, 2, TC])
        v_sb = sb("v_sb", [P, 2, PER, KV * HD])
        ps_qk = pb("ps_qk", [P, 2, 2, TC])
        ps_v = pb("ps_v", [P, PER, KV * HD])

        w_ld = tally("qkv_w_ld")
        rope_ld = [tally("rope_ld0", 32), tally("rope_ld1", 32, 1)]
        xt_ld = [tally("xt3_ld0"), tally("xt3_ld1")]
        qk_ps = tally("qk_ps", PAIRS)
        v_ps = tally("v_ps")
        v_ev = tally("v_ev", 1, 1)
        even_done = tally("even_done", PAIRS)
        odd_done = tally("odd_done", PAIRS, 1)
        rot_done = tally("rot_done", PAIRS)
        qk_out = [tally("qk_out0", 32 * PAIRS, 1), tally("qk_out1", 32 * PAIRS, 1)]
        v_out = [tally("v_out0", 16, 1), tally("v_out1", 16, 1)]

        block = ctx.enter_context(nc.Block())

        @block.sync
        def _(sp):
            sp.dma_start(xt[:, 0, :, :], xT_view[:, :, 0:TC]).then_inc(xt_ld[0].sem, 16)
            sp.dma_start(w_qk[:, :, :, :], Wqk.rearrange("(k p) b n -> p k b n", p=P)).then_inc(w_ld.sem, 16)
            sp.dma_start(w_v[:, :, :], Wv.rearrange("(k p) n -> p k n", p=P)).then_inc(w_ld.sem, 16)
            rope_ld[1].credit(sp)
            for half in range(2):
                cols = slice(half * LENGTH // 2, (half + 1) * LENGTH // 2)
                for kind, src in enumerate((rope_q, rope_k)):
                    sp.dma_start(rope[:, kind, :, cols], src[:, :, cols]).then_inc(rope_ld[half].sem, 16)
                if half == 0:
                    sp.dma_start(xt[:, 1, :, :], xT_view[:, :, TC:2 * TC]).then_inc(xt_ld[1].sem, 16)
            for o in qk_out + v_out:
                o.credit(sp)
            with sp.Fori(0, CHUNKS // 2) as i:
                ahead = [sp.snap(((2 * i + s + 2) % CHUNKS) * TC) for s in range(2)]
                batch = sp.snap(i // (CHUNKS // 4))
                pos = [sp.snap(((2 * i + s) % (CHUNKS // 2)) * TC) for s in range(2)]
                first = [sp.snap((2 * i + s) * PER) for s in range(2)]
                q_row = [sp.snap(batch * HEADS + GROUP * g) for g in range(KV)]
                k_row = sp.snap(batch * KV)
                for s in range(2):
                    c = 2 * i + s
                    for p in range(PAIRS):
                        slot = (s * PAIRS + p) % 2
                        sp.wait_ge(rot_done.sem, rot_done.at(c, p + 1))
                        for eo in range(2):
                            rows = slice(eo * HALF, (eo + 1) * HALF)
                            to = (q_scr[bass.ds(q_row[p], GROUP), rows, bass.ds(pos[s], TC)] if p < KV
                                  else k_scr[bass.ds(k_row, KV), rows, bass.ds(pos[s], TC)])
                            sp.dma_start(to, rot[:, slot, eo, :]).then_inc(qk_out[slot].sem, 16)
                    sp.wait_ge(v_ev.sem, v_ev.at(c))
                    sp.dma_start(v_view[:, bass.ds(first[s], PER), :], v_sb[:, s, :, :]).then_inc(v_out[s].sem, 16)
                    sp.dma_start(xt[:, s, :, :], xT_view[:, :, bass.ds(ahead[s], TC)]).then_inc(xt_ld[s].sem, 16)
            for s in range(2):
                sp.wait_ge(xt_ld[s].sem, 16 * (CHUNKS // 2 + 1))
                sp.wait_ge(v_out[s].sem, v_out[s].at(CHUNKS // 2 - 1))
                sp.wait_ge(qk_out[s].sem, qk_out[s].at(CHUNKS // 2 - 1))

        @block.tensor
        def _(pe):
            pe.wait_ge(w_ld.sem, 32)
            with pe.Fori(0, CHUNKS // 2) as i:
                for s in range(2):
                    c = 2 * i + s
                    pe.wait_ge(xt_ld[s].sem, 16 * (i + 1))
                    for p in range(PAIRS):
                        slot = (s * PAIRS + p) % 2
                        pe.wait_ge(odd_done.sem, odd_done.at(c, p - 1))
                        for eo in range(2):
                            for k in range(KD):
                                last = nc.tensor.matmul(ps_qk[:, slot, eo, :], w_qk[:, k, 2 * p + eo, :], xt[:, s, k, :],
                                                        start=k == 0, stop=k == KD - 1)
                        last.then_inc(qk_ps.sem, 1)
                    pe.wait_ge(v_ev.sem, v_ev.at(c - 1))
                    for n in range(PER):
                        for k in range(KD):
                            last = nc.tensor.matmul(ps_v[:, n, :], xt[:, s, k, n * P:(n + 1) * P], w_v[:, k, :],
                                                    start=k == 0, stop=k == KD - 1)
                    last.then_inc(v_ps.sem, 1)

        @block.scalar
        def _(act):
            v_ev.credit(act)
            with act.Fori(0, CHUNKS // 2) as i:
                for s in range(2):
                    c = 2 * i + s
                    act.wait_ge(v_ps.sem, v_ps.at(c))
                    act.wait_ge(v_out[s].sem, v_out[s].at(i - 1))
                    nc.scalar.activation(v_sb[:, s, :, :], ps_v[:, :, :], ACT.Copy).then_inc(v_ev.sem, 1)

        @block.vector
        def _(dve):
            odd_done.credit(dve)
            dve.wait_ge(rope_ld[0].sem, 32)
            with dve.Fori(0, CHUNKS // 2) as i:
                pos = [dve.snap(((2 * i + s) % (CHUNKS // 2)) * TC) for s in range(2)]
                dve.wait_ge(rope_ld[1].sem, rope_ld[1].at(i % 2 - 1))
                for s in range(2):
                    c = 2 * i + s
                    for p in range(PAIRS):
                        slot = (s * PAIRS + p) % 2
                        kind = p // KV
                        dve.wait_ge(qk_ps.sem, qk_ps.at(c, p + 1))
                        for eo, dst, done in ((0, even, even_done), (1, odd, odd_done)):
                            nc.vector.tensor_tensor(dst[:, slot, :, :],
                                                    ps_qk[:, slot, eo:eo + 1, :].to_broadcast((P, 2, TC)),
                                                    rope[:, kind, 2 * eo:2 * eo + 2, bass.ds(pos[s], TC)],
                                                    ALU.mult).then_inc(done.sem, 1)
                        dve.wait_ge(even_done.sem, even_done.at(c, p + 1))
                        dve.wait_ge(odd_done.sem, odd_done.at(c, p + 1))
                        dve.wait_ge(qk_out[slot].sem, qk_out[slot].at(i - 1, 32 * ((s * PAIRS + p) // 2) + 32 * PAIRS))
                        nc.vector.tensor_tensor(rot[:, slot, :, :], even[:, slot, :, :], odd[:, slot, :, :],
                                                ALU.add).then_inc(rot_done.sem, 1)
    nc.clear_and_free_semaphores(sems)
    nc.all_engine_barrier()


def attention(nc, q_scr, k_scr, v_scr, ident, causal, attn):
    BAND = 4
    QT = LENGTH // P
    BANDS = QT // BAND
    CW = 512
    CB = CW // P
    UNITS = [(BANDS - 1 - k, k) for k in range(BANDS // 2)]
    NU = len(UNITS)
    CHUNKS = [[(s, j, c) for s in unit for j in range(BAND) for c in range(s + 1)] for unit in UNITS]
    GROUPS = [[(s, kb) for s in unit for kb in range(CB * (s + 1))] for unit in UNITS]
    STEPS = len(CHUNKS[0])
    assert all(len(u) == STEPS for u in CHUNKS + GROUPS)
    PER = NU * STEPS
    FOLD = [CB * (long + 1) + 2 for long, short in UNITS]
    TURNS = STEPS + 2
    BLOCKS = sum(BAND * s + j + 1 for s in UNITS[0] for j in range(BAND))
    RING = 5
    SLOTS = 4
    LEAD = STEPS
    AHEAD = LEAD - BAND
    LAG = 2
    LATE = STEPS - 2
    QUEUE = [s for unit in UNITS for s in unit]
    V_ORDER = sorted(range(BANDS), key=lambda b: max(k * STEPS + g for k in range(NU) for g, (s, kb) in enumerate(GROUPS[k]) if kb // BAND == b))
    V_USED = [max(k * STEPS + g + 1 for k in range(NU) for g, (s, kb) in enumerate(GROUPS[k]) if kb // BAND == b) for b in V_ORDER]
    NHEADS = BATCH * HEADS
    NGROUPS = BATCH * KV
    assert STEPS % RING == 0 and STEPS % SLOTS == 0 and TURNS % 2 == 0
    attn_view = attn.rearrange("(n p) d -> p n d", p=P)
    v_view = v_scr.rearrange("(n p) d -> p n d", p=P)

    def blocks(s, j, c):
        return CB if c < s else j + 1

    def place(k, s, j, kb):
        start = sum(BAND * s + b + 1 for b in range(j))
        if s == UNITS[k][1]:
            start += sum(BAND * UNITS[k][0] + b + 1 for b in range(BAND))
        return start + kb

    def use(k, g):
        return k * TURNS + g + (g > FOLD[k])

    def fold_use(k, short):
        return k * TURNS + (TURNS - 1 if short else FOLD[k] + 1)

    def chunk(k, v, lead):
        n = k * STEPS + v + lead
        return n // PER, n % PER // STEPS, n % STEPS

    sems = []
    with ExitStack() as ctx:
        def sb(name, shape, dt=F32):
            return ctx.enter_context(nc.sbuf_tensor(name, shape, dt))

        def pb(name, shape):
            return ctx.enter_context(nc.psum_tensor(name, shape, F32))

        def tally(name, per=1, ahead=0):
            sems.append(nc.alloc_semaphore(name))
            return Tally(sems[-1], per, ahead)

        idn = sb("idn3", [P, P])
        idn_r = sb("idn_r", [P, P], F32R)
        idn_2 = sb("idn_2", [P, HD])
        mask = sb("mask", [P, P])
        mask_r = sb("mask_r", [P, P], F32R)
        qstage = sb("qstage", [P, QT, P])
        kstage = sb("kstage", [P, LENGTH])
        vstage = sb("vstage", [P, QT, HD])
        qbuf = sb("qbuf", [P, QT, P], F32R)
        kbuf = sb("kbuf", [P, 2, 2, LENGTH], F32R)
        vnext = sb("vnext", [P, QT, 2, HD], F32R)
        vbuf = sb("vbuf", [P, QT, 2, HD], F32R)
        probs = sb("probs", [P, NU, BLOCKS, P])
        probsT = sb("probsT", [P, SLOTS, 2, CW], F32R)
        pmax = sb("pmax", [P, 2 * BAND, BANDS])
        negm = sb("negm", [P, 2 * BAND, 1])
        sums = sb("sums", [P, BANDS, BAND, BANDS])
        total = sb("total", [P, BANDS, BAND])
        rinv = sb("rinv", [P, BANDS, BAND, 1])
        folding = sb("folding", [P, CW])
        ostage = sb("ostage", [P, QT, HD])
        ps_s = pb("ps_s", [P, RING, CW])
        ps_t = pb("ps_t3", [P, 2, CW])
        ps_o = pb("ps_o3", [P, CW])

        consts = tally("consts3b")
        rounded = tally("rounded")
        q_ld = [tally("q_ld%d" % j, 32) for j in range(BANDS)]
        k_ld = tally("k_ld", 32)
        v_ld = tally("v_ld", 16)
        high_k = tally("high_k")
        k_ready = tally("k_ready")
        high_v = tally("high_v")
        v_ready = tally("v_ready")
        v_set = tally("v_set", BANDS)
        high_q = tally("high_q", BANDS)
        q_ready = tally("q_ready", BANDS)
        pool_seen = tally("pool_seen")
        sp_seen = tally("sp_seen")
        s_done = tally("s_done", PER, 1)
        t_done = tally("t_done", PER, 1)
        pv_done = tally("pv_done", PER, 1)
        f_done = tally("f_done", 2 * NU, 1)
        exp_done = tally("exp_done", PER, 1)
        high_t = tally("high_t", PER)
        o_ev = tally("o_ev", 2 * NU, 1)
        t_out = tally("t_out", NU * TURNS, 1)
        cmax = tally("cmax", PER)
        m_done = tally("m_done", QT)
        sum_done = tally("sum_done", 2 * NU)
        r_done = tally("r_done", 2 * NU, 1)
        o_out = [tally("o_out%d" % s, 16, 1) for s in range(BANDS)]
        NCONST = 4

        def band_end(k, s):
            return (k + 1) * STEPS if s == UNITS[k][1] else k * STEPS + BAND * (s + 1)

        def tile_end(k, tile):
            s, j = UNITS[k][tile // BAND], tile % BAND
            return band_end(k, s) - (BAND - 1 - j) * (s + 1)

        block = ctx.enter_context(nc.Block())

        @block.sync
        def _(sp):
            def load_keys(group):
                for half in range(2):
                    sp.dma_start(kstage[half * HD:(half + 1) * HD, :], k_scr[bass.ds(group, 1)].rearrange("g p t -> p (g t)")
                                 ).then_inc(k_ld.sem, 16)

            def load_values(first, col):
                sp.dma_start(vstage[:, :, :], v_view[:, bass.ds(first, QT), bass.ds(col, HD)]).then_inc(v_ld.sem, 16)

            def load_queries(hx, j):
                for half in range(2):
                    sp.dma_start(qstage[half * HD:(half + 1) * HD, BAND * j:BAND * (j + 1), :].rearrange("p n t -> p (n t)"),
                                 q_scr[bass.ds(hx, 1), :, j * CW:(j + 1) * CW].rearrange("o p t -> p (o t)")
                                 ).then_inc(q_ld[j].sem, 16)

            load_keys(0)
            for j in QUEUE[:2]:
                load_queries(0, j)
            for dst, src in ((idn[:, :], ident), (mask[:, :], causal), (idn_2[0:HD, :], ident[0:HD, 0:HD]),
                             (idn_2[HD:P, :], ident[0:HD, 0:HD])):
                sp.dma_start(dst, src).then_inc(consts.sem, 16)
            load_values(0, 0)
            for j in QUEUE[2:]:
                load_queries(0, j)
            for o in o_out:
                o.credit(sp)
            with sp.Fori(0, NGROUPS) as g:
                group = sp.snap((g + 1) % NGROUPS)
                first_kv = sp.snap((group // KV) * QT)
                col_kv = sp.snap((group % KV) * HD)
                sp.wait_ge(k_ready.sem, k_ready.at(g))
                load_keys(group)
                sp.wait_ge(v_ready.sem, v_ready.at(g))
                sp.sem_inc(sp_seen.sem)
                load_values(first_kv, col_kv)
                with sp.Fori(0, GROUP) as j4:
                    hx = sp.snap(g * GROUP + j4)
                    nxt = sp.snap((hx + 1) % NHEADS)
                    first = [sp.snap((hx // HEADS) * QT + BAND * s) for s in range(BANDS)]
                    col = sp.snap((hx % HEADS) * HD)
                    for n, j in enumerate(QUEUE):
                        sp.wait_ge(q_ready.sem, q_ready.at(hx, n + 1))
                        sp.sem_inc(sp_seen.sem)
                        load_queries(nxt, j)
                    for k in range(NU):
                        for short, s in enumerate(UNITS[k]):
                            sp.wait_ge(t_out.sem, t_out.at(hx, fold_use(k, short) + 1))
                            sp.dma_start(attn_view[:, bass.ds(first[s], BAND), bass.ds(col, HD)],
                                         ostage[:, BAND * s:BAND * (s + 1), :]).then_inc(o_out[s].sem, 16)
            for j in range(BANDS):
                sp.wait_ge(q_ld[j].sem, q_ld[j].at(NHEADS))
                sp.wait_ge(o_out[j].sem, o_out[j].at(NHEADS - 1))
            sp.wait_ge(q_ready.sem, q_ready.at(NHEADS))
            sp.wait_ge(k_ready.sem, k_ready.at(NGROUPS))
            sp.wait_ge(v_ready.sem, v_ready.at(NGROUPS))
            sp.wait_ge(k_ld.sem, k_ld.at(NGROUPS))
            sp.wait_ge(v_ld.sem, v_ld.at(NGROUPS))

        @block.tensor
        def _(pe):
            def scores(hx, kslot, k, v):
                s, j, c = CHUNKS[k][v]
                u = k * STEPS + v
                w = blocks(s, j, c) * P
                pe.wait_ge(exp_done.sem, exp_done.at(hx, u - RING + 1))
                for part in range(2):
                    last = nc.tensor.matmul(ps_s[:, u % RING, 0:w], qbuf[:, BAND * s + j, :],
                                            kbuf[:, bass.ds(kslot, 1), part, c * CW:c * CW + w],
                                            start=part == 0, stop=part == 1 and c < s)
                if c == s:
                    last = nc.tensor.matmul(ps_s[:, u % RING, w - P:w], idn_r[:, :], mask_r[:, :], start=False, stop=True)
                last.then_inc(s_done.sem, 1)

            def turn(hx, k, g):
                s, kb = GROUPS[k][g]
                t = use(k, g)
                pe.wait_ge(exp_done.sem, exp_done.at(hx, band_end(k, s)))
                pe.wait_ge(t_out.sem, t_out.at(hx, t - 1))
                for j in range(max(0, kb - BAND * s), BAND):
                    last = nc.tensor.transpose(ps_t[:, t % 2, j * P:(j + 1) * P], probs[:, k, place(k, s, j, kb), :], idn[:, :])
                last.then_inc(t_done.sem, 1)

            def weigh(hx, group, k, g):
                s, kb = GROUPS[k][g]
                lo = max(0, kb - BAND * s) * P
                pe.wait_ge(t_out.sem, t_out.at(hx, use(k, g) + 1))
                if kb == 0:
                    pe.wait_ge(o_ev.sem, o_ev.at(hx, 2 * k + (s == UNITS[k][1])))
                if kb % BAND == 0:
                    pe.wait_ge(v_set.sem, v_set.at(group, V_ORDER.index(kb // BAND) + 1))
                for part in range(2):
                    last = nc.tensor.matmul(ps_o[:, lo:], vbuf[:, kb, :, :],
                                            probsT[:, g % SLOTS, part, lo:],
                                            start=kb == 0 and part == 0, stop=kb == BAND * s + BAND - 1 and part == 1)
                last.then_inc(pv_done.sem, 1)

            def fold(hx, k, short):
                t = fold_use(k, short)
                pe.wait_ge(o_ev.sem, o_ev.at(hx, 2 * k + short + 1))
                pe.wait_ge(t_out.sem, t_out.at(hx, t - 1))
                for j in range(BAND):
                    last = nc.tensor.matmul(ps_t[:, t % 2, j * HD:(j + 1) * HD], folding[:, j * P:(j + 1) * P], idn_2[:, :],
                                            start=True, stop=True)
                last.then_inc(f_done.sem, 1)

            pe.wait_ge(rounded.sem, 2)
            s_done.credit(pe)
            t_done.credit(pe)
            pv_done.credit(pe)
            f_done.credit(pe)
            pe.wait_ge(k_ready.sem, 1)
            pe.wait_ge(q_ready.sem, 2)
            for v in range(LEAD + 1):
                if v == STEPS:
                    pe.wait_ge(q_ready.sem, BANDS)
                scores(0, 0, *chunk(0, v, 0)[1:])
            with pe.Fori(0, NHEADS) as hx:
                group = pe.snap(hx // GROUP)
                slot = pe.snap(group % 2)
                slot_next = pe.snap(((hx + 1) // GROUP) % 2)
                for k in range(NU):
                    def next_scores(v):
                        heads, unit, number = chunk(k, v, LEAD)
                        if number == 0 and unit == 0:
                            pe.wait_ge(q_ready.sem, q_ready.at(hx + 1, 2))
                            pe.wait_ge(k_ready.sem, (hx + 1) // GROUP + 1)
                        elif number == 0:
                            pe.wait_ge(q_ready.sem, q_ready.at(hx + heads, 4))
                        scores(hx + heads, slot_next if heads else slot, unit, number)

                    for v in range(STEPS):
                        if 0 < v < LATE:
                            next_scores(v)
                        turn(hx, k, v)
                        if v >= LAG:
                            weigh(hx, group, k, v - LAG)
                        if v == FOLD[k]:
                            fold(hx, k, 0)
                    weigh(hx, group, k, STEPS - 2)
                    next_scores(LATE)
                    weigh(hx, group, k, STEPS - 1)
                    for v in range(LATE + 1, STEPS + 1):
                        next_scores(v)
                    fold(hx, k, 1)

        @block.gpsimd
        def _(pool):
            def after(sem, value):
                pool.wait_ge(sem, value)
                pool.sem_inc(pool_seen.sem)

            def keys(g):
                after(k_ld.sem, k_ld.at(g))
                slot = bass.ds(g % 2, 1)
                nc.gpsimd.tensor_copy(kbuf[:, slot, 0, :], kstage[:, :]).then_inc(high_k.sem, 1)
                after(high_k.sem, high_k.at(g))
                nc.gpsimd.tensor_tensor(kbuf[:, slot, 1, :], kstage[:, :], kbuf[:, slot, 0, :].bitcast(F32),
                                        ALU.subtract).then_inc(k_ready.sem, 1)
                after(k_ready.sem, k_ready.at(g))

            def values(g):
                after(v_ld.sem, v_ld.at(g))
                nc.gpsimd.tensor_copy(vnext[:, :, 0, :], vstage[:, :, :]).then_inc(high_v.sem, 1)
                after(high_v.sem, high_v.at(g))
                nc.gpsimd.tensor_tensor(vnext[:, :, 1, :], vstage[:, :, :], vnext[:, :, 0, :].bitcast(F32),
                                        ALU.subtract).then_inc(v_ready.sem, 1)
                after(v_ready.sem, v_ready.at(g))

            def queries(hx, n):
                j, low = QUEUE[n], slice(HD, P)
                tiles = slice(BAND * j, BAND * (j + 1))
                after(q_ld[j].sem, q_ld[j].at(hx))
                nc.gpsimd.tensor_copy(qbuf[:, tiles, :], qstage[:, tiles, :]).then_inc(high_q.sem, 1)
                after(high_q.sem, high_q.at(hx, n + 1))
                nc.gpsimd.tensor_tensor(qbuf[low, tiles, :], qstage[low, tiles, :], qbuf[low, tiles, :].bitcast(F32),
                                        ALU.subtract).then_inc(q_ready.sem, 1)
                after(q_ready.sem, q_ready.at(hx, n + 1))

            def set_values(g, n):
                b = slice(BAND * V_ORDER[n], BAND * (V_ORDER[n] + 1))
                nc.gpsimd.tensor_copy(vbuf[:, b, :, :], vnext[:, b, :, :].bitcast(F32)).then_inc(v_set.sem, 1)

            def head_queries(hx):
                for k in range(NU):
                    after(s_done.sem, s_done.at(hx, (k + 1) * STEPS))
                    for n in (2 * k, 2 * k + 1):
                        queries(hx + 1, n)

            for n in range(2):
                queries(0, n)
            values(0)
            for n in range(BANDS):
                set_values(0, n)
            for n in range(2, BANDS):
                queries(0, n)
            with pool.Fori(0, NGROUPS) as g:
                head_queries(g * GROUP)
                keys(g + 1)
                after(v_set.sem, v_set.at(g))
                values(g + 1)
                with pool.Fori(1, GROUP) as j4:
                    head_queries(pool.snap(g * GROUP + j4))
                for n, used in enumerate(V_USED):
                    after(pv_done.sem, pv_done.at(g * GROUP + GROUP - 1, used))
                    set_values(g + 1, n)

        @block.scalar
        def _(act):
            def exps(hx, k, v):
                s, j, c = CHUNKS[k][v]
                u = k * STEPS + v
                tile = BAND * (s == UNITS[k][1]) + j
                n = blocks(s, j, c)
                if v == 0:
                    act.wait_ge(t_done.sem, t_done.at(hx - 1, (k + 1) * STEPS))
                    act.wait_ge(r_done.sem, r_done.at(hx - 1, 2 * k + 2))
                if c == 0:
                    act.wait_ge(m_done.sem, m_done.at(hx, 2 * BAND * k + tile + 1))
                at = place(k, s, j, c * CB)
                nc.scalar.activation(probs[:, k, at:at + n, :], ps_s[:, u % RING, 0:n * P], ACT.Exp, bias=negm[:, tile, :],
                                     accum_out=sums[:, s, j, c:c + 1]).then_inc(exp_done.sem, 1)

            def high(hx, k, g):
                s, kb = GROUPS[k][g]
                t, lo = use(k, g), max(0, kb - BAND * s) * P
                act.wait_ge(t_done.sem, t_done.at(hx, k * STEPS + g + 1))
                act.wait_ge(pv_done.sem, pv_done.at(hx, k * STEPS + g - SLOTS + 1))
                nc.scalar.activation(probsT[:, g % SLOTS, 0, lo:], ps_t[:, t % 2, lo:], ACT.Copy).then_inc(high_t.sem, 1)

            def take(hx, k, short):
                n = 2 * k + short
                act.wait_ge(pv_done.sem, pv_done.at(hx, band_end(k, UNITS[k][short])))
                act.wait_ge(f_done.sem, f_done.at(hx, n))
                nc.scalar.activation(folding[:, :], ps_o[:, :], ACT.Copy).then_inc(o_ev.sem, 1)

            act.wait_ge(k_ld.sem, k_ld.at(0))
            nc.scalar.activation(kbuf[:, 0, 0, :], kstage[:, :], ACT.Copy).then_inc(high_k.sem, 1)
            act.wait_ge(consts.sem, 16 * NCONST)
            for dst, src in ((idn_r, idn), (mask_r, mask)):
                nc.scalar.activation(dst[:, :], src[:, :], ACT.Copy).then_inc(rounded.sem, 1)
            exp_done.credit(act)
            o_ev.credit(act)
            for v in range(AHEAD + 1):
                exps(0, *chunk(0, v, 0)[1:])
            with act.Fori(0, NHEADS) as hx:
                for k in range(NU):
                    def next_exps(v):
                        heads, unit, number = chunk(k, v, AHEAD)
                        exps(hx + heads, unit, number)

                    for v in range(STEPS):
                        if v:
                            next_exps(v)
                        high(hx, k, v)
                        if v == FOLD[k] - 1:
                            take(hx, k, 0)
                    next_exps(STEPS)
                    take(hx, k, 1)

        @block.vector
        def _(dve):
            def peak(hx, k, v):
                s, j, c = CHUNKS[k][v]
                u = k * STEPS + v
                tile = BAND * (s == UNITS[k][1]) + j
                dve.wait_ge(s_done.sem, s_done.at(hx, u + 1))
                nc.vector.reduce_max(pmax[:, tile, c:c + 1], ps_s[:, u % RING, 0:blocks(s, j, c) * P],
                                     axis=mybir.AxisListType.X).then_inc(cmax.sem, 1)

            def settle(hx, k, v):
                s, j, c = CHUNKS[k][v]
                u = k * STEPS + v
                tile = BAND * (s == UNITS[k][1]) + j
                if c == s:
                    dve.wait_ge(cmax.sem, cmax.at(hx, u + 1))
                    before = (k - 1) % NU
                    dve.wait_ge(exp_done.sem, exp_done.at(hx, tile_end(before, tile) - (0 if k else PER)))
                    nc.vector.reduce_max(negm[:, tile, :], pmax[:, tile, 0:s + 1], axis=mybir.AxisListType.X,
                                         negate=True).then_inc(m_done.sem, 1)

            def low(hx, k, g):
                s, kb = GROUPS[k][g]
                t, lo = use(k, g), max(0, kb - BAND * s) * P
                dve.wait_ge(high_t.sem, high_t.at(hx, k * STEPS + g + 1))
                nc.vector.tensor_tensor(probsT[:, g % SLOTS, 1, lo:], ps_t[:, t % 2, lo:],
                                        probsT[:, g % SLOTS, 0, lo:].bitcast(F32), ALU.subtract).then_inc(t_out.sem, 1)

            def add_up(hx, k, short):
                s, n = UNITS[k][short], 2 * k + short
                dve.wait_ge(exp_done.sem, exp_done.at(hx, band_end(k, s)))
                nc.vector.reduce_sum(total[:, s, :], sums[:, s, :, 0:s + 1], axis=mybir.AxisListType.X).then_inc(sum_done.sem, 1)

            def invert(hx, k, short):
                s, n = UNITS[k][short], 2 * k + short
                dve.wait_ge(sum_done.sem, sum_done.at(hx, n + 1))
                nc.vector.reciprocal(rinv[:, s, :, 0], total[:, s, :]).then_inc(r_done.sem, 1)

            def normalise(hx, k, short):
                s, n, t = UNITS[k][short], 2 * k + short, fold_use(k, short)
                dve.wait_ge(f_done.sem, f_done.at(hx, n + 1))
                dve.wait_ge(r_done.sem, r_done.at(hx, n + 1))
                dve.wait_ge(o_out[s].sem, o_out[s].at(hx - 1))
                nc.vector.tensor_tensor(ostage[:, BAND * s:BAND * (s + 1), :],
                                        ps_t[:, t % 2, 0:BAND * HD].rearrange("p (n d) -> p n d", n=BAND),
                                        rinv[:, s, :, :].to_broadcast((P, BAND, HD)), ALU.mult).then_inc(t_out.sem, 1)

            dve.wait_ge(high_k.sem, high_k.at(0))
            nc.vector.tensor_tensor(kbuf[:, 0, 1, :], kstage[:, :], kbuf[:, 0, 0, :].bitcast(F32),
                                    ALU.subtract).then_inc(k_ready.sem, 1)
            t_out.credit(dve)
            r_done.credit(dve)
            for v in range(LEAD + 1):
                peak(0, *chunk(0, v, 0)[1:])
                settle(0, *chunk(0, v, 0)[1:])
            with dve.Fori(0, NHEADS) as hx:
                for k in range(NU):
                    def ahead(v):
                        heads, unit, number = chunk(k, v, LEAD)
                        return hx + heads, unit, number

                    for v in range(STEPS):
                        if 0 < v < LATE:
                            peak(*ahead(v))
                            settle(*ahead(v))
                        low(hx, k, v)
                        if v in (BAND, BAND + 1):
                            add_up(hx, k, v - BAND)
                        elif v in (BAND + 2, BAND + 3):
                            invert(hx, k, v - BAND - 2)
                        if v == FOLD[k]:
                            normalise(hx, k, 0)
                    for v in range(LATE, STEPS + 1):
                        peak(*ahead(v))
                        if v > LATE:
                            settle(*ahead(v - 1))
                    settle(*ahead(STEPS))
                    normalise(hx, k, 1)
    nc.clear_and_free_semaphores(sems)
    nc.all_engine_barrier()


I32 = mybir.dt.int32
U32 = mybir.dt.uint32
EXPERTS, TOPK, FF = 64, 8, 192
VMAX = TOKENS * TOPK
SPARE = 8
MAXG = TOKENS * TOPK // P + EXPERTS + SPARE
COLS = EXPERTS * NT + SPARE


def route(nc, attn, x2_rows, Wo, gate_wT, ident, before, iota_e, v_first, base, e_base, iota_g, incl, no_place,
          x3_rows, table, plan):
    AD = HEADS * HD
    AB = AD // P
    STEPS = 9

    sems = []
    with ExitStack() as ctx:
        def sb(name, shape, dt=F32):
            return ctx.enter_context(nc.sbuf_tensor(name, shape, dt))

        def pb(name, shape):
            return ctx.enter_context(nc.psum_tensor(name, shape, F32))

        def tally(name, per=1, ahead=0):
            sems.append(nc.alloc_semaphore(name))
            return Tally(sems[-1], per, ahead)

        w_o = sb("w_o", [P, AB, DM])
        w_g = sb("w_g", [P, KD, EXPERTS])
        idn = sb("idn4", [P, P])
        before_sb = sb("before_sb", [P, P])
        iota_sb = sb("iota_sb", [P, EXPERTS])
        ones = sb("ones4", [P, P])
        at = sb("at", [P, 2, AD])
        x2t = sb("x2t", [P, 2, DM])
        aT = sb("aT", [P, AB, P])
        r3 = sb("r3", [P, DM])
        x3 = sb("x3", [P, 2, DM])
        idx_f = sb("idx_f", [P, TOPK])
        entry = sb("entry", [P, 2, TOPK, 2])
        xT = sb("xT4", [P, KD, P])
        stats = sb("stats4", [P, 6])
        mv = sb("mv4", [P, 2])
        rstd = sb("rstd4", [P, 1])
        nhalf = sb("nhalf4", [P, 1])
        eps_sb = sb("eps4", [P, 1])
        negm = sb("negm4", [P, 1])
        ex = sb("ex", [P, EXPERTS])
        esum = sb("esum", [P, 1])
        erec = sb("erec", [P, 1])
        sc = sb("sc", [P, EXPERTS])
        top = sb("top", [P, TOPK])
        idx = sb("idx", [P, TOPK], U32)
        rest = sb("rest", [P, EXPERTS])
        chosen = sb("chosen", [P, EXPERTS])
        tsum = sb("tsum", [P, 1])
        macc = sb("macc", [P, EXPERTS])
        junk = sb("junk4", [P, TOPK, EXPERTS])
        dest_f = sb("dest_f", [P, TOPK])
        dest_i = sb("dest_i", [P, TOPK], I32)
        col = sb("col", [P, TOPK], I32)
        dest = sb("dest", [P, 2, TOPK], I32)
        e_base_sb = sb("e_base_sb", [EXPERTS, 1])
        g_sb = sb("g_sb", [EXPERTS, MAXG])
        incl_sb = sb("incl_sb", [EXPERTS, 2, EXPERTS])
        n_i = sb("n_i", [EXPERTS, 1], I32)
        n_f = sb("n_f", [EXPERTS, 1])
        ends = sb("ends", [EXPERTS, 1])
        past = sb("past", [EXPERTS, MAXG])
        first_f = sb("first_f", [1, MAXG])
        plan_sb = sb("plan_sb", [1, 2 * MAXG + EXPERTS + 1], I32)
        ps_t = pb("ps_t4", [P, 2, 4, P])
        ps_o = pb("ps_o4", [P, 512])
        ps_x = pb("ps_x4", [P, 4, P])
        ps_g = pb("ps_g4", [P, 512])
        ps_p = pb("ps_p4", [P, 512])

        front_ld = tally("front_ld3c", 32)
        consts = tally("consts4")
        nh_set = tally("nh_set4")
        in_ld = [tally("in4_ld0", 32), tally("in4_ld1", 32)]
        at_tr = tally("at_tr", 2)
        at_ev = tally("at_ev", 2, 1)
        op_ps = tally("op_ps4", 1, 1)
        sum3 = tally("sum3", 1, 1)
        stat = tally("stat4")
        stat_seen = tally("stat_seen4")
        aggr = tally("aggr4")
        add = tally("add4")
        pw = tally("pow4")
        x3_ready = tally("x3_ready")
        x3_out = [tally("x3_out0", 16, 1), tally("x3_out1", 16, 1)]
        tx = tally("tx4")
        xT_ev = tally("xT4_ev", 1, 1)
        lg = tally("lg4", 1, 1)
        nm = tally("nm4")
        ex_done = tally("ex_done", 1, 1)
        step = tally("step4", STEPS)
        seen = tally("seen4")
        mask_ready = tally("mask_ready")
        pos_ps = tally("pos_ps")
        counted = tally("counted", 1, 1)
        picked = tally("picked", 4)
        dest_ready = tally("dest_ready", 1, 1)
        sent = [tally("sent0", 16 * TOPK), tally("sent1", 16 * TOPK)]
        plan_step = tally("plan_step")
        plan_ps = tally("plan_ps")
        plan_out = tally("plan_out")
        NCONST = 8

        block = ctx.enter_context(nc.Block())

        @block.sync
        def _(sp):
            def load(slot, rows):
                sp.dma_start(at[:, slot, :], attn[rows, :]).then_inc(in_ld[slot].sem, 16)
                sp.dma_start(x2t[:, slot, :], x2_rows[rows, :]).then_inc(in_ld[slot].sem, 16)

            load(0, slice(0, P))
            sp.dma_start(idn[:, :], ident).then_inc(front_ld.sem, 16)
            sp.dma_start(w_o[:, :, :], Wo.rearrange("(k p) n -> p k n", p=P)).then_inc(front_ld.sem, 16)
            load(1, slice(P, 2 * P))
            with nc.allow_non_contiguous_dma(reason="small, once"):
                for dst, src in (
                    (w_g[:, :, :], gate_wT.rearrange("(k p) n -> p k n", p=P)),
                    (before_sb[:, :], before),
                    (iota_sb[:, :], iota_e),
                    (entry[:, 1, :, 0], v_first),
                    (macc[:, :], base),
                    (e_base_sb[:, :], e_base),
                    (g_sb[:, :], iota_g),
                    (incl_sb[:, :, :], incl),
                ):
                    sp.dma_start(dst, src).then_inc(consts.sem, 16)
            for o in x3_out:
                o.credit(sp)
            with sp.Fori(0, NT // 2) as i:
                ahead = [sp.snap(((2 * i + s + 2) % NT) * P) for s in range(2)]
                here = [sp.snap((2 * i + s) * P) for s in range(2)]
                for s in range(2):
                    t = 2 * i + s
                    sp.wait_ge(sum3.sem, sum3.at(t))
                    load(s, bass.ds(ahead[s], P))
                    sp.wait_ge(x3_ready.sem, x3_ready.at(t))
                    sp.dma_start(x3_rows[bass.ds(here[s], P), :], x3[:, s, :]).then_inc(x3_out[s].sem, 16)
            for s in range(2):
                sp.wait_ge(in_ld[s].sem, 32 * (NT // 2 + 1))
                sp.wait_ge(x3_out[s].sem, x3_out[s].at(NT // 2 - 1))
            sp.wait_ge(plan_step.sem, 10)
            sp.dma_start(plan, plan_sb[:, :]).then_inc(plan_out.sem, 16)
            sp.wait_ge(plan_out.sem, 16)

        @block.tensor
        def _(pe):
            def out_proj(t, s, loads, between=None):
                pe.wait_ge(in_ld[s].sem, 32 * loads)
                for g in range(2):
                    pe.wait_ge(at_ev.sem, at_ev.at(t - 1, g + 1))
                    for j in range(4):
                        b = 4 * g + j
                        last = nc.tensor.transpose(ps_t[:, g, j, :], at[:, s, b * P:(b + 1) * P], idn[:, :])
                    last.then_inc(at_tr.sem, 1)
                pe.wait_ge(at_ev.sem, at_ev.at(t))
                pe.wait_ge(sum3.sem, sum3.at(t - 1))
                for b in range(AB):
                    if b == AB // 2 and between:
                        between()
                    last = nc.tensor.matmul(ps_o[:, 0:DM], aT[:, b, :], w_o[:, b, :], start=b == 0, stop=b == AB - 1)
                last.then_inc(op_ps.sem, 1)

            def logits(t, s):
                pe.wait_ge(x3_ready.sem, x3_ready.at(t))
                for k in range(KD):
                    last = nc.tensor.transpose(ps_x[:, k, :], x3[:, s, k * P:(k + 1) * P], idn[:, :])
                last.then_inc(tx.sem, 1)
                pe.wait_ge(xT_ev.sem, xT_ev.at(t))
                pe.wait_ge(ex_done.sem, ex_done.at(t - 1))
                for k in range(KD):
                    last = nc.tensor.matmul(ps_g[:, 0:EXPERTS], xT[:, k, :], w_g[:, k, :], start=k == 0, stop=k == KD - 1)
                last.then_inc(lg.sem, 1)

            def places(t):
                pe.wait_ge(mask_ready.sem, mask_ready.at(t))
                pe.wait_ge(dest_ready.sem, dest_ready.at(t - 1))
                pe.wait_ge(counted.sem, counted.at(t - 1))
                nc.tensor.matmul(ps_p[:, 0:EXPERTS], before_sb[:, :], chosen[:, :], start=True, stop=False)
                nc.tensor.matmul(ps_p[:, 0:EXPERTS], ones[:, :], macc[:, :], start=False, stop=True).then_inc(pos_ps.sem, 1)

            pe.wait_ge(front_ld.sem, 32)
            out_proj(0, 0, 1)
            out_proj(1, 1, 1)
            pe.wait_ge(consts.sem, 16 * NCONST)
            pe.wait_ge(nh_set.sem, 3)
            with pe.Fori(0, NT // 2) as i:
                for s in range(2):
                    t = 2 * i + s
                    logits(t, s)
                    out_proj(t + 2, s, i + 2, lambda: places(t))
            pe.wait_ge(counted.sem, counted.at(NT - 1))
            pe.wait_ge(dest_ready.sem, dest_ready.at(NT - 1))
            pe.wait_ge(ex_done.sem, ex_done.at(NT - 1))
            nc.tensor.matmul(ps_g[0:EXPERTS, 0:1], macc[:, :], ones[:, 0:1], start=True, stop=True).then_inc(plan_ps.sem, 1)
            pe.wait_ge(plan_step.sem, 3)
            pe.wait_ge(sum3.sem, sum3.at(NT + 1))
            nc.tensor.matmul(ps_o[0:EXPERTS, 0:1], incl_sb[:, 0, :], n_f[:, :], start=True, stop=True).then_inc(plan_ps.sem, 1)
            nc.tensor.matmul(ps_g[0:1, 0:EXPERTS], n_f[:, :], incl_sb[:, 1, :], start=True, stop=True).then_inc(plan_ps.sem, 1)
            pe.wait_ge(plan_step.sem, 6)
            nc.tensor.matmul(ps_p[0:1, 0:MAXG], ones[0:EXPERTS, 0:1], past[:, :], start=True, stop=True).then_inc(plan_ps.sem, 1)
            nc.tensor.matmul(ps_o[0:1, 0:MAXG], n_f[:, :], past[:, :], start=True, stop=True).then_inc(plan_ps.sem, 1)

        @block.scalar
        def _(act):
            def take_attn(t):
                act.wait_ge(op_ps.sem, op_ps.at(t - 1))
                for g in range(2):
                    act.wait_ge(at_tr.sem, at_tr.at(t, g + 1))
                    nc.scalar.activation(aT[:, 4 * g:4 * g + 4, :], ps_t[:, g, :, :], ACT.Copy).then_inc(at_ev.sem, 1)

            at_ev.credit(act)
            op_ps.credit(act)
            xT_ev.credit(act)
            lg.credit(act)
            ex_done.credit(act)
            take_attn(0)
            take_attn(1)
            with act.Fori(0, NT // 2) as i:
                for s in range(2):
                    t = 2 * i + s
                    act.wait_ge(tx.sem, tx.at(t))
                    act.wait_ge(lg.sem, lg.at(t - 1))
                    nc.scalar.activation(xT[:, :, :], ps_x[:, 0:KD, :], ACT.Copy).then_inc(xT_ev.sem, 1)
                    act.wait_ge(nm.sem, nm.at(t))
                    nc.scalar.activation(ex[:, :], ps_g[:, 0:EXPERTS], ACT.Exp, bias=negm[:, :],
                                         accum_out=esum[:, :]).then_inc(ex_done.sem, 1)
                    take_attn(t + 2)

        @block.gpsimd
        def _(pool):
            def inv_std(t):
                pool.wait_ge(aggr.sem, aggr.at(t))
                nc.gpsimd.tensor_tensor(rstd[:, :], mv[:, 1:2], eps_sb[:, :], ALU.add).then_inc(add.sem, 1)
                pool.wait_ge(add.sem, add.at(t))
                nc.gpsimd.tensor_tensor(rstd[:, :], rstd[:, :], nhalf[:, :], ALU.pow).then_inc(pw.sem, 1)

            nc.gpsimd.memset(nhalf[:, :], -0.5).then_inc(nh_set.sem, 1)
            nc.gpsimd.memset(eps_sb[:, :], EPS).then_inc(nh_set.sem, 1)
            nc.gpsimd.memset(ones[:, :], 1.0).then_inc(nh_set.sem, 1)
            for s in range(2):
                half = slice(s * P // 2, (s + 1) * P // 2)
                pool.dma_start(table.rearrange("(p c) n -> p (c n)", p=P)[half, :], no_place[half, :]).then_inc(sent[s].sem, 16)
            pool.wait_ge(nh_set.sem, 3)
            inv_std(0)
            inv_std(1)
            for s in range(2):
                pool.wait_ge(sent[s].sem, 16)
            pool.wait_ge(consts.sem, 16 * NCONST)
            with pool.Fori(0, NT // 2) as i:
                for s in range(2):
                    t = 2 * i + s
                    pool.wait_ge(dest_ready.sem, dest_ready.at(t))
                    pool.sem_inc(seen.sem)
                    for k in range(TOPK):
                        pool.indirect_dma_start(out=table, out_offset=bass.IndirectOffsetOnAxis(ap=dest[:, s, k:k + 1], axis=0),
                                                in_=entry[:, s, k, :], in_offset=None).then_inc(sent[s].sem, 16)
                        if k == 0:
                            inv_std(t + 2)
            for s in range(2):
                pool.wait_ge(sent[s].sem, 16 + sent[s].at(NT // 2 - 1))

        @block.vector
        def _(dve):
            def moments(t, s, first=False):
                dve.wait_ge(op_ps.sem, op_ps.at(t))
                if not first:
                    dve.wait_ge(x3_ready.sem, x3_ready.at(t - 1))
                nc.vector.tensor_tensor(r3[:, :], ps_o[:, 0:DM], x2t[:, s, :], ALU.add).then_inc(sum3.sem, 1)
                dve.wait_ge(sum3.sem, sum3.at(t))
                nc.vector.bn_stats(stats[:, :], r3[:, :]).then_inc(stat.sem, 1)
                dve.wait_ge(stat.sem, stat.at(t))
                dve.sem_inc(stat_seen.sem)
                nc.vector.bn_aggr(mv[:, :], stats[:, :]).then_inc(aggr.sem, 1)

            def norm(t, s, prev):
                dve.wait_ge(pw.sem, pw.at(t))
                dve.wait_ge(x3_out[s].sem, x3_out[s].at(prev))
                nc.vector.tensor_scalar(x3[:, s, :], r3[:, :], mv[:, 0:1], rstd[:, :], ALU.subtract,
                                        ALU.mult).then_inc(x3_ready.sem, 1)

            def after(t, n):
                dve.wait_ge(step.sem, step.at(t, n))

            def choose(i, t, s):
                dve.wait_ge(lg.sem, lg.at(t))
                nc.vector.reduce_max(negm[:, :], ps_g[:, 0:EXPERTS], axis=mybir.AxisListType.X,
                                     negate=True).then_inc(nm.sem, 1)
                dve.wait_ge(ex_done.sem, ex_done.at(t))
                nc.vector.reciprocal(erec[:, :], esum[:, :]).then_inc(step.sem, 1)
                after(t, 1)
                nc.vector.tensor_scalar(sc[:, :], ex[:, :], erec[:, :], None, ALU.mult).then_inc(step.sem, 1)
                after(t, 2)
                dve.sem_inc(stat_seen.sem)
                nc.vector.max(top[:, :], sc[:, :]).then_inc(step.sem, 1)
                after(t, 3)
                dve.sem_inc(stat_seen.sem)
                nc.vector.match_replace(rest[:, :], top[:, :], sc[:, :], -1.0).then_inc(step.sem, 1)
                nc.vector.max_index(idx[:, :], top[:, :], sc[:, :]).then_inc(step.sem, 1)
                after(t, 4)
                nc.vector.tensor_scalar(chosen[:, :], rest[:, :], -1.0, None, ALU.is_equal).then_inc(mask_ready.sem, 1)
                nc.vector.reduce_sum(tsum[:, :], top[:, :], axis=mybir.AxisListType.X).then_inc(step.sem, 1)
                after(t, 6)
                nc.vector.tensor_scalar(tsum[:, :], tsum[:, :], 1e-20, None, ALU.add).then_inc(step.sem, 1)
                after(t, 7)
                nc.vector.reciprocal(tsum[:, :], tsum[:, :]).then_inc(step.sem, 1)
                nc.vector.tensor_copy(idx_f[:, :], idx[:, :])
                dve.wait_ge(sent[s].sem, 16 + 16 * TOPK * i)
                nc.vector.tensor_scalar(entry[:, s, :, 0], entry[:, 1 - s, :, 0], float(P * TOPK), None, ALU.add)
                after(t, 8)
                nc.vector.tensor_scalar(entry[:, s, :, 1], top[:, :], tsum[:, :], None, ALU.mult).then_inc(step.sem, 1)

            def send(t, s):
                dve.wait_ge(step.sem, step.at(t))
                dve.wait_ge(pos_ps.sem, pos_ps.at(t))
                for k in range(TOPK):
                    ins = nc.vector.scalar_tensor_tensor(junk[:, k, :], iota_sb[:, :], idx_f[:, k:k + 1],
                                                         ps_p[:, 0:EXPERTS], ALU.is_equal, ALU.mult,
                                                         accum_out=dest_f[:, k:k + 1])
                ins.then_inc(picked.sem, 1)
                dve.wait_ge(picked.sem, picked.at(t, 1))
                nc.vector.tensor_copy(dest_i[:, :], dest_f[:, :]).then_inc(picked.sem, 1)
                dve.wait_ge(picked.sem, picked.at(t, 2))
                nc.vector.tensor_scalar(col[:, :], dest_i[:, :], 7, None, ALU.arith_shift_right).then_inc(picked.sem, 1)
                nc.vector.tensor_scalar(dest_i[:, :], dest_i[:, :], P - 1, None, ALU.bitwise_and).then_inc(picked.sem, 1)
                dve.wait_ge(picked.sem, picked.at(t, 4))
                nc.vector.scalar_tensor_tensor(dest[:, s, :], dest_i[:, :], float(COLS), col[:, :], ALU.mult,
                                               ALU.add).then_inc(dest_ready.sem, 1)
                nc.vector.tensor_tensor(macc[:, :], macc[:, :], chosen[:, :], ALU.add).then_inc(counted.sem, 1)

            sum3.credit(dve)
            counted.credit(dve)
            dest_ready.credit(dve)
            moments(0, 0, True)
            norm(0, 0, -1)
            moments(1, 1)
            dve.wait_ge(consts.sem, 16 * NCONST)
            with dve.Fori(0, NT // 2) as i:
                for s in range(2):
                    t = 2 * i + s
                    choose(i, t, s)
                    send(t, s)
                    norm(t + 1, 1 - s, i - 1 + s)
                    moments(t + 2, s)

            def plan_after(n):
                dve.wait_ge(plan_step.sem, n)

            dve.wait_ge(plan_ps.sem, 1)
            nc.vector.tensor_scalar(n_i[:, :], ps_g[0:EXPERTS, 0:1], e_base_sb[:, :], None, ALU.subtract).then_inc(plan_step.sem, 1)
            plan_after(1)
            nc.vector.tensor_scalar(n_i[:, :], n_i[:, :], 7, None, ALU.arith_shift_right).then_inc(plan_step.sem, 1)
            plan_after(2)
            nc.vector.tensor_scalar(n_f[:, :], n_i[:, :], 1.0, None, ALU.max).then_inc(plan_step.sem, 1)
            dve.wait_ge(plan_ps.sem, 3)
            nc.vector.tensor_copy(ends[:, :], ps_o[0:EXPERTS, 0:1]).then_inc(plan_step.sem, 1)
            plan_after(4)
            nc.vector.tensor_scalar(past[:, :], g_sb[:, :], ends[:, :], None, ALU.is_ge).then_inc(plan_step.sem, 1)
            nc.vector.tensor_copy(plan_sb[:, 2 * MAXG:2 * MAXG + EXPERTS], ps_g[0:1, 0:EXPERTS]).then_inc(plan_step.sem, 1)
            dve.wait_ge(plan_ps.sem, 5)
            nc.vector.tensor_scalar(plan_sb[:, 0:MAXG], ps_p[0:1, 0:MAXG], float(EXPERTS - 1), None, ALU.min).then_inc(plan_step.sem, 1)
            nc.vector.tensor_tensor(first_f[:, :], g_sb[0:1, :], ps_o[0:1, 0:MAXG], ALU.subtract)
            nc.vector.tensor_copy(plan_sb[:, 2 * MAXG + EXPERTS:], ps_o[0:1, MAXG - 1:MAXG]).then_inc(plan_step.sem, 1)
            plan_after(8)
            nc.vector.scalar_tensor_tensor(first_f[:, :], ps_p[0:1, 0:MAXG], float(NT), first_f[:, :], ALU.mult,
                                           ALU.add).then_inc(plan_step.sem, 1)
            plan_after(9)
            nc.vector.tensor_scalar(plan_sb[:, MAXG:2 * MAXG], first_f[:, :], float(COLS - 1), None,
                                    ALU.min).then_inc(plan_step.sem, 1)
    nc.clear_and_free_semaphores(sems)
    nc.all_engine_barrier()


def experts(nc, table, plan, x3_rows, W_guT, W_downT, ident, y8):
    H2 = FF // 2
    WSLOTS = 4

    sems = []
    with ExitStack() as ctx:
        def sb(name, shape, dt=F32):
            return ctx.enter_context(nc.sbuf_tensor(name, shape, dt))

        def pb(name, shape):
            return ctx.enter_context(nc.psum_tensor(name, shape, F32))

        def tally(name, per=1, ahead=0):
            sems.append(nc.alloc_semaphore(name))
            return Tally(sems[-1], per, ahead)

        idn = sb("idn5", [P, P])
        entries = sb("entries", [P, COLS, 2])
        token_all = sb("token_all", [P, COLS, 1], I32)
        place_all = sb("place_all", [P, COLS, 1], I32)
        token = sb("token", [P, 2, 1], I32)
        place = sb("place", [P, 2, 1], I32)
        weight = sb("weight", [P, 2, 1])
        plan_sb = sb("plan5", [1, 2 * MAXG + EXPERTS + 1], I32)
        pairs_sb = sb("pairs5", [1, 1], I32)
        w_gu = sb("w_gu", [P, WSLOTS, KD, 2 * FF])
        w_d = sb("w_d", [H2, WSLOTS, 2, DM])
        xr = sb("xr", [P, 2, DM])
        xT = sb("xT5", [P, 2, KD, P])
        sg = sb("sg", [P, 2, FF])
        hid = sb("hid", [P, 2, FF])
        hT = sb("hT", [H2, 2, 2, P])
        y_sb = sb("y5", [P, 2, DM])
        ps_x = pb("ps_x5", [P, 2, 4, P])
        ps_gu = pb("ps_gu", [P, 2, 512])
        ps_h = pb("ps_h", [P, 2, 4, P])
        ps_y = pb("ps_y5", [P, 2, 512])

        consts = tally("consts5")
        pairs_step = tally("pairs_step")
        w_ld = [tally("w_ld%d" % q, 32, 1) for q in range(WSLOTS)]
        w_ready = tally("w_ready")
        x_ld = [tally("x5_ld0", 16), tally("x5_ld1", 16)]
        tx = tally("tx5")
        xT_ev = tally("xT5_ev")
        gu = tally("gu")
        gate = tally("gate")
        hid_ready = tally("hid_ready")
        th = tally("th")
        hT_ev = tally("hT_ev")
        down = tally("down", 1, 2)
        listed = tally("listed")
        token_ready = tally("token_ready")
        token_seen = tally("token_seen")
        weighed = tally("weighed")
        y_ready = tally("y5_ready", 1, 2)
        y_seen = tally("y5_seen")
        y_out = [tally("y5_out0", 16), tally("y5_out1", 16)]
        NCONST = 2

        def planned(row, g):
            return plan_sb[0:1, bass.ds(row * MAXG + g, 1)]

        def pair_count(eng):
            eng.wait_ge(pairs_step.sem, 2)
            return eng.value_load(pairs_sb[0:1, 0:1], min_val=1, max_val=MAXG // 2)

        block = ctx.enter_context(nc.Block())

        @block.sync
        def _(sp):
            def weights(slot, e):
                sp.dma_start(w_gu[:, slot, :, :], W_guT[bass.ds(e, 1)].rearrange("o (k p) n -> p (o k) n", p=P)
                             ).then_inc(w_ld[slot].sem, 16)
                sp.dma_start(w_d[:, slot, :, :], W_downT[bass.ds(e, 1)].rearrange("o (k p) n -> p (o k) n", p=H2)
                             ).then_inc(w_ld[slot].sem, 16)

            def arrived(q, load):
                sp.wait_ge(w_ld[q].sem, w_ld[q].at(load))
                sp.sem_inc(w_ready.sem)

            sp.dma_start(plan_sb[:, :], plan).then_inc(consts.sem, 16)
            sp.dma_start(idn[:, :], ident).then_inc(consts.sem, 16)
            for w in w_ld:
                w.credit(sp)
            for q in range(WSLOTS):
                weights(q, q)
            for q in range(WSLOTS - 1):
                arrived(q, 0)
            sp.wait_ge(consts.sem, 16 * NCONST)
            with sp.Fori(1, EXPERTS // WSLOTS) as j:
                for q in range(WSLOTS):
                    e = sp.snap(WSLOTS * j + q)
                    start = sp.value_load(plan_sb[0:1, bass.ds(2 * MAXG + WSLOTS * (j - 1) + q + 1, 1)], min_val=1, max_val=MAXG)
                    sp.wait_ge(down.sem, start + down.ahead)
                    weights(q, e)
                    arrived((q - 1) % WSLOTS, j if q else j - 1)
            arrived(WSLOTS - 1, EXPERTS // WSLOTS - 1)

        @block.tensor
        def _(pe):
            def expert(g):
                return pe.value_load(planned(0, g), min_val=0, max_val=EXPERTS - 1)

            def turn_x(g, s, loads):
                pe.wait_ge(x_ld[s].sem, 16 * loads)
                for k in range(KD):
                    last = nc.tensor.transpose(ps_x[:, s, k, :], xr[:, s, k * P:(k + 1) * P], idn[:, :])
                last.then_inc(tx.sem, 1)

            def gate_up(g, s, e):
                pe.wait_ge(w_ready.sem, e + 1)
                pe.wait_ge(xT_ev.sem, xT_ev.at(g))
                for k in range(KD):
                    last = nc.tensor.matmul(ps_gu[:, s, 0:2 * FF], xT[:, s, k, :], w_gu[:, bass.ds(e % WSLOTS, 1), k, :],
                                            start=k == 0, stop=k == KD - 1)
                last.then_inc(gu.sem, 1)

            def turn_h(g, s):
                pe.wait_ge(hid_ready.sem, hid_ready.at(g))
                for b in range(2):
                    last = nc.tensor.transpose(ps_h[0:H2, s, b, :], hid[:, s, b * H2:(b + 1) * H2], idn[:, :])
                last.then_inc(th.sem, 1)

            def output(g, s, e):
                pe.wait_ge(hT_ev.sem, hT_ev.at(g))
                pe.wait_ge(y_ready.sem, y_ready.at(g - 2))
                for b in range(2):
                    last = nc.tensor.matmul(ps_y[:, s, 0:DM], hT[:, s, b, :], w_d[:, bass.ds(e % WSLOTS, 1), b, :],
                                            start=b == 0, stop=b == 1)
                last.then_inc(down.sem, 1)

            pe.wait_ge(consts.sem, 16 * NCONST)
            pairs = pair_count(pe)
            down.credit(pe)
            turn_x(0, 0, 1)
            turn_x(1, 1, 1)
            experts_here = [pe.alloc_register("expert%d" % s) for s in range(2)]
            for s in range(2):
                e = expert(s)
                pe.reg_mov(experts_here[s], e)
                gate_up(s, s, e)
            with pe.Fori(0, pairs) as i:
                here = [pe.snap(experts_here[s], min_val=0, max_val=EXPERTS - 1) for s in range(2)]
                ahead = [expert(2 * i + 2 + s) for s in range(2)]
                for s in range(2):
                    turn_x(2 * i + 2 + s, s, i + 2)
                    turn_h(2 * i + s, s)
                gate_up(2 * i + 2, 0, ahead[0])
                output(2 * i, 0, here[0])
                gate_up(2 * i + 3, 1, ahead[1])
                output(2 * i + 1, 1, here[1])
                for s in range(2):
                    pe.reg_mov(experts_here[s], ahead[s])

        @block.scalar
        def _(act):
            def take_x(g, s):
                act.wait_ge(tx.sem, tx.at(g))
                nc.scalar.activation(xT[:, s, :, :], ps_x[:, s, 0:KD, :], ACT.Copy).then_inc(xT_ev.sem, 1)

            def take_h(g, s):
                act.wait_ge(th.sem, th.at(g))
                act.wait_ge(down.sem, down.at(g - 2))
                nc.scalar.activation(hT[:, s, :, :], ps_h[0:H2, s, 0:2, :], ACT.Copy).then_inc(hT_ev.sem, 1)

            act.wait_ge(consts.sem, 16 * NCONST)
            def silu(g, s):
                act.wait_ge(gu.sem, gu.at(g))
                nc.scalar.activation(sg[:, s, :], ps_gu[:, s, 0:FF], ACT.Silu).then_inc(gate.sem, 1)

            pairs = pair_count(act)
            for s in range(2):
                take_x(s, s)
            for s in range(2):
                silu(s, s)
            with act.Fori(0, pairs) as i:
                for s in range(2):
                    take_x(2 * i + 2 + s, s)
                    take_h(2 * i + s, s)
                for s in range(2):
                    silu(2 * i + 2 + s, s)

        @block.gpsimd
        def _(pool):
            def gather(g, s, turned=True):
                pool.wait_ge(token_ready.sem, token_ready.at(g))
                if turned:
                    pool.wait_ge(tx.sem, tx.at(g - 2))
                pool.sem_inc(token_seen.sem)
                pool.indirect_dma_start(out=xr[:, s, :], out_offset=None, in_=x3_rows,
                                        in_offset=bass.IndirectOffsetOnAxis(ap=token[:, s, :], axis=0)
                                        ).then_inc(x_ld[s].sem, 16)

            for s in range(2):
                half = slice(s * P // 2, (s + 1) * P // 2)
                pool.dma_start(entries[half, :, :], table.rearrange("(p c) n -> p c n", p=P)[half, :, :]).then_inc(y_out[s].sem, 16)
            y_ready.credit(pool)
            pool.wait_ge(consts.sem, 16 * NCONST)
            pairs = pair_count(pool)
            for g in range(4):
                gather(g, g % 2, g >= 2)
            with pool.Fori(0, pairs) as i:
                for s in range(2):
                    gather(2 * i + 4 + s, s)
                for s in range(2):
                    pool.wait_ge(y_ready.sem, y_ready.at(2 * i + s))
                    pool.sem_inc(y_seen.sem)
                    pool.indirect_dma_start(out=y8, out_offset=bass.IndirectOffsetOnAxis(ap=place[:, s, :], axis=0),
                                            in_=y_sb[:, s, :], in_offset=None).then_inc(y_out[s].sem, 16)
            for s in range(2):
                pool.wait_ge(y_out[s].sem, 16 * (pairs + 1))
                pool.sem_inc(y_seen.sem)
                pool.wait_ge(x_ld[s].sem, 16 * (pairs + 2))
                pool.sem_inc(token_seen.sem)

        @block.vector
        def _(dve):
            def tokens(g, s, loads):
                c = dve.value_load(planned(1, g), min_val=0, max_val=COLS - 1)
                if loads is not None:
                    dve.wait_ge(x_ld[s].sem, 16 * loads)
                nc.vector.tensor_copy(token[:, s, :], token_all[:, bass.ds(c, 1), :]).then_inc(token_ready.sem, 1)

            def unit(g, s):
                dve.wait_ge(gate.sem, gate.at(g))
                nc.vector.tensor_tensor(hid[:, s, :], ps_gu[:, s, FF:2 * FF], sg[:, s, :], ALU.mult).then_inc(hid_ready.sem, 1)

            def scale(i, g, s):
                c = dve.value_load(planned(1, g), min_val=0, max_val=COLS - 1)
                dve.wait_ge(y_out[s].sem, 16 * (i + 1))
                dve.wait_ge(y_ready.sem, y_ready.at(g - 2))
                nc.vector.tensor_copy(place[:, s, :], place_all[:, bass.ds(c, 1), :])
                nc.vector.tensor_copy(weight[:, s, :], entries[:, bass.ds(c, 1), 1:2]).then_inc(weighed.sem, 1)
                dve.wait_ge(weighed.sem, weighed.at(g))
                dve.wait_ge(down.sem, down.at(g))
                nc.vector.tensor_scalar(y_sb[:, s, :], ps_y[:, s, 0:DM], weight[:, s, :], None, ALU.mult).then_inc(y_ready.sem, 1)

            dve.wait_ge(consts.sem, 16 * NCONST)
            nc.vector.tensor_scalar(pairs_sb[:, :], plan_sb[:, 2 * MAXG + EXPERTS:], 1, None, ALU.add).then_inc(pairs_step.sem, 1)
            dve.wait_ge(pairs_step.sem, 1)
            nc.vector.tensor_scalar(pairs_sb[:, :], pairs_sb[:, :], 1, None, ALU.arith_shift_right).then_inc(pairs_step.sem, 1)
            pairs = pair_count(dve)
            for s in range(2):
                dve.wait_ge(y_out[s].sem, 16)
            nc.vector.tensor_copy(place_all[:, :, :], entries[:, :, 0:1]).then_inc(listed.sem, 1)
            dve.wait_ge(listed.sem, 1)
            nc.vector.tensor_scalar(token_all[:, :, :], place_all[:, :, :], 3, None, ALU.arith_shift_right).then_inc(listed.sem, 1)
            dve.wait_ge(listed.sem, 2)
            nc.vector.tensor_scalar(token_all[:, :, :], token_all[:, :, :], TOKENS - 1, None, ALU.min).then_inc(listed.sem, 1)
            dve.wait_ge(listed.sem, 3)
            for g in range(4):
                tokens(g, g % 2, 1 if g >= 2 else None)
            for s in range(2):
                unit(s, s)
            with dve.Fori(0, pairs) as i:
                for s in range(2):
                    tokens(2 * i + 4 + s, s, i + 2)
                for s in range(2):
                    unit(2 * i + 2 + s, s)
                    scale(i, 2 * i + s, s)
    nc.clear_and_free_semaphores(sems)
    nc.all_engine_barrier()


def combine(nc, y8, x3_rows, out):
    SLOTS = 4
    y_view = y8[0:VMAX, :].rearrange("(t k) d -> t k d", k=TOPK)

    sems = []
    with ExitStack() as ctx:
        def sb(name, shape, dt=F32):
            return ctx.enter_context(nc.sbuf_tensor(name, shape, dt))

        def tally(name, per=1, ahead=0):
            sems.append(nc.alloc_semaphore(name))
            return Tally(sems[-1], per, ahead)

        parts = sb("parts", [P, SLOTS, TOPK + 1, DM])
        r4 = sb("r4", [P, 2, DM])
        o_sb = sb("o_sb", [P, SLOTS, DM])
        stats = sb("stats6", [P, 2, 6])
        mv = sb("mv6", [P, 2, 2])
        rstd = sb("rstd6", [P, 2, 1])
        nhalf = sb("nhalf6", [P, 1])
        eps_sb = sb("eps6", [P, 1])

        nh_set = tally("nh_set6")
        in_ld = [tally("in6_ld%d" % s, 32) for s in range(SLOTS)]
        summed = tally("summed", 2)
        stat = tally("stat6")
        stat_seen = tally("stat_seen6")
        aggr = tally("aggr6")
        add = tally("add6")
        pw = tally("pow6")
        o_ready = tally("o_ready", 1, 2)
        o_out = [tally("o6_out%d" % s, 16, 1) for s in range(SLOTS)]

        block = ctx.enter_context(nc.Block())

        @block.sync
        def _(sp):
            def load(slot, rows):
                sp.dma_start(parts[:, slot, 0:TOPK, :], y_view[rows, :, :]).then_inc(in_ld[slot].sem, 16)
                sp.dma_start(parts[:, slot, TOPK, :], x3_rows[rows, :]).then_inc(in_ld[slot].sem, 16)

            for s in range(SLOTS):
                load(s, slice(s * P, (s + 1) * P))
            with sp.Fori(0, NT // SLOTS) as i:
                ahead = [sp.snap(((SLOTS * (i + 1) + s) % NT) * P) for s in range(SLOTS)]
                for s in range(SLOTS):
                    sp.wait_ge(summed.sem, summed.at(SLOTS * i + s))
                    load(s, bass.ds(ahead[s], P))
            for s in range(SLOTS):
                sp.wait_ge(in_ld[s].sem, in_ld[s].at(NT // SLOTS))

        @block.scalar
        def _(act):
            for o in o_out:
                o.credit(act)
            with act.Fori(0, NT // SLOTS) as i:
                here = [act.snap((SLOTS * i + s) * P) for s in range(SLOTS)]
                for s in range(SLOTS):
                    act.wait_ge(o_ready.sem, o_ready.at(SLOTS * i + s))
                    act.dma_start(out[bass.ds(here[s], P), :], o_sb[:, s, :]).then_inc(o_out[s].sem, 16)
            for s in range(SLOTS):
                act.wait_ge(o_out[s].sem, o_out[s].at(NT // SLOTS - 1))

        @block.gpsimd
        def _(pool):
            nc.gpsimd.memset(nhalf[:, :], -0.5).then_inc(nh_set.sem, 1)
            nc.gpsimd.memset(eps_sb[:, :], EPS).then_inc(nh_set.sem, 1)
            pool.wait_ge(nh_set.sem, 2)
            with pool.Fori(0, NT // SLOTS) as i:
                for s in range(SLOTS):
                    t, h = SLOTS * i + s, s % 2
                    pool.wait_ge(aggr.sem, aggr.at(t))
                    nc.gpsimd.tensor_tensor(rstd[:, h, :], mv[:, h, 1:2], eps_sb[:, :], ALU.add).then_inc(add.sem, 1)
                    pool.wait_ge(add.sem, add.at(t))
                    nc.gpsimd.tensor_tensor(rstd[:, h, :], rstd[:, h, :], nhalf[:, :], ALU.pow).then_inc(pw.sem, 1)

        @block.vector
        def _(dve):
            def total(t, s, loads, half):
                dve.wait_ge(in_ld[s].sem, 32 * loads)
                dve.wait_ge(o_ready.sem, o_ready.at(t - 2))
                cols = slice(half * DM // 2, (half + 1) * DM // 2)
                nc.vector.reduce_sum(r4[:, s % 2, cols], parts[:, s, :, cols].rearrange("p k d -> p d k"),
                                     axis=mybir.AxisListType.X).then_inc(summed.sem, 1)

            o_ready.credit(dve)
            for half in range(2):
                total(0, 0, 1, half)
            with dve.Fori(0, NT // SLOTS) as i:
                for s in range(SLOTS):
                    t, h = SLOTS * i + s, s % 2
                    following = (t + 1, (s + 1) % SLOTS, i + 1 + (s + 1) // SLOTS)
                    dve.wait_ge(summed.sem, summed.at(t))
                    nc.vector.bn_stats(stats[:, h, :], r4[:, h, :]).then_inc(stat.sem, 1)
                    total(*following, 0)
                    dve.wait_ge(stat.sem, stat.at(t))
                    dve.sem_inc(stat_seen.sem)
                    nc.vector.bn_aggr(mv[:, h, :], stats[:, h, :]).then_inc(aggr.sem, 1)
                    total(*following, 1)
                    dve.wait_ge(pw.sem, pw.at(t))
                    dve.wait_ge(o_out[s].sem, o_out[s].at(i - 1))
                    nc.vector.tensor_scalar(o_sb[:, s, :], r4[:, h, :], mv[:, h, 0:1], rstd[:, h, :], ALU.subtract,
                                            ALU.mult).then_inc(o_ready.sem, 1)
    nc.clear_and_free_semaphores(sems)
    nc.all_engine_barrier()


def layers(nc, x_T, x_rows, W_inT, conv_w, W_xprojT, W_dtT, b_dt, A_log, D_skip, W_outT, F_inT, F_bias, F_outT, Wqk, Wv,
           Wo, gate_wT, W_guT, W_downT, sel_bc, keep, ident, rope_q, rope_k, causal, before, iota_e, v_first, base, e_base,
           iota_g, incl, no_place, out):
    def scratch(name, shape, dt=F32):
        return nc.dram_tensor(name, shape, dt).ap()

    y_scr = scratch("y_scr", (512, TOKENS))
    x2_rows = scratch("x2_rows", (TOKENS, DM))
    x2_T = scratch("x2_T", (DM, TOKENS))
    q_scr = scratch("q_scr", (BATCH * HEADS, HD, LENGTH))
    k_scr = scratch("k_scr", (BATCH * KV, HD, LENGTH))
    v_scr = scratch("v_scr", (TOKENS, KV * HD))
    attn = scratch("attn", (TOKENS, HEADS * HD))
    x3_rows = scratch("x3_rows", (TOKENS, DM))
    table = scratch("table", (P * COLS, 2))
    plan = scratch("plan", (1, 2 * MAXG + EXPERTS + 1), I32)
    y8 = scratch("y8", (VMAX + 2 * P, DM))

    mamba(nc, x_T, W_inT, conv_w, W_xprojT, W_dtT, b_dt, A_log, D_skip, sel_bc, keep, ident, y_scr)
    tree_ffn(nc, y_scr, x_rows, W_outT, F_inT, F_bias, F_outT, ident, x2_rows, x2_T)
    qkv(nc, x2_T, Wqk, Wv, rope_q, rope_k, q_scr, k_scr, v_scr)
    attention(nc, q_scr, k_scr, v_scr, ident, causal, attn)
    route(nc, attn, x2_rows, Wo, gate_wT, ident, before, iota_e, v_first, base, e_base, iota_g, incl, no_place,
          x3_rows, table, plan)
    experts(nc, table, plan, x3_rows, W_guT, W_downT, ident, y8)
    combine(nc, y8, x3_rows, out)


def constants():
    import numpy as np
    f = np.float32
    i, e, k = np.arange(P), np.arange(EXPERTS), np.arange(TOPK)
    RANK, NST = 16, 16
    n = np.arange(2 * NST)
    sel = np.zeros((64 + RANK + 2 * NST, 2 * NST, P), f)
    sel[RANK + n, n, :] = 1
    sel[64 + RANK + n, n, :] = 1
    keep = np.ones((P, 4), f)
    keep[:, 1::2] = 0
    inv = f(1) / np.power(f(10000), np.arange(0, HD, 2, dtype=f) / f(HD))
    freqs = np.arange(LENGTH, dtype=f)[:, None] * inv[None, :]
    emb = np.concatenate([freqs, freqs], -1)
    cos, sin = np.cos(emb)[:, 0::2].T, np.sin(emb)[:, 0::2].T
    rope = np.tile(np.stack([cos, sin, -sin, cos], 1).astype(f), (GROUP, 1, 1))
    base = np.zeros((P, EXPERTS), f)
    base[0] = e * TOKENS
    no_place = np.zeros((P, COLS, 2), f)
    no_place[:, :, 0] = VMAX + P * (np.arange(COLS) // NT % 2)[None, :] + i[:, None]
    return dict(
        sel_bc=sel, keep=keep, ident=np.eye(P, dtype=f), rope_q=rope * f(HD ** -0.5), rope_k=rope,
        causal=np.triu(np.full((P, P), -2.0 ** 100, f), 1), before=(i[:, None] < i[None, :]).astype(f),
        iota_e=np.tile(e.astype(f), (P, 1)), v_first=(i[:, None] * TOPK + k[None, :] - P * TOPK).astype(f), base=base,
        e_base=(e * TOKENS - (P - 1)).astype(f)[:, None], iota_g=np.tile(np.arange(MAXG, dtype=f), (EXPERTS, 1)),
        incl=np.stack([e[:, None] <= e[None, :], e[:, None] < e[None, :]], 1).astype(f), no_place=no_place.reshape(P, 2 * COLS))


def kernel(**inputs):
    import numpy as np
    import concourse.bacc as bacc
    from concourse.bass_utils import run_bass_kernel_spmd

    def a(name):
        return np.asarray(inputs[name])

    def heads(w, n):
        return w.reshape(DM, n, GROUP, HD // 2, 2).transpose(0, 1, 4, 2, 3).reshape(DM, 2 * n, P)

    x = a("L0_attn_x").reshape(TOKENS, DM)
    given = dict(
        x_T=x.T, x_rows=x, W_inT=a("L0_attn_W_in").T, conv_w=a("L0_attn_W_conv").reshape(512, 4),
        W_xprojT=a("L0_attn_W_xproj").T, W_dtT=a("L0_attn_W_dt").T, b_dt=a("L0_attn_b_dt"), A_log=a("L0_attn_A_log"),
        D_skip=a("L0_attn_D"), W_outT=a("L0_attn_W_out").T, F_inT=a("L0_ffn_W_in").T, F_bias=a("L0_ffn_b_in"),
        F_outT=a("L0_ffn_W_out").T,
        Wqk=np.concatenate([heads(a("L1_attn_Wq"), HEADS // GROUP), heads(a("L1_attn_Wk"), KV // GROUP)], 1),
        Wv=a("L1_attn_Wv"), Wo=a("L1_attn_Wo"), gate_wT=a("L1_ffn_gate_w").T,
        W_guT=np.concatenate([a("L1_ffn_w_gate").transpose(0, 2, 1), a("L1_ffn_w_up").transpose(0, 2, 1)], 2),
        W_downT=a("L1_ffn_w_down").transpose(0, 2, 1))
    nc = bacc.Bacc("TRN2", target_bir_lowering=False, num_devices=1)
    arrays, args = {}, {}
    for name, value in {**given, **constants()}.items():
        arrays[name] = np.ascontiguousarray(value)
        args[name] = nc.dram_tensor(name, arrays[name].shape, mybir.dt.from_np(arrays[name].dtype), kind="ExternalInput").ap()
    out = nc.dram_tensor("out", (TOKENS, DM), F32, kind="ExternalOutput").ap()
    layers(nc, out=out, **args)
    r = run_bass_kernel_spmd(nc, [arrays], core_ids=[0])
    return r.results[0]["out"].reshape(BATCH, LENGTH, DM)
```
